# Optimizing a Trainium2 kernel written in Bass

```python
import numpy as np
import jax
import jax.numpy as jnp

def _softmax(x, axis=-1):
    return jax.nn.softmax(x, axis=axis)

def _gelu(x):
    return jax.nn.gelu(x, approximate=True)

def _silu(x):
    return jax.nn.silu(x)

def _sigmoid(x):
    return jax.nn.sigmoid(x)

def _layernorm(x, axis=-1, eps=1e-05):
    m = jnp.mean(x, axis=axis, keepdims=True)
    v = jnp.var(x, axis=axis, keepdims=True)
    return (x - m) / jnp.sqrt(v + eps)

def _scatter_add(tgt, idx, src, axis=0):
    return tgt.at[idx].add(src)

def _segment_sum(src, seg, n):
    return jax.ops.segment_sum(src, seg, n)
kernel_name = 'mk_flamingo_gated_d2_seqx_r8_a7bb2d'

def setup_inputs(seed: int=0):
    np.random.seed(seed)
    _w = jnp.asarray

    def _rec_inputs():
        import jax
        import jax.numpy as jnp
        _rk = jax.random.key(seed)
        x = -0.0003929 + 0.9999 * jax.random.normal(jax.random.fold_in(_rk, 1), (64, 64, 256), jnp.float32)
        _lenS = 64 - jax.random.randint(jax.random.fold_in(_rk, 7), (64,), 0, max(1, 64 // 4) + 1, jnp.int32)
        _lenS2 = 64 - jax.random.randint(jax.random.fold_in(_rk, 8), (64,), 0, max(1, 64 // 4) + 1, jnp.int32)
        _ctx_2048P = jax.random.normal(jax.random.fold_in(_rk, 11), (64, 16, 256), jnp.float32)
        _ctx_2048c = jax.random.dirichlet(jax.random.fold_in(_rk, 511), 0.3 * jnp.ones((16,), jnp.float32), (64, 64))
        _ctx_2048t = jnp.einsum('bsk,bkd->bsd', _ctx_2048c, _ctx_2048P)
        _ctx_2048t = _ctx_2048t * jax.lax.rsqrt(jnp.mean(jnp.square(_ctx_2048t)) + 1e-12) * 0.953939
        ctx_2048 = 1.72703e-05 + 1.00003 * (_ctx_2048t + 0.3 * jax.random.normal(jax.random.fold_in(_rk, 611), (64, 64, 256), jnp.float32))
        _g = jax.random.normal(jax.random.fold_in(_rk, 9001), (2, 2), jnp.float32)
        _g = jnp.sign(_g) * jnp.maximum(jnp.abs(_g), 1.0) + (_g == 0) * 1.0
        g_xattn = _g[0]
        g_ffn = _g[1]
        return (x, ctx_2048, g_xattn, g_ffn)
    x, ctx_2048, g_xattn, g_ffn = _rec_inputs()

    def _L0_xattn_setup():
        import jax, jax.numpy as jnp
        import numpy as np
        DIM = 256
        H = 16
        D = 128
        INNER = H * D
        N_IMG = 257
        EPS = 1e-06

        def rms_norm(x, scale, eps=EPS):
            ms = jnp.mean(jnp.square(x), axis=-1, keepdims=True)
            return x * jax.lax.rsqrt(ms + eps) * scale

        def sdpa(q, k, v):
            scale = 1.0 / jnp.sqrt(jnp.asarray(D, q.dtype))
            scores = jnp.einsum('bshd,blhd->bhsl', q, k) * scale
            attn = jax.nn.softmax(scores, axis=-1)
            return jnp.einsum('bhsl,blhd->bshd', attn, v)
        key = jax.random.key(seed)
        ks = jax.random.split(key, 16)
        std = 1.0 / np.sqrt(DIM)
        inp = {'x': jax.random.normal(ks[0], (2, 512, DIM), jnp.float32), 'context': jax.random.normal(ks[1], (2, 769, DIM), jnp.float32), 'q_w': jax.random.normal(ks[2], (DIM, INNER), jnp.float32) * std, 'q_b': jnp.zeros((INNER,), jnp.float32), 'k_w': jax.random.normal(ks[3], (DIM, INNER), jnp.float32) * std, 'k_b': jnp.zeros((INNER,), jnp.float32), 'v_w': jax.random.normal(ks[4], (DIM, INNER), jnp.float32) * std, 'v_b': jnp.zeros((INNER,), jnp.float32), 'ki_w': jax.random.normal(ks[5], (DIM, INNER), jnp.float32) * std, 'ki_b': jnp.zeros((INNER,), jnp.float32), 'vi_w': jax.random.normal(ks[6], (DIM, INNER), jnp.float32) * std, 'vi_b': jnp.zeros((INNER,), jnp.float32), 'o_w': jax.random.normal(ks[7], (INNER, DIM), jnp.float32) * std, 'o_b': jnp.zeros((DIM,), jnp.float32), 'nq_s': jnp.ones((INNER,), jnp.float32), 'nkt_s': jnp.ones((INNER,), jnp.float32), 'nki_s': jnp.ones((INNER,), jnp.float32)}
        return inp
    _L0_xattn_all = _L0_xattn_setup()
    _L0_xattn_in = {k: v for k, v in _L0_xattn_all.items() if k in ('q_w', 'q_b', 'k_w', 'k_b', 'v_w', 'v_b', 'ki_w', 'ki_b', 'vi_w', 'vi_b', 'o_w', 'o_b', 'nq_s', 'nkt_s', 'nki_s')}
    del _L0_xattn_all

    def _L0_ffn_setup():
        import jax, jax.numpy as jnp
        import numpy as np
        K = 2
        SCALING = 16.0 / 16.0
        key = jax.random.key(seed)
        ks = jax.random.split(key, 7)
        B, T, D, O, E, R = (2, 512, 256, 256, 8, 16)
        return {'x': jax.random.normal(ks[0], (B, T, D), dtype=jnp.float32), 'W': jax.random.normal(ks[1], (O, D), dtype=jnp.float32) * (1.0 / np.sqrt(D)), 'b': jax.random.normal(ks[2], (O,), dtype=jnp.float32) * 0.02, 'lora_A': jax.random.normal(ks[3], (E, R, D), dtype=jnp.float32) * (1.0 / np.sqrt(D)), 'lora_B': jax.random.normal(ks[4], (E, O, R), dtype=jnp.float32) * 0.02, 'gate_w': jax.random.normal(ks[5], (E, D), dtype=jnp.float32) * 0.02, 'gate_b': jax.random.normal(ks[6], (E,), dtype=jnp.float32) * 0.02}
    _L0_ffn_all = _L0_ffn_setup()
    _L0_ffn_in = {k: v for k, v in _L0_ffn_all.items() if k in ('W', 'b', 'lora_A', 'lora_B', 'gate_w', 'gate_b')}
    del _L0_ffn_all

    def _L1_xattn_setup():
        import jax, jax.numpy as jnp
        import numpy as np
        from math import sqrt
        key = jax.random.key(seed)
        kq, kk, kv = jax.random.split(key, 3)
        B, D, N = (8, 128, 256)
        Q = jax.random.normal(kq, (B, D, N), dtype=jnp.float32)
        K = jax.random.normal(kk, (B, D, N), dtype=jnp.float32)
        V = jax.random.normal(kv, (B, D, N), dtype=jnp.float32)
        return {'Q': Q, 'K': K, 'V': V}
    _L1_xattn_all = _L1_xattn_setup()
    _L1_xattn_in = {k: v for k, v in _L1_xattn_all.items() if k in ()}
    del _L1_xattn_all

    def _L1_ffn_setup():
        import jax, jax.numpy as jnp
        import numpy as np
        B, S, D, R, E = (4, 256, 256, 64, 8)
        SCALING = 64.0 / 16.0
        key = jax.random.key(seed)
        k1, k2, k3, k4 = jax.random.split(key, 4)
        x = jax.random.normal(k1, (B, S, D), dtype=jnp.float32)
        A = jax.random.normal(k2, (E, R, D), dtype=jnp.float32) * 0.02
        Bw = jax.random.normal(k3, (E, D, R), dtype=jnp.float32) * 0.02
        Wg = jax.random.normal(k4, (E, D), dtype=jnp.float32) * 0.02
        return {'x': x, 'A': A, 'Bw': Bw, 'Wg': Wg}
    _L1_ffn_all = _L1_ffn_setup()
    _L1_ffn_in = {k: v for k, v in _L1_ffn_all.items() if k in ('A', 'Bw', 'Wg')}
    del _L1_ffn_all
    return {'x': x, 'ctx_2048': ctx_2048, 'g_xattn': g_xattn, 'g_ffn': g_ffn, 'L0_xattn_q_w': _L0_xattn_in['q_w'], 'L0_xattn_q_b': _L0_xattn_in['q_b'], 'L0_xattn_k_w': _L0_xattn_in['k_w'], 'L0_xattn_k_b': _L0_xattn_in['k_b'], 'L0_xattn_v_w': _L0_xattn_in['v_w'], 'L0_xattn_v_b': _L0_xattn_in['v_b'], 'L0_xattn_ki_w': _L0_xattn_in['ki_w'], 'L0_xattn_ki_b': _L0_xattn_in['ki_b'], 'L0_xattn_vi_w': _L0_xattn_in['vi_w'], 'L0_xattn_vi_b': _L0_xattn_in['vi_b'], 'L0_xattn_o_w': _L0_xattn_in['o_w'], 'L0_xattn_o_b': _L0_xattn_in['o_b'], 'L0_xattn_nq_s': _L0_xattn_in['nq_s'], 'L0_xattn_nkt_s': _L0_xattn_in['nkt_s'], 'L0_xattn_nki_s': _L0_xattn_in['nki_s'], 'L0_ffn_W': _L0_ffn_in['W'], 'L0_ffn_b': _L0_ffn_in['b'], 'L0_ffn_lora_A': _L0_ffn_in['lora_A'], 'L0_ffn_lora_B': _L0_ffn_in['lora_B'], 'L0_ffn_gate_w': _L0_ffn_in['gate_w'], 'L0_ffn_gate_b': _L0_ffn_in['gate_b'], 'L1_ffn_A': _L1_ffn_in['A'], 'L1_ffn_Bw': _L1_ffn_in['Bw'], 'L1_ffn_Wg': _L1_ffn_in['Wg']}

def reference(x, ctx_2048, g_xattn, g_ffn, L0_xattn_q_w, L0_xattn_q_b, L0_xattn_k_w, L0_xattn_k_b, L0_xattn_v_w, L0_xattn_v_b, L0_xattn_ki_w, L0_xattn_ki_b, L0_xattn_vi_w, L0_xattn_vi_b, L0_xattn_o_w, L0_xattn_o_b, L0_xattn_nq_s, L0_xattn_nkt_s, L0_xattn_nki_s, L0_ffn_W, L0_ffn_b, L0_ffn_lora_A, L0_ffn_lora_B, L0_ffn_gate_w, L0_ffn_gate_b, L1_ffn_A, L1_ffn_Bw, L1_ffn_Wg):
    import jax
    import jax.numpy as jnp

    def _L0_xattn_ref(x, context, q_w, q_b, k_w, k_b, v_w, v_b, ki_w, ki_b, vi_w, vi_b, o_w, o_b, nq_s, nkt_s, nki_s):
        import jax, jax.numpy as jnp
        import numpy as np
        DIM = 256
        H = 16
        D = 128
        INNER = H * D
        N_IMG = 257
        EPS = 1e-06

        def rms_norm(x, scale, eps=EPS):
            ms = jnp.mean(jnp.square(x), axis=-1, keepdims=True)
            return x * jax.lax.rsqrt(ms + eps) * scale

        def sdpa(q, k, v):
            scale = 1.0 / jnp.sqrt(jnp.asarray(D, q.dtype))
            scores = jnp.einsum('bshd,blhd->bhsl', q, k) * scale
            attn = jax.nn.softmax(scores, axis=-1)
            return jnp.einsum('bhsl,blhd->bshd', attn, v)
        B, S, _ = x.shape
        img_ctx = context[:, :N_IMG]
        txt_ctx = context[:, N_IMG:]
        q = rms_norm(x @ q_w + q_b, nq_s).reshape(B, S, H, D)
        k_txt = rms_norm(txt_ctx @ k_w + k_b, nkt_s).reshape(B, -1, H, D)
        v_txt = (txt_ctx @ v_w + v_b).reshape(B, -1, H, D)
        out_txt = sdpa(q, k_txt, v_txt)
        k_img = rms_norm(img_ctx @ ki_w + ki_b, nki_s).reshape(B, -1, H, D)
        v_img = (img_ctx @ vi_w + vi_b).reshape(B, -1, H, D)
        out_img = sdpa(q, k_img, v_img)
        out = (out_txt + out_img).reshape(B, S, INNER)
        return out @ o_w + o_b

    def _L0_ffn_ref(x, W, b, lora_A, lora_B, gate_w, gate_b):
        import jax, jax.numpy as jnp
        import numpy as np
        K = 2
        SCALING = 16.0 / 16.0
        orig_shape = x.shape
        D = orig_shape[-1]
        O = W.shape[0]
        x_flat = x.reshape(-1, D)
        base = x_flat @ W.T + b
        logits = x_flat @ gate_w.T + gate_b
        topk_logits, topk_idx = jax.lax.top_k(logits, K)
        gates = jax.nn.softmax(topk_logits, axis=-1)
        xA = jnp.einsum('nd,erd->ner', x_flat, lora_A)
        delta_all = jnp.einsum('ner,eor->neo', xA, lora_B)
        delta_topk = jnp.take_along_axis(delta_all, topk_idx[:, :, None], axis=1)
        lora_update = jnp.sum(delta_topk * gates[:, :, None], axis=1)
        out = base + SCALING * lora_update
        return out.reshape(*orig_shape[:-1], O)

    def _L1_xattn_ref(Q, K, V):
        import jax, jax.numpy as jnp
        import numpy as np
        from math import sqrt
        dk = Q.shape[1]
        x = jnp.einsum('bdn,bdm->bnm', Q, K) / sqrt(dk)
        score = jax.nn.sigmoid(x)
        out = jnp.einsum('bvn,bnm->bvm', V, score)
        return out

    def _L1_ffn_ref(x, A, Bw, Wg):
        import jax, jax.numpy as jnp
        import numpy as np
        B, S, D, R, E = (4, 256, 256, 64, 8)
        SCALING = 64.0 / 16.0
        bsz, seq_len, dim = x.shape
        xf = x.reshape(-1, dim)
        logits = jnp.einsum('nd,ed->ne', xf, Wg)
        prob = jax.nn.softmax(logits, axis=-1)
        gate = jnp.argmax(prob, axis=-1)
        prob_sel = jnp.take_along_axis(prob, gate[:, None], axis=1)
        mask = jax.nn.one_hot(gate, E, dtype=xf.dtype)
        h = jnp.einsum('nd,erd->ner', xf, A)
        h = h * mask[:, :, None]
        y = jnp.einsum('ner,eor->no', h, Bw)
        y = y * SCALING * prob_sel
        return y.reshape(bsz, seq_len, -1)
    x = x + jnp.tanh(g_xattn[0]) * _L0_xattn_ref(_layernorm(x, axis=-1), ctx_2048, L0_xattn_q_w, L0_xattn_q_b, L0_xattn_k_w, L0_xattn_k_b, L0_xattn_v_w, L0_xattn_v_b, L0_xattn_ki_w, L0_xattn_ki_b, L0_xattn_vi_w, L0_xattn_vi_b, L0_xattn_o_w, L0_xattn_o_b, L0_xattn_nq_s, L0_xattn_nkt_s, L0_xattn_nki_s)
    x = x + jnp.tanh(g_ffn[0]) * _L0_ffn_ref(_layernorm(x, axis=-1), L0_ffn_W, L0_ffn_b, L0_ffn_lora_A, L0_ffn_lora_B, L0_ffn_gate_w, L0_ffn_gate_b)
    x = x + jnp.tanh(g_xattn[1]) * _L1_xattn_ref(_layernorm(x, axis=-1), ctx_2048, ctx_2048)
    x = x + jnp.tanh(g_ffn[1]) * _L1_ffn_ref(_layernorm(x, axis=-1), L1_ffn_A, L1_ffn_Bw, L1_ffn_Wg)
    return x

_drawn_inputs = setup_inputs


def setup_inputs(seed=0):
    import zlib

    import numpy as np

    out = dict(_drawn_inputs(seed))
    spreads = {'g_ffn': (-1.0, 0.6),
     'L0_xattn_q_b': (0.0, 0.338),
     'L0_xattn_k_b': (0.0, 0.1),
     'L0_xattn_v_b': (0.0, 0.1),
     'L0_xattn_ki_b': (0.0, 0.8),
     'L0_xattn_vi_b': (0.0, 0.1),
     'L0_xattn_o_b': (0.0, 0.1),
     'L0_xattn_nq_s': (1.0, 0.6),
     'L0_xattn_nkt_s': (1.0, 0.2),
     'L0_xattn_nki_s': (1.0, 0.6)}
    factors = {'L0_ffn_b': 7.24,
     'L0_ffn_lora_A': 4.149,
     'L0_ffn_lora_B': 4.224,
     'L0_ffn_gate_w': 5.492,
     'L0_ffn_gate_b': 8.0,
     'L1_ffn_A': 8.0,
     'L1_ffn_Bw': 8.0,
     'L1_ffn_Wg': 8.0}
    for name, (base, spread) in spreads.items():
        noise = np.random.default_rng([zlib.crc32(name.encode()), seed]).standard_normal(out[name].shape)
        drawn = base * np.exp(spread * noise) if base else spread * noise
        out[name] = jnp.asarray(drawn.astype(out[name].dtype))
    for name, factor in factors.items():
        out[name] = (out[name] * factor).astype(out[name].dtype)
    return out
```

```python
from contextlib import ExitStack

import concourse.bass as bass
from concourse import mybir

F32 = mybir.dt.float32
F32R = mybir.dt.float32r
I32 = mybir.dt.int32
ALU = mybir.AluOpType
ACT = mybir.ActivationFunctionType
AXX = mybir.AxisListType.X

P = 128
BATCH, SEQ, D = 64, 64, 256
H, HD = 16, 128
INNER = H * HD
DC = D // P
NT = 4
GT = NT * P
NG = BATCH * SEQ // GT
E0, R0 = 8, 16
E1, R1 = 8, 64
K0 = 2
LN_EPS, RMS_EPS = 1e-5, 1e-6
LORA_SCALING, EXPERT_SCALING = 16.0 / 16.0, 64.0 / 16.0
RSQRT_SEED = 0x5F3759DF
BIG = 1e30


class Signal:

    def __init__(self, sem, per):
        self.sem, self.per = sem, per

    def wait(self, eng, g, i):
        value = g * self.per + (i + 1)
        if isinstance(g, int) and value <= 0:
            return
        eng.wait_ge(self.sem, value)


class Chain:

    def __init__(self, eng, sem):
        self.eng, self.sem, self.base, self.n = eng, sem, 0, 0

    def start(self, base):
        self.base, self.n = base, 0

    def mark(self, ins):
        self.n += 1
        ins.then_inc(self.sem, 1)

    def wait(self):
        self.eng.wait_ge(self.sem, self.base + self.n)

    def link(self, ins):
        self.mark(ins)
        self.wait()


def rsqrt(dve, chain, y, t, v):
    chain.link(dve.tensor_scalar(t.bitcast(I32), v.bitcast(I32), 1, None, ALU.logical_shift_right))
    chain.link(dve.tensor_scalar(y.bitcast(I32), t.bitcast(I32), -1.0, float(RSQRT_SEED), ALU.mult, ALU.add))
    for _ in range(3):
        chain.link(dve.tensor_tensor(t, y, y, ALU.mult))
        chain.link(dve.scalar_tensor_tensor(out=t, in0=t, scalar=-0.5, in1=v, op0=ALU.mult, op1=ALU.mult))
        chain.link(dve.scalar_tensor_tensor(out=y, in0=t, scalar=1.5, in1=y, op0=ALU.add, op1=ALU.mult))


def moments(dve, chain, mean, var_eps, t, stats):
    chain.mark(dve.tensor_tensor(mean, stats[:, :, 1], stats[:, :, 4], ALU.add))
    chain.mark(dve.tensor_tensor(t, stats[:, :, 1], stats[:, :, 4], ALU.subtract))
    chain.link(dve.tensor_tensor(var_eps, stats[:, :, 2], stats[:, :, 5], ALU.add))
    chain.mark(dve.tensor_scalar(mean, mean, 0.5, None, ALU.mult))
    chain.link(dve.tensor_tensor(t, t, t, ALU.mult))
    chain.link(dve.scalar_tensor_tensor(out=t, in0=t, scalar=0.25 * D, in1=var_eps, op0=ALU.mult, op1=ALU.add))
    chain.link(dve.tensor_scalar(var_eps, t, 1.0 / D, LN_EPS, ALU.mult, ALU.add))


def identity(pool, sem, ident):
    pool.memset(ident, 0.0).then_inc(sem, 1)
    pool.wait_ge(sem, 1)
    pool.affine_select(out=ident, in_=ident, compare_op=ALU.not_equal, fill=1.0, base=0,
                       pattern=[[-1, P]], channel_multiplier=1).then_inc(sem, 1)


IDENT_READY = 2


def first_attention(nc, x, ctx, g_xattn, q_w, q_b, ki_w, ki_b, vi_w, vi_b, o_w, o_b, nq_s, nki_s, x1_dram):
    CHAIN_PER = 112
    EARLY_PER = 12
    x_t = x.rearrange("b s d -> (b s) d").rearrange("(g t p) d -> g p t d", g=NG, p=P)
    c_t = ctx.rearrange("b s d -> (b s) d").rearrange("(g t p) d -> g p t d", g=NG, p=P)
    with ExitStack() as stack:
        def sb(name, shape, dt=F32):
            return stack.enter_context(nc.sbuf_tensor(name, shape, dt))

        def sem(name):
            return stack.enter_context(nc.semaphore(name))

        def signal(name, per):
            return Signal(sem(name), per)

        w_hi = {n: sb(f"{n}_hi", [P, DC, INNER], F32R) for n in "qkv"}
        w_lo = {n: sb(f"{n}_lo", [P, DC, INNER], F32R) for n in "qkv"}
        wo_hi = sb("wo_hi", [P, H, D], F32R)
        wo_lo = sb("wo_lo", [P, H, D], F32R)
        gram = sb("gram", [P, 2, DC, D])
        gram_row = sb("gram_row", [P, 2, D + 2])
        ident = sb("ident", [P, P])
        ones = sb("ones", [P, P])
        vecs = sb("vecs", [P, 5 * H])
        qscale = sb("qscale", [P, H])
        qbias = sb("qbias", [P, H])
        tg = sb("tg", [P, 2])
        obias = sb("obias", [P, D])
        xin = sb("xin", [P, NT, D])
        cin = sb("cin", [P, NT, D])
        stats = sb("stats", [P, NT, 6])
        mean = sb("mean", [P, NT])
        var_eps = sb("var_eps", [P, NT])
        rstd = sb("rstd", [P, NT])
        nt_t = sb("nt_t", [P, NT])
        sums = sb("sums", [P, 2 * NT])
        sums_b = sb("sums_b", [P, 2 * NT])
        rqk = sb("rqk", [P, 2 * NT])
        nqk_t = sb("nqk_t", [P, 2 * NT])
        gram_t = sb("gram_t", [P, D])
        gram_j = sb("gram_j", [P, D])
        xs = sb("xs", [P, DC, GT])
        cs = sb("cs", [P, DC, GT])
        rmax = sb("rmax", [P, NT])
        rsum = sb("rsum", [P, NT])
        rinv = sb("rinv", [P, NT])

        prep = ExitStack()
        raw = [prep.enter_context(nc.sbuf_tensor(f"raw{i}", [P, INNER], F32)) for i in range(2)]
        wt = prep.enter_context(nc.sbuf_tensor("wt", [P, H, D + 1], F32))
        vrow = prep.enter_context(nc.sbuf_tensor("vrow", [5 * H, HD], F32))
        urow = prep.enter_context(nc.sbuf_tensor("urow", [1, D + 1], F32))
        prep.close()
        xt_hi = sb("xt_hi", [P, DC, GT], F32R)
        xt_lo = sb("xt_lo", [P, DC, GT], F32R)
        ct_hi = sb("ct_hi", [P, DC, GT], F32R)
        ct_lo = sb("ct_lo", [P, DC, GT], F32R)
        q_sb = sb("q_sb", [P, GT])
        k_sb = sb("k_sb", [P, GT])
        v_sb = sb("v_sb", [P, 2, NT, 2 * HD])
        logit = sb("logit", [P, NT, SEQ])
        expo = sb("expo", [P, NT, SEQ])
        prob = sb("prob", [P, NT, SEQ])
        rr = sb("rr", [P, NT, SEQ])
        pt = sb("pt", [P, NT, P])
        ao_hi = sb("ao_hi", [P, GT], F32R)
        ao_lo = sb("ao_lo", [P, GT], F32R)
        diag = sb("diag", [P, NT, P])
        xres = sb("xres", [P, NT, D])

        banks = [stack.enter_context(nc.psum_tensor(f"bank{i}", [P, 512], F32)) for i in range(8)]
        o_ps, pj_ps, at_ps, pv_ps, tr_ps, gr_ps = banks[0:2], banks[2:4], banks[4], banks[5], banks[6], banks[7]

        s_ident = sem("s_ident")
        s_ones = sem("s_ones")
        s_vec = sem("s_vec")
        s_gate = sem("s_gate")
        s_obias = sem("s_obias")
        s_tanh = sem("s_tanh")
        s_raw = [sem("s_raw0"), sem("s_raw1")]
        s_whi = sem("s_whi")
        s_wlo = sem("s_wlo")
        s_prep = sem("s_prep")
        s_prepev = sem("s_prepev")
        s_ptzero = sem("s_ptzero")
        s_chain = sem("s_chain")
        xin_in = signal("xin_in", 16)
        cin_in = signal("cin_in", 16)
        xres_in = signal("xres_in", 16)
        x1_out = signal("x1_out", 16)
        xres_ready = signal("xres_ready", 1)
        xn_ready = signal("xn_ready", 1)
        tr_full = signal("tr_full", NT)
        tr_read = signal("tr_read", NT)
        gr_full = signal("gr_full", NT)
        gr_read = signal("gr_read", NT)
        diag_ready = signal("diag_ready", 1)
        rk_full = signal("rk_full", 1)
        rr_ready = signal("rr_ready", 1)
        split_hi = signal("split_hi", 2)
        split_lo = signal("split_lo", 2)
        pj_full = signal("pj_full", 3 * H)
        pj_read = signal("pj_read", 3 * H)
        qk_full = signal("qk_full", H)
        l_ready = signal("l_ready", H)
        e_ready = signal("e_ready", H)
        p_ready = signal("p_ready", H)
        pt_full = signal("pt_full", H)
        pt_ready = signal("pt_ready", H)
        pv_full = signal("pv_full", H)
        ao_hi_ready = signal("ao_hi_ready", H)
        ao_ready = signal("ao_ready", H)
        o_full = signal("o_full", H)
        x1_ready = signal("x1_ready", 1)

        NAMES = [("q", 0), ("q", 1), ("k", 0), ("k", 1), ("v", 0), ("v", 1), ("o", 0), ("o", 1)]

        def weight_parts(i):
            n, c = NAMES[i]
            if n == "o":
                half = slice(c * H // 2, (c + 1) * H // 2)
                return (wo_hi[:, half, :].rearrange("p h d -> p (h d)"),
                        wo_lo[:, half, :].rearrange("p h d -> p (h d)"))
            return w_hi[n][:, c, :], w_lo[n][:, c, :]

        block = stack.enter_context(nc.Block())

        @block.sync
        def _(sp):
            src = {"q": q_w, "k": ki_w, "v": vi_w}

            def load_inputs(g):
                at = g if isinstance(g, int) else bass.ds(g, 1)

                def view(t):
                    return t[at] if isinstance(g, int) else t[at].rearrange("g p t d -> p (g t) d")

                gr_read.wait(sp, g, -1)
                sp.dma_start(xin[:, :, :], view(x_t)).then_inc(xin_in.sem, 16)
                sp.dma_start(cin[:, :, :], view(c_t)).then_inc(cin_in.sem, 16)

            for j, v in enumerate((q_b, nq_s, nki_s, ki_b, vi_b)):
                sp.dma_start(vrow[j * H:(j + 1) * H, :], v.rearrange("(h d) -> h d", h=H)).then_inc(s_vec, 16)
            for i, (n, c) in enumerate(NAMES):
                if i >= 2:
                    sp.wait_ge(s_wlo, i - 1)
                    if i - 2 < 4:
                        sp.wait_ge(s_prep, 1 + EARLY_PER * ((i - 2) // 2) + 4 * ((i - 2) % 2) + 4)
                if n == "o":
                    half = o_w.rearrange("(h p) d -> p h d", h=H)[:, c * H // 2:(c + 1) * H // 2, :]
                    sp.dma_start(raw[i % 2][:, :].rearrange("p (h d) -> p h d", d=D), half).then_inc(s_raw[i % 2], 16)
                else:
                    sp.dma_start(raw[i % 2][:, :], src[n][c * P:(c + 1) * P, :]).then_inc(s_raw[i % 2], 16)
                if i == 1:
                    load_inputs(0)

            def group(g, last):
                at = g if isinstance(g, int) else bass.ds(g, 1)

                def view(t):
                    return t[at] if isinstance(g, int) else t[at].rearrange("g p t d -> p (g t) d")

                if not last:
                    load_inputs(g + 1)
                x1_out.wait(sp, g - 1, 15)
                if isinstance(g, int) and g == 0:
                    sp.wait_ge(s_prepev, 1 + 2 * EARLY_PER)
                    sp.wait_ge(s_wlo, 8)
                sp.dma_start(xres[:, :, :], view(x_t)).then_inc(xres_in.sem, 16)
                x1_ready.wait(sp, g, 0)
                sp.dma_start(view(x1_dram), xres[:, :, :]).then_inc(x1_out.sem, 16)

            group(0, False)
            with sp.Fori(1, NG - 1) as g:
                group(g, False)
            group(NG - 1, True)
            x1_out.wait(sp, NG - 1, 15)

        @block.gpsimd
        def _(pool):
            identity(pool, s_ident, ident[:, :])
            pool.memset(ones[:, :], 1.0).then_inc(s_ones, 1)
            pool.dma_start(tg[:, :], g_xattn.partition_broadcast(P)).then_inc(s_gate, 16)
            pool.dma_start(obias[:, :], o_b.partition_broadcast(P)).then_inc(s_gate, 16)
            pool.wait_ge(s_prepev, 1 + 2 * EARLY_PER)
            pool.wait_ge(s_wlo, 8)
            pool.memset(pt[:, :, :], 0.0).then_inc(s_ptzero, 1)
            pool.wait_ge(s_obias, 1)

            def group(g):
                xres_in.wait(pool, g, 15)
                pool.tensor_tensor(xres[:, :, :], xres[:, :, :],
                                   obias[:, :].unsqueeze(1).to_broadcast([P, NT, D]),
                                   ALU.add).then_inc(xres_ready.sem, 1)

            group(0)
            with pool.Fori(1, NG) as g:
                group(g)

        @block.scalar
        def _(act):
            act.wait_ge(s_gate, 32)
            act.activation(tg[:, :], tg[:, :], ACT.Tanh).then_inc(s_tanh, 1)

            def high_part(i):
                act.wait_ge(s_raw[i % 2], 16 * (i // 2 + 1))
                act.activation(weight_parts(i)[0], raw[i % 2][:, :], ACT.Copy).then_inc(s_whi, 1)

            def transposed(g, t):
                tr_full.wait(act, g, t)
                act.activation(xs[:, :, t * P:(t + 1) * P],
                               tr_ps[:, 0:D].rearrange("p (c n) -> p c n", c=DC), ACT.Copy)
                act.activation(cs[:, :, t * P:(t + 1) * P],
                               tr_ps[:, D:2 * D].rearrange("p (c n) -> p c n", c=DC), ACT.Copy).then_inc(tr_read.sem, 1)

            def split(g):
                tr_read.wait(act, g, NT - 1)
                if isinstance(g, int) and g == 0:
                    act.wait_ge(s_wlo, 8)
                    act.wait_ge(s_prepev, 1 + 2 * EARLY_PER)
                pj_full.wait(act, g, -1)
                act.activation(ct_hi[:, :, :], cs[:, :, :], ACT.Copy).then_inc(split_hi.sem, 1)
                act.activation(xt_hi[:, :, :], xs[:, :, :], ACT.Copy).then_inc(split_hi.sem, 1)

            def attn_hi(g, h):
                pv_full.wait(act, g, h)
                act.activation(ao_hi[:, :], pv_ps[:, :], ACT.Identity,
                               bias=vecs[:, 4 * H + h % H:4 * H + h % H + 1]).then_inc(ao_hi_ready.sem, 1)

            def exps(g, h):
                l_ready.wait(act, g, h)
                act.activation(expo[:, :, :], logit[:, :, :], ACT.Exp).then_inc(e_ready.sem, 1)

            def project(g, h, j):
                pj_full.wait(act, g, 3 * h + j)
                bank = pj_ps[(3 * h + j) % 2]
                if j == 0:
                    t = 2 * (h % 2)
                    act.activation(v_sb[:, (h // 2) % 2, t:t + 2, :],
                                   bank[:, :].rearrange("p (t n) -> p t n", t=2), ACT.Copy).then_inc(pj_read.sem, 1)
                elif j == 1:
                    act.activation(k_sb[:, :], bank[:, :], ACT.Identity,
                                   bias=vecs[:, 3 * H + h:3 * H + h + 1]).then_inc(pj_read.sem, 1)
                else:
                    act.activation(q_sb[:, :], bank[:, :], ACT.Identity, scale=qscale[:, h:h + 1],
                                   bias=qbias[:, h:h + 1]).then_inc(pj_read.sem, 1)

            def step(g, h, first, last):
                if h >= 2 or not first:
                    attn_hi(g, h - 2)
                if h < H:
                    project(g, h, 0)
                if (h >= 1 or not first) and h - 1 < H:
                    exps(g, h - 1)
                if h < H:
                    project(g, h, 1)
                    project(g, h, 2)
                if not last and 8 <= h < 8 + NT:
                    transposed(g + 1, h - 8)

            for i in range(4):
                high_part(i)
            for t in range(NT):
                transposed(0, t)
            for i in range(4, len(NAMES)):
                high_part(i)
            split(0)
            for h in range(H):
                step(0, h, True, False)
            split(1)
            with act.Fori(1, NG - 1) as g:
                for h in range(H):
                    step(g, h, False, False)
                split(g + 1)
            for h in range(H + 2):
                step(NG - 1, h, False, True)

        @block.tensor
        def _(pe):
            def three(out, lhs, rhs, start, stop, **kw):
                pairs = [(0, 0), (0, 1), (1, 0)]
                for n, (a, b) in enumerate(pairs):
                    last = pe.matmul(out, lhs[a], rhs[b], start=start and n == 0, stop=stop and n == 2, **kw)
                return last

            use = [0]

            def bank():
                if use[0] >= 8:
                    pe.wait_ge(s_prepev, use[0] - 7)
                use[0] += 1
                return banks[(use[0] - 1) % 8]

            pe.wait_ge(s_ident, IDENT_READY)
            pe.wait_ge(s_vec, 80)
            pe.transpose(bank()[:, 0:5 * H], vrow[:, :], ident[0:5 * H, 0:5 * H]).then_inc(s_prep, 1)
            for n in range(2):
                for c in range(DC):
                    i = 2 * n + c
                    pe.wait_ge(s_raw[i % 2], 16 * (i // 2 + 1))
                    for f in range(4):
                        b = bank()
                        for j in range(4):
                            h = 4 * f + j
                            last = pe.transpose(b[:, j * P:(j + 1) * P], raw[i % 2][:, h * P:(h + 1) * P], ident[:, :])
                        last.then_inc(s_prep, 1)
                pe.wait_ge(s_prepev, 1 + EARLY_PER * n + 8)
                for c in range(DC):
                    b = bank()
                    for h in range(H):
                        last = pe.matmul(b[:, 0:D], wt[:, h, c * P:(c + 1) * P], wt[:, h, 0:D],
                                         start=h == 0, stop=h == H - 1)
                    last.then_inc(s_prep, 1)
                b = bank()
                for h in range(H):
                    v = (0, 3)[n] * H + h
                    last = pe.matmul(b[0:1, 0:D + 1], vecs[:, v:v + 1], wt[:, h, :], start=h == 0, stop=h == H - 1)
                last.then_inc(s_prep, 1)
                b = bank()
                pe.wait_ge(s_prepev, 1 + EARLY_PER * n + 11)
                pe.wait_ge(s_ones, 1)
                pe.matmul(b[:, 0:D + 1], ones[0:1, :], urow[:, :], start=True, stop=True).then_inc(s_prep, 1)

            def transposes(g, t):
                tr_read.wait(pe, g, t - 1)
                if t == 0:
                    xn_ready.wait(pe, g, 0)
                    cin_in.wait(pe, g, 15)
                    rr_ready.wait(pe, g, -1)
                for s, src in enumerate((xin, cin)):
                    for c in range(DC):
                        last = pe.transpose(tr_ps[:, (2 * s + c) * P:(2 * s + c + 1) * P],
                                            src[:, t, c * P:(c + 1) * P], ident[:, :])
                last.then_inc(tr_full.sem, 1)

            def gram_products(g, t):
                tr_read.wait(pe, g, t)
                gr_read.wait(pe, g, t - 1)
                for n, src in enumerate((xs, cs)):
                    for c in range(DC):
                        last = pe.matmul(gr_ps[:, n * D:(n + 1) * D], src[:, c, t * P:(t + 1) * P],
                                         gram[:, n, c, :], start=c == 0, stop=c == DC - 1)
                last.then_inc(gr_full.sem, 1)

            def norms(g):
                tr_read.wait(pe, g, NT - 1)
                diag_ready.wait(pe, g, 0)
                pe.matmul(tr_ps[:, :], ones[:, :], diag[:, :, :].rearrange("p t n -> p (t n)"),
                          start=True, stop=True).then_inc(rk_full.sem, 1)

            def prob_transpose(g, h):
                p_ready.wait(pe, g, h)
                for q in range(2):
                    last = pe.transpose(at_ps[:, q * P:(q + 1) * P],
                                        prob[:, 2 * q:2 * q + 2, :].rearrange("p t l -> p (t l)"), ident[:, :])
                last.then_inc(pt_full.sem, 1)

            def attend(g, h):
                pt_ready.wait(pe, g, h)
                pj_read.wait(pe, g, 3 * (h + 1 - h % 2))
                ao_ready.wait(pe, g, h - 1)
                for t in range(NT):
                    last = pe.matmul(pv_ps[:, t * P:(t + 1) * P],
                                     v_sb[:, (h // 2) % 2, t, (h % 2) * HD:(h % 2 + 1) * HD],
                                     pt[:, t, :], start=True, stop=True)
                last.then_inc(pv_full.sem, 1)

            def scores(g, h):
                pj_read.wait(pe, g, 3 * h + 2)
                pt_ready.wait(pe, g, h - 1)
                for t in range(NT):
                    for b in range(2):
                        s = slice(t * P + b * SEQ, t * P + (b + 1) * SEQ)
                        last = pe.matmul(at_ps[b * SEQ:(b + 1) * SEQ, t * SEQ:(t + 1) * SEQ],
                                         q_sb[:, s], k_sb[:, s], start=True, stop=True)
                last.then_inc(qk_full.sem, 1)

            def output(g, h):
                ao_ready.wait(pe, g, h)
                if h % H == 0:
                    x1_ready.wait(pe, g + h // H, -1)
                for t in range(NT):
                    s = slice(t * P, (t + 1) * P)
                    last = three(o_ps[t // 2][:, (t % 2) * D:(t % 2 + 1) * D], (ao_hi[:, s], ao_lo[:, s]),
                                 (wo_hi[:, h % H, :], wo_lo[:, h % H, :]),
                                 start=h % H == 0 and t % 2 == 0, stop=h % H == H - 1, skip_group_check=True)
                last.then_inc(o_full.sem, 1)

            def bank_for(g, u):
                pj_read.wait(pe, g, u - 2)
                return pj_ps[u % 2]

            def values(g, h):
                b = bank_for(g, 3 * h)
                if h == 0:
                    split_lo.wait(pe, g, 0)
                pair = slice((h - h % 2) * HD, (h - h % 2 + 2) * HD)
                for i in range(2):
                    t = 2 * (h % 2) + i
                    s = slice(t * P, (t + 1) * P)
                    for c in range(DC):
                        last = three(b[:, i * 2 * HD:(i + 1) * 2 * HD], (ct_hi[:, c, s], ct_lo[:, c, s]),
                                     (w_hi["v"][:, c, pair], w_lo["v"][:, c, pair]), start=c == 0, stop=c == DC - 1)
                last.then_inc(pj_full.sem, 1)

            def project(g, h, j):
                b = bank_for(g, 3 * h + j)
                n, hi, lo = (("k", ct_hi, ct_lo), ("q", xt_hi, xt_lo))[j - 1]
                if h == 0:
                    split_lo.wait(pe, g, j - 1)
                cols = slice(h * HD, (h + 1) * HD)
                for c in range(DC):
                    last = three(b[:, :], (w_hi[n][:, c, cols], w_lo[n][:, c, cols]), (hi[:, c, :], lo[:, c, :]),
                                 start=c == 0, stop=c == DC - 1)
                last.then_inc(pj_full.sem, 1)

            def step(g, h, first, last):
                if h >= 2 or not first:
                    if h - 2 < H:
                        prob_transpose(g, h - 2)
                if h >= 3 or not first:
                    output(g, h - 3)
                if h >= 2 or not first:
                    if h - 2 < H:
                        attend(g, h - 2)
                if (h >= 1 or not first) and h - 1 < H:
                    scores(g, h - 1)
                if h < H:
                    values(g, h)
                    project(g, h, 1)
                    project(g, h, 2)
                if not last:
                    if 8 <= h < 8 + NT:
                        transposes(g + 1, h - 8)
                    if 9 <= h < 9 + NT:
                        gram_products(g + 1, h - 9)
                    if h == H - 1:
                        norms(g + 1)

            pe.wait_ge(s_prepev, 1 + 2 * EARLY_PER)
            for t in range(NT):
                transposes(0, t)
                gram_products(0, t)
            norms(0)
            pe.wait_ge(s_wlo, len(NAMES))
            for h in range(H):
                if h == 2:
                    pe.wait_ge(s_ptzero, 1)
                step(0, h, True, False)
            with pe.Fori(1, NG - 1) as g:
                for h in range(H):
                    step(g, h, False, False)
            for h in range(H + 3):
                step(NG - 1, h, False, True)

        @block.vector
        def _(dve):
            chain = Chain(dve, s_chain)
            use = [0]

            def prepared():
                use[0] += 1
                dve.wait_ge(s_prep, use[0])
                return banks[(use[0] - 1) % 8]

            def low_part(i):
                hi, lo = weight_parts(i)
                dve.wait_ge(s_whi, i + 1)
                dve.tensor_tensor(lo, raw[i % 2][:, :], hi.bitcast(F32), ALU.subtract).then_inc(s_wlo, 1)

            dve.tensor_copy(vecs[:, :], prepared()[:, 0:5 * H]).then_inc(s_prepev, 1)
            dve.wait_ge(s_prepev, 1)
            chain.link(dve.tensor_tensor(qscale[:, :], vecs[:, H:2 * H], vecs[:, 2 * H:3 * H], ALU.mult))
            chain.mark(dve.tensor_tensor(qbias[:, :], vecs[:, 0:H], qscale[:, :], ALU.mult))
            dve.wait_ge(s_tanh, 1)
            dve.tensor_scalar(obias[:, :], obias[:, :], tg[:, 0:1], None, ALU.mult).then_inc(s_obias, 1)
            for n in range(2):
                v = (0, 3)[n] * H
                chain.link(dve.tensor_copy(wt[:, :, D:D + 1], vecs[:, v:v + H].unsqueeze(2)))
                for c in range(DC):
                    low_part(2 * n + c)
                    for f in range(4):
                        dve.tensor_copy(wt[:, 4 * f:4 * f + 4, c * P:(c + 1) * P],
                                        prepared()[:, :].rearrange("p (h n) -> p h n", h=4)).then_inc(s_prepev, 1)
                for c in range(DC):
                    dve.tensor_copy(gram[:, n, c, :], prepared()[:, 0:D]).then_inc(s_prepev, 1)
                dve.tensor_copy(urow[:, :], prepared()[0:1, 0:D + 1]).then_inc(s_prepev, 1)
                b = prepared()
                dve.tensor_scalar(gram_row[:, n, 0:D], b[:, 0:D], 2.0, None, ALU.mult)
                dve.tensor_copy(gram_row[:, n, D:D + 1], b[:, D:D + 1]).then_inc(s_prepev, 1)
            dve.wait_ge(s_prepev, 1 + 2 * EARLY_PER)

            def tile_stats(g, t):
                if t == 0:
                    xin_in.wait(dve, g, 15)
                chain.mark(dve.bn_stats(stats[:, t, :], xin[:, t, :]))

            def layernorm(g):
                chain.wait()
                moments(dve, chain, mean[:, :], var_eps[:, :], nt_t[:, :], stats)
                rsqrt(dve, chain, rstd[:, :], nt_t[:, :], var_eps[:, :])
                for t in range(NT):
                    last = dve.tensor_scalar(xin[:, t, :], xin[:, t, :], mean[:, t:t + 1], rstd[:, t:t + 1],
                                             ALU.subtract, ALU.mult)
                last.then_inc(xn_ready.sem, 1)

            def gram_sums(g, t):
                gr_full.wait(dve, g, t)
                for n, src in enumerate((xin, cin)):
                    chain.link(dve.tensor_tensor(gram_t[:, :], gr_ps[:, n * D:(n + 1) * D],
                                                 gram_row[:, n, 0:D], ALU.add))
                    last = dve.tensor_tensor_reduce(gram_j[:, :], gram_t[:, :], src[:, t, :], 1.0, 0.0, ALU.mult,
                                                    ALU.add, sums[:, n * NT + t:n * NT + t + 1])
                    if n == 0:
                        chain.link(last)
                last.then_inc(gr_read.sem, 1)

            def norm_factors(g):
                gr_read.wait(dve, g, NT - 1)
                for n in range(2):
                    half = slice(n * NT, (n + 1) * NT)
                    chain.mark(dve.tensor_scalar(sums_b[:, half], sums[:, half], gram_row[:, n, D:D + 1],
                                                 1.0 / INNER, ALU.add, ALU.mult))
                chain.wait()
                chain.link(dve.tensor_scalar(sums_b[:, :], sums_b[:, :], RMS_EPS, None, ALU.add))
                rsqrt(dve, chain, rqk[:, :], nqk_t[:, :], sums_b[:, :])
                for t in range(NT):
                    last = dve.tensor_scalar(diag[:, t, :], ident[:, :], rqk[:, NT + t:NT + t + 1], None, ALU.mult)
                last.then_inc(diag_ready.sem, 1)

            def score_factors(g):
                rk_full.wait(dve, g, 0)
                for t in range(NT):
                    for b in range(2):
                        rows = slice(b * SEQ, (b + 1) * SEQ)
                        last = dve.tensor_scalar(rr[rows, t, :], tr_ps[rows, t * P + b * SEQ:t * P + (b + 1) * SEQ],
                                                 rqk[rows, t:t + 1], float(HD) ** -0.5, ALU.mult, ALU.mult)
                last.then_inc(rr_ready.sem, 1)

            def split(g):
                for n, (lo, hi, src) in enumerate(((ct_lo, ct_hi, cs), (xt_lo, xt_hi, xs))):
                    split_hi.wait(dve, g, n)
                    dve.tensor_tensor(lo[:, :, :], src[:, :, :], hi[:, :, :].bitcast(F32),
                                      ALU.subtract).then_inc(split_lo.sem, 1)

            def prob_copy(g, h):
                pt_full.wait(dve, g, h)
                for q in range(2):
                    for b in range(2):
                        src = at_ps[q * SEQ:(q + 1) * SEQ, 0:2 * P].rearrange("p (t s) -> p t s", t=2)
                        last = dve.tensor_copy(pt[b * SEQ:(b + 1) * SEQ, q::2, b * SEQ:(b + 1) * SEQ],
                                               src[:, :, b * SEQ:(b + 1) * SEQ])
                last.then_inc(pt_ready.sem, 1)

            def attn_lo(g, h):
                v = 4 * H + h % H
                ao_hi_ready.wait(dve, g, h)
                dve.scalar_tensor_tensor(out=ao_lo[:, :], in0=pv_ps[:, :], scalar=vecs[:, v:v + 1],
                                         in1=ao_hi[:, :].bitcast(F32), op0=ALU.add,
                                         op1=ALU.subtract).then_inc(ao_ready.sem, 1)

            def softmax(g, h):
                qk_full.wait(dve, g, h)
                chain.link(dve.tensor_tensor(logit[:, :, :], at_ps[:, 0:NT * SEQ].rearrange("p (t l) -> p t l", t=NT),
                                             rr[:, :, :], ALU.mult))
                chain.link(dve.tensor_reduce(rmax[:, :], logit[:, :, :], AXX, ALU.max))
                dve.tensor_tensor(logit[:, :, :], logit[:, :, :],
                                  rmax[:, :].unsqueeze(2).to_broadcast([P, NT, SEQ]),
                                  ALU.subtract).then_inc(l_ready.sem, 1)
                e_ready.wait(dve, g, h)
                chain.link(dve.tensor_reduce(rsum[:, :], expo[:, :, :], AXX, ALU.add))
                chain.link(dve.reciprocal(rinv[:, :], rsum[:, :]))
                dve.tensor_tensor(prob[:, :, :], expo[:, :, :], rinv[:, :].unsqueeze(2).to_broadcast([P, NT, SEQ]),
                                  ALU.mult).then_inc(p_ready.sem, 1)

            def residual(g):
                o_full.wait(dve, g, H - 1)
                xres_ready.wait(dve, g, 0)
                for i in range(2):
                    rows = xres[:, 2 * i:2 * i + 2, :].rearrange("p t d -> p (t d)")
                    last = dve.scalar_tensor_tensor(out=rows, in0=o_ps[i][:, :], scalar=tg[:, 0:1], in1=rows,
                                                    op0=ALU.mult, op1=ALU.add)
                last.then_inc(x1_ready.sem, 1)

            def step(g, h, first, last):
                if h >= 2 or not first:
                    if h - 2 < H:
                        prob_copy(g, h - 2)
                        attn_lo(g, h - 2)
                if (h >= 1 or not first) and h - 1 < H:
                    softmax(g, h - 1)
                if h == 0 and not first:
                    score_factors(g)
                if h == 2 and not first:
                    residual(g - 1)
                if not last:
                    if 3 <= h < 3 + NT:
                        tile_stats(g + 1, h - 3)
                    if h == 7:
                        layernorm(g + 1)
                    if 9 <= h < 9 + NT:
                        gram_sums(g + 1, h - 9)
                    if h == 13:
                        norm_factors(g + 1)

            for t in range(NT):
                tile_stats(0, t)
            layernorm(0)
            for t in range(NT):
                gram_sums(0, t)
            norm_factors(0)
            score_factors(0)
            for i in range(4, len(NAMES)):
                low_part(i)
            split(0)
            for h in range(H):
                if h == 2:
                    dve.wait_ge(s_ptzero, 1)
                step(0, h, True, False)
            done = chain.n
            with dve.Fori(1, NG - 1) as g:
                chain.start(done + (g - 1) * CHAIN_PER)
                split(g)
                for h in range(H):
                    step(g, h, False, False)
                assert chain.n == CHAIN_PER, chain.n
            chain.start(done + (NG - 2) * CHAIN_PER)
            split(NG - 1)
            for h in range(H + 2):
                step(NG - 1, h, False, True)
            residual(NG - 1)


def remaining_layers(nc, x1_dram, ctx, g_xattn, g_ffn, w0, b0, lora_a, lora_b, gate_w, gate_b, a1, b1, wg1, out):
    CHAIN_PER = 97
    c_t = ctx.rearrange("b s d -> (b s) d").rearrange("(g t p) d -> g p t d", g=NG, p=P)
    out_t = out.rearrange("b s d -> (b s) d").rearrange("(g t p) d -> g p t d", g=NG, p=P)
    C0, C1 = E0 * R0, E1 * R1
    CT1 = C1 // P
    B_NT = 2 * NT
    with ExitStack() as stack:
        def sb(name, shape, dt=F32):
            return stack.enter_context(nc.sbuf_tensor(name, shape, dt))

        def sem(name):
            return stack.enter_context(nc.semaphore(name))

        def signal(name, per):
            return Signal(sem(name), per)

        def both(name, shape):
            return sb(name + "_hi", shape, F32R), sb(name + "_lo", shape, F32R)

        w0t = both("w0t", [P, DC, D])
        a0t = both("a0t", [P, DC, C0 + E0])
        b0t = both("b0t", [P, D])
        a1t = both("a1t", [P, DC, C1])
        g1t = both("g1t", [P, DC, E1])
        b1t = both("b1t", [P, CT1, D])
        raw_w0 = sb("raw_w0", [P, DC, D])
        raw_a0 = sb("raw_a0", [P, D])
        raw_g = sb("raw_g", [E0, 2, D])
        raw_b0 = sb("raw_b0", [P, 2, E0, R0])
        raw_a1 = sb("raw_a1", [P, CT1, D])
        raw_b1 = sb("raw_b1", [P, 2, E1, R1])
        ident = sb("ident2", [P, P])
        tg = sb("tg2", [P, 4])
        tgh = sb("tgh", [P, 1])
        bias0 = sb("bias0", [P, D])
        gbias = sb("gbias", [P, E0])
        prefer = sb("prefer", [P, NT, E0])

        x1 = sb("x1", [P, NT, D])
        xn1 = sb("xn1", [P, NT, D])
        stats = sb("stats2", [P, NT, 6])
        mean = sb("mean2", [P, NT])
        var_eps = sb("var_eps2", [P, NT])
        rstd = sb("rstd2", [P, NT])
        ntmp = sb("ntmp2", [P, NT])
        xt1 = both("xt1", [P, DC, GT])
        xa = sb("xa", [P, NT, C0])
        lg0 = sb("lg0", [P, NT, E0])
        work = sb("work", [P, NT, E0])
        pick = [sb(f"pick{i}", [P, NT, E0]) for i in range(2)]
        top = sb("top", [P, 2, NT])
        best = sb("best", [P, NT])
        gexp = sb("gexp", [P, NT])
        gw = sb("gw", [P, 2, NT])
        gates = sb("gates", [P, NT, E0])
        xg = sb("xg", [P, NT, C0])
        xgt = both("xgt", [P, GT])
        x2 = sb("x2", [P, NT, D])
        xn2 = sb("xn2", [P, NT, D])
        cin = sb("cin2", [P, NT, D])
        ct = sb("ct", [P, DC, GT])
        csum = sb("csum", [P, NT])
        th = sb("th", [P, B_NT, DC, D])
        x3 = sb("x3", [P, NT, D])
        xn3 = sb("xn3", [P, NT, D])
        xt3 = both("xt3", [P, DC, GT])
        lg1 = sb("lg1", [P, NT, E1])
        ex1 = sb("ex1", [P, NT, E1])
        coef = sb("coef", [P, NT, E1])
        hm = sb("hm", [P, NT, C1])
        hmt = both("hmt", [P, NT, CT1, P])
        banks = [stack.enter_context(nc.psum_tensor(f"ban2k{i}", [P, 512], F32)) for i in range(8)]

        s_ident = sem("s_ident2")
        s_const = sem("s_const")
        s_raw = sem("s_rawin")
        s_gate = sem("s_gate2")
        s_tanh = sem("s_tanh2")
        s_scaled = sem("s_scaled")
        s_prep = sem("s_prep2")
        s_prep_hi = sem("s_prep_hi")
        s_prep_lo = sem("s_prep_lo")
        s_chain = sem("s_chain2")
        x1_in = signal("x1_in2", 16)
        cin_in = signal("cin_in2", 16)
        out_sent = signal("out_sent", 16)
        x1b_ready = signal("x1b_ready", 1)
        xn1_ready = signal("xn1_ready", 1)
        xn2_ready = signal("xn2_ready", 1)
        xn3_ready = signal("xn3_ready", 1)
        xt1_hi_ready = signal("xt1_hi_ready", 2)
        xt1_ready = signal("xt1_ready", 2)
        xa_ready = signal("xa_ready", 2)
        lg0_ready = signal("lg0_ready", 2)
        gap_ready = signal("gap_ready", 1)
        gexp_ready = signal("gexp_ready", 1)
        gates_ready = signal("gates_ready", 1)
        xg_ready = signal("xg_ready", 1)
        xgt_hi_ready = signal("xgt_hi_ready", 1)
        xgt_ready = signal("xgt_ready", 1)
        x2_ready = signal("x2_ready", 2)
        ct_ready = signal("ct_ready", 2)
        th_ready = signal("th_ready", B_NT)
        x3_ready = signal("x3_ready", 2)
        xt3_hi_ready = signal("xt3_hi_ready", 2)
        xt3_ready = signal("xt3_ready", 2)
        lg1_ready = signal("lg1_ready", 1)
        lg1_read = signal("lg1_read", 1)
        ex1_ready = signal("ex1_ready", 1)
        hm_ready = signal("hm_ready", NT)
        hmt_hi_ready = signal("hmt_hi_ready", NT)
        hmt_ready = signal("hmt_ready", NT)
        y_ready = signal("y_ready", 2)

        RING = [("xt1", 2, "A", xt1_ready), ("ct", 2, "B", ct_ready), ("aff", B_NT, "B", th_ready),
                ("xa", 2, "A", lg0_ready), ("att", 2, "B", x3_ready), ("xg", 1, "A", xgt_ready),
                ("xt3", 2, "B", xt3_ready), ("lora", 2, "A", x2_ready), ("lg", 1, "B", lg1_read),
                ("h", NT, "B", hm_ready), ("hm", NT, "B", hmt_ready), ("y", 2, "B", y_ready)]
        full = {name: signal(f"{name}_full", n) for name, n, _, _ in RING}
        USES = [(name, i, part, read) for name, n, part, read in RING for i in range(n)]
        PLACE = {(name, i): u for u, (name, i, _, _) in enumerate(USES)}
        assert len(USES) % len(banks) == 0

        def bank_of(name, i):
            return banks[PLACE[name, i] % len(banks)]

        block = stack.enter_context(nc.Block())

        @block.sync
        def _(sp):
            def at(t, g):
                return t[g] if isinstance(g, int) else t[bass.ds(g, 1)].rearrange("g p t d -> p (g t) d")

            def load_x1(g):
                x2_ready.wait(sp, g - 1, 1)
                sp.dma_start(x1[:, :, :], at(x1_dram, g)).then_inc(x1_in.sem, 16)

            def load_ctx(g):
                x3_ready.wait(sp, g - 1, 1)
                sp.dma_start(cin[:, :, :], at(c_t, g)).then_inc(cin_in.sem, 16)

            def store(g):
                y_ready.wait(sp, g, 1)
                sp.dma_start(at(out_t, g), x3[:, :, :]).then_inc(out_sent.sem, 16)

            load_x1(0)
            sp.dma_start(raw_w0[:, :, :], w0.rearrange("(c p) d -> p c d", p=P)).then_inc(s_raw, 16)
            sp.dma_start(raw_a0[:, :], lora_a.rearrange("e r d -> (e r) d")).then_inc(s_raw, 16)
            sp.dma_start(raw_g[:, 0, :], gate_w).then_inc(s_raw, 16)
            sp.dma_start(raw_g[:, 1, :], wg1).then_inc(s_raw, 16)
            load_ctx(0)
            load_x1(1)
            with sp.Fori(1, NG - 1) as i:
                load_ctx(i)
                load_x1(i + 1)
                store(i - 1)
            load_ctx(NG - 1)
            store(NG - 2)
            store(NG - 1)
            out_sent.wait(sp, NG - 1, 15)

        @block.gpsimd
        def _(pool):
            pool.dma_start(tg[:, 0:2], g_xattn.partition_broadcast(P)).then_inc(s_gate, 16)
            pool.dma_start(tg[:, 2:4], g_ffn.partition_broadcast(P)).then_inc(s_gate, 16)
            pool.dma_start(bias0[:, :], b0.partition_broadcast(P)).then_inc(s_gate, 16)
            pool.dma_start(gbias[:, :], gate_b.partition_broadcast(P)).then_inc(s_gate, 16)
            identity(pool, s_ident, ident[:, :])
            for e in range(E0):
                pool.memset(prefer[:, :, e:e + 1], float(E0 - e)).then_inc(s_const, 1)
            pool.wait_ge(s_scaled, 1)

            def group(g):
                xn1_ready.wait(pool, g, 0)
                pool.tensor_tensor(x1[:, :, :], x1[:, :, :], bias0[:, :].unsqueeze(1).to_broadcast([P, NT, D]),
                                   ALU.add).then_inc(x1b_ready.sem, 1)

            group(0)
            with pool.Fori(1, NG) as g:
                group(g)

        def prep_uses():
            return [
                ([(raw_w0[:, o, c * P:(c + 1) * P], P, c * D + o * P) for c in range(DC) for o in range(2)],
                 [(0, DC * D, [t[:, :, :].rearrange("p c d -> p (c d)") for t in w0t])]),
                ([(raw_a0[:, c * P:(c + 1) * P], P, c * C0) for c in range(DC)]
                 + [(raw_g[:, w, c * P:(c + 1) * P], E0, DC * C0 + (w * DC + c) * E0) for w in range(2) for c in range(DC)],
                 [(c * C0, C0, [t[:, c, 0:C0] for t in a0t]) for c in range(DC)]
                 + [(DC * C0 + c * E0, E0, [t[:, c, C0:C0 + E0] for t in a0t]) for c in range(DC)]
                 + [(DC * C0 + DC * E0, DC * E1, [t[:, :, :].rearrange("p c e -> p (c e)") for t in g1t])]),
                ([(raw_b0[:, o, :, :].rearrange("p e r -> p (e r)"), P, o * P) for o in range(2)],
                 [(0, D, [t[:, :] for t in b0t])]),
                *[([(raw_a1[:, r, c * P:(c + 1) * P], P, r * P) for r in range(CT1)],
                   [(0, C1, [t[:, c, :] for t in a1t])]) for c in range(DC)],
                *[([(raw_b1[:, o, 2 * k:2 * k + 2, :].rearrange("p e r -> p (e r)"), P, (k - k0) * D + o * P)
                    for k in (k0, k0 + 1) for o in range(2)],
                   [(0, 2 * D, [t[:, k0:k0 + 2, :].rearrange("p k d -> p (k d)") for t in b1t])])
                  for k0 in range(0, CT1, 2)],
            ]

        @block.scalar
        def _(act):
            for o in range(2):
                act.dma_start(raw_b0[:, o, :, :], lora_b[:, o * P:(o + 1) * P, :].rearrange("e p r -> p e r")).then_inc(s_raw, 16)
                act.dma_start(raw_b1[:, o, :, :], b1[:, o * P:(o + 1) * P, :].rearrange("e p r -> p e r")).then_inc(s_raw, 16)
            act.dma_start(raw_a1[:, :, :], a1.rearrange("e r d -> (e r) d").rearrange("(c p) d -> p c d", p=P)).then_inc(s_raw, 16)
            act.wait_ge(s_gate, 64)
            act.activation(tg[:, :], tg[:, :], ACT.Tanh).then_inc(s_tanh, 1)
            for u, (_, parts) in enumerate(prep_uses()):
                act.wait_ge(s_prep, u + 1)
                for at, n, (hi, _) in parts:
                    last = act.activation(hi, banks[u][:, at:at + n], ACT.Copy)
                last.then_inc(s_prep_hi, 1)

            def copies(g, name, dst, ready):
                for i in range(2):
                    full[name].wait(act, g, i)
                    act.activation(dst[:, :, 2 * i * P:2 * (i + 1) * P].rearrange("p c (t n) -> p t c n", t=2),
                                   bank_of(name, i)[:, :].rearrange("p (t c n) -> p t c n", t=2, c=DC),
                                   ACT.Copy).then_inc(ready.sem, 1)

            def stage(name, g):
                if name == "xt1":
                    copies(g, name, xt1[0], xt1_hi_ready)
                elif name == "ct":
                    copies(g, name, ct, ct_ready)
                elif name == "aff":
                    for b in range(B_NT):
                        full[name].wait(act, g, b)
                        act.activation(th[:, b, :, :].rearrange("p c d -> p (c d)"), bank_of(name, b)[:, :], ACT.Tanh,
                                       scale=0.5 * float(SEQ) ** -0.5).then_inc(th_ready.sem, 1)
                elif name == "xa":
                    for i in range(2):
                        full[name].wait(act, g, i)
                        act.activation(xa[:, 2 * i:2 * i + 2, :],
                                       bank_of(name, i)[:, 0:2 * (C0 + E0)].rearrange("p (t n) -> p t n", t=2)[:, :, 0:C0],
                                       ACT.Copy).then_inc(xa_ready.sem, 1)
                    gap_ready.wait(act, g, 0)
                    act.activation(gexp[:, :], best[:, :], ACT.Exp).then_inc(gexp_ready.sem, 1)
                elif name == "xg":
                    full[name].wait(act, g, 0)
                    act.activation(xgt[0][:, :], bank_of(name, 0)[:, :], ACT.Copy).then_inc(xgt_hi_ready.sem, 1)
                elif name == "xt3":
                    copies(g, name, xt3[0], xt3_hi_ready)
                elif name == "lg":
                    lg1_ready.wait(act, g, 0)
                    act.activation(ex1[:, :, :], lg1[:, :, :], ACT.Exp).then_inc(ex1_ready.sem, 1)
                elif name == "hm":
                    for t in range(NT):
                        full[name].wait(act, g, t)
                        act.activation(hmt[0][:, t, :, :].rearrange("p k n -> p (k n)"), bank_of(name, t)[:, :],
                                       ACT.Copy).then_inc(hmt_hi_ready.sem, 1)

            def iteration(i, parts):
                for name, _, part, _ in RING:
                    if part in parts:
                        stage(name, i if part == "A" else i - 1)

            iteration(0, "A")
            iteration(1, "AB")
            with act.Fori(2, NG) as i:
                iteration(i, "AB")
            iteration(NG, "B")

        @block.tensor
        def _(pe):
            def three(out, lhs, rhs, start, stop, **kw):
                pairs = [(0, 0), (0, 1), (1, 0)]
                for n, (a, b) in enumerate(pairs):
                    last = pe.matmul(out, lhs[a], rhs[b], start=start and n == 0, stop=stop and n == 2, **kw)
                return last

            pe.wait_ge(s_ident, IDENT_READY)
            pe.wait_ge(s_raw, 9 * 16)
            for u, (blocks, _) in enumerate(prep_uses()):
                for src, rows, at in blocks:
                    last = pe.transpose(banks[u][:, at:at + rows], src, ident[0:rows, 0:rows])
                last.then_inc(s_prep, 1)
            pe.wait_ge(s_prep_lo, len(prep_uses()))

            def take(i, parts, before, name, j):
                u = PLACE[name, j]
                for back in range(len(banks), 2 * len(USES), len(banks)):
                    v, it = (u - back) % len(USES), i - (0 if back <= u else (back - u - 1) // len(USES) + 1)
                    prev, k, part, read = USES[v]
                    if part in (parts if back <= u else before):
                        read.wait(pe, it if part == "A" else it - 1, k)
                        break
                return banks[u % len(banks)]

            def stage(name, g, i, parts, before):
                def bank(j):
                    return take(i, parts, before, name, j)

                def turned(j, src):
                    b = bank(j)
                    for t in range(2):
                        for c in range(DC):
                            last = pe.transpose(b[:, (t * DC + c) * P:(t * DC + c + 1) * P],
                                                src[:, 2 * j + t, c * P:(c + 1) * P], ident[:, :])
                    last.then_inc(full[name].sem, 1)

                if name == "xt1":
                    xn1_ready.wait(pe, g, 0)
                    for j in range(2):
                        turned(j, xn1)
                elif name == "ct":
                    cin_in.wait(pe, g, 15)
                    for j in range(2):
                        turned(j, cin)
                elif name == "xt3":
                    xn3_ready.wait(pe, g, 0)
                    for j in range(2):
                        turned(j, xn3)
                elif name == "aff":
                    xn2_ready.wait(pe, g, 0)
                    for j in range(B_NT):
                        b, t, rows = bank(j), j // 2, slice(j % 2 * SEQ, (j % 2 + 1) * SEQ)
                        for c in range(DC):
                            last = pe.matmul(b[:, c * D:(c + 1) * D], xn2[rows, t, c * P:(c + 1) * P], cin[rows, t, :],
                                             start=True, stop=True)
                        last.then_inc(full[name].sem, 1)
                elif name == "xa":
                    for j in range(2):
                        xt1_ready.wait(pe, g, j)
                        b = bank(j)
                        for t in range(2):
                            s = slice((2 * j + t) * P, (2 * j + t + 1) * P)
                            for c in range(DC):
                                last = three(b[:, t * (C0 + E0):(t + 1) * (C0 + E0)], [h[:, c, s] for h in xt1],
                                             [h[:, c, :] for h in a0t], start=c == 0, stop=c == DC - 1)
                        last.then_inc(full[name].sem, 1)
                elif name == "att":
                    for j in range(2):
                        ct_ready.wait(pe, g, j)
                        th_ready.wait(pe, g, 4 * j + 3)
                        b = bank(j)
                        for t in range(2):
                            for c in range(DC):
                                for h in range(2):
                                    tok = (2 * j + t) * P + h * SEQ
                                    last = pe.matmul(b[h * SEQ:(h + 1) * SEQ, t * D:(t + 1) * D],
                                                     ct[:, c, tok:tok + SEQ], th[:, 4 * j + 2 * t + h, c, :],
                                                     start=c == 0, stop=c == DC - 1)
                        last.then_inc(full[name].sem, 1)
                elif name == "xg":
                    xg_ready.wait(pe, g, 0)
                    b = bank(0)
                    for t in range(NT):
                        last = pe.transpose(b[:, t * P:(t + 1) * P], xg[:, t, :], ident[:, :])
                    last.then_inc(full[name].sem, 1)
                elif name == "lora":
                    xgt_ready.wait(pe, g, 0)
                    for j in range(2):
                        b = bank(j)
                        for t in range(2):
                            s = slice((2 * j + t) * P, (2 * j + t + 1) * P)
                            dst = b[:, t * D:(t + 1) * D]
                            for c in range(DC):
                                three(dst, [h[:, c, s] for h in xt1], [h[:, c, :] for h in w0t],
                                      start=c == 0, stop=False)
                            last = three(dst, [h[:, s] for h in xgt], [h[:, :] for h in b0t], start=False, stop=True)
                        last.then_inc(full[name].sem, 1)
                elif name == "lg":
                    b = bank(0)
                    for t in range(NT):
                        xt3_ready.wait(pe, g, t // 2)
                        s = slice(t * P, (t + 1) * P)
                        for c in range(DC):
                            last = three(b[:, t * E1:(t + 1) * E1], [h[:, c, s] for h in xt3],
                                         [h[:, c, :] for h in g1t], start=c == 0, stop=c == DC - 1)
                    last.then_inc(full[name].sem, 1)
                elif name == "h":
                    for t in range(NT):
                        b = bank(t)
                        s = slice(t * P, (t + 1) * P)
                        for c in range(DC):
                            last = three(b[:, :], [h[:, c, s] for h in xt3], [h[:, c, :] for h in a1t],
                                         start=c == 0, stop=c == DC - 1)
                        last.then_inc(full[name].sem, 1)
                elif name == "hm":
                    for t in range(NT):
                        hm_ready.wait(pe, g, t)
                        b = bank(t)
                        for k in range(CT1):
                            last = pe.transpose(b[:, k * P:(k + 1) * P], hm[:, t, k * P:(k + 1) * P], ident[:, :])
                        last.then_inc(full[name].sem, 1)
                elif name == "y":
                    for j in range(2):
                        b = bank(j)
                        for t in range(2):
                            hmt_ready.wait(pe, g, 2 * j + t)
                            for k in range(CT1):
                                last = three(b[:, t * D:(t + 1) * D], [h[:, 2 * j + t, k, :] for h in hmt],
                                             [h[:, k, :] for h in b1t], start=k == 0, stop=k == CT1 - 1)
                        last.then_inc(full[name].sem, 1)

            def iteration(i, parts, before):
                for name, _, part, _ in RING:
                    if part in parts:
                        stage(name, i if part == "A" else i - 1, i, parts, before)

            iteration(0, "A", "")
            iteration(1, "AB", "A")
            iteration(2, "AB", "AB")
            with pe.Fori(3, NG) as i:
                iteration(i, "AB", "AB")
            iteration(NG, "B", "AB")

        @block.vector
        def _(dve):
            chain = Chain(dve, s_chain)
            dve.wait_ge(s_tanh, 1)
            dve.tensor_scalar(bias0[:, :], bias0[:, :], tg[:, 2:3], None, ALU.mult).then_inc(s_scaled, 1)
            chain.mark(dve.tensor_scalar(tgh[:, :], tg[:, 1:2], 0.5, None, ALU.mult))
            for u, (_, parts) in enumerate(prep_uses()):
                dve.wait_ge(s_prep_hi, u + 1)
                for at, n, (hi, lo) in parts:
                    last = dve.tensor_tensor(lo, banks[u][:, at:at + n], hi.bitcast(F32), ALU.subtract)
                last.then_inc(s_prep_lo, 1)
            dve.wait_ge(s_const, E0)
            chain.wait()

            def wide(v):
                return v.unsqueeze(2).to_broadcast([P, NT, E0])

            def layernorm(src, dst, ready):
                for t in range(NT):
                    chain.mark(dve.bn_stats(stats[:, t, :], src[:, t, :]))
                chain.wait()
                moments(dve, chain, mean[:, :], var_eps[:, :], ntmp[:, :], stats)
                rsqrt(dve, chain, rstd[:, :], ntmp[:, :], var_eps[:, :])
                for t in range(NT):
                    last = dve.tensor_scalar(dst[:, t, :], src[:, t, :], mean[:, t:t + 1], rstd[:, t:t + 1],
                                             ALU.subtract, ALU.mult)
                last.then_inc(ready.sem, 1)

            def low_parts(g, name, parts, hi_ready, ready):
                for j in range(2):
                    hi_ready.wait(dve, g, j)
                    hi, lo = [h[:, :, 2 * j * P:2 * (j + 1) * P].rearrange("p c (t n) -> p t c n", t=2) for h in parts]
                    dve.tensor_tensor(lo, bank_of(name, j)[:, :].rearrange("p (t c n) -> p t c n", t=2, c=DC),
                                      hi.bitcast(F32), ALU.subtract).then_inc(ready.sem, 1)

            def first_of_largest(values, top, pick):
                chain.link(dve.tensor_reduce(top, values, AXX, ALU.max))
                chain.link(dve.tensor_tensor(work[:, :, :], values, wide(top), ALU.is_ge))
                chain.link(dve.tensor_tensor(work[:, :, :], work[:, :, :], prefer[:, :, :], ALU.mult))
                chain.link(dve.tensor_reduce(best[:, :], work[:, :, :], AXX, ALU.max))
                chain.link(dve.tensor_tensor(pick, work[:, :, :], wide(best[:, :]), ALU.is_equal))

            def stage(name, g):
                if name == "xt1":
                    low_parts(g, name, xt1, xt1_hi_ready, xt1_ready)
                elif name == "ct":
                    cin_in.wait(dve, g, 15)
                    chain.link(dve.tensor_reduce(csum[:, :], cin[:, :, :], AXX, ALU.add))
                    chain.link(dve.tensor_scalar(csum[:, :], csum[:, :], tgh[:, 0:1], None, ALU.mult))
                    for t in range(NT):
                        chain.mark(dve.tensor_scalar(x2[:, t, :], x2[:, t, :], csum[:, t:t + 1], None, ALU.add))
                elif name == "xa":
                    for j in range(2):
                        xa_ready.wait(dve, g, j)
                        src = bank_of(name, j)[:, 0:2 * (C0 + E0)].rearrange("p (t n) -> p t n", t=2)[:, :, C0:C0 + E0]
                        dve.tensor_tensor(lg0[:, 2 * j:2 * j + 2, :], src,
                                          gbias[:, :].unsqueeze(1).to_broadcast([P, 2, E0]),
                                          ALU.add).then_inc(lg0_ready.sem, 1)
                    lg0_ready.wait(dve, g, 1)
                    first_of_largest(lg0[:, :, :], top[:, 0, :], pick[0][:, :, :])
                    chain.link(dve.scalar_tensor_tensor(out=lg0[:, :, :], in0=pick[0][:, :, :], scalar=-BIG,
                                                        in1=lg0[:, :, :], op0=ALU.mult, op1=ALU.add))
                    first_of_largest(lg0[:, :, :], top[:, 1, :], pick[1][:, :, :])
                    dve.tensor_tensor(best[:, :], top[:, 1, :], top[:, 0, :], ALU.subtract).then_inc(gap_ready.sem, 1)
                    gexp_ready.wait(dve, g, 0)
                    chain.link(dve.tensor_scalar(gw[:, 1, :], gexp[:, :], 1.0, None, ALU.add))
                    chain.link(dve.reciprocal(gw[:, 0, :], gw[:, 1, :]))
                    chain.link(dve.tensor_tensor(gw[:, 1, :], gexp[:, :], gw[:, 0, :], ALU.mult))
                    for k in range(K0):
                        chain.link(dve.tensor_tensor(pick[k][:, :, :], pick[k][:, :, :], wide(gw[:, k, :]), ALU.mult))
                    chain.link(dve.tensor_tensor(gates[:, :, :], pick[0][:, :, :], pick[1][:, :, :], ALU.add))
                    dve.tensor_tensor(xg[:, :, :].rearrange("p t (e r) -> p (t e) r", r=R0),
                                      xa[:, :, :].rearrange("p t (e r) -> p (t e) r", r=R0),
                                      gates[:, :, :].rearrange("p t e -> p (t e)").unsqueeze(2).to_broadcast([P, NT * E0, R0]),
                                      ALU.mult).then_inc(xg_ready.sem, 1)
                elif name == "att":
                    for j in range(2):
                        full[name].wait(dve, g, j)
                        rows = slice(2 * j, 2 * j + 2)
                        if j == 0:
                            chain.wait()
                            out_sent.wait(dve, g - 1, 15)
                        dve.scalar_tensor_tensor(out=x3[:, rows, :].rearrange("p t d -> p (t d)"), in0=bank_of(name, j)[:, :],
                                                 scalar=tgh[:, 0:1], in1=x2[:, rows, :].rearrange("p t d -> p (t d)"),
                                                 op0=ALU.mult, op1=ALU.add).then_inc(x3_ready.sem, 1)
                    x3_ready.wait(dve, g, 1)
                    layernorm(x3, xn3, xn3_ready)
                elif name == "xg":
                    xgt_hi_ready.wait(dve, g, 0)
                    dve.tensor_tensor(xgt[1][:, :], bank_of(name, 0)[:, :], xgt[0][:, :].bitcast(F32),
                                      ALU.subtract).then_inc(xgt_ready.sem, 1)
                elif name == "xt3":
                    low_parts(g, name, xt3, xt3_hi_ready, xt3_ready)
                elif name == "lora":
                    x1b_ready.wait(dve, g, 0)
                    for j in range(2):
                        full[name].wait(dve, g, j)
                        rows = slice(2 * j, 2 * j + 2)
                        dve.scalar_tensor_tensor(out=x2[:, rows, :].rearrange("p t d -> p (t d)"), in0=bank_of(name, j)[:, :],
                                                 scalar=tg[:, 2:3], in1=x1[:, rows, :].rearrange("p t d -> p (t d)"),
                                                 op0=ALU.mult, op1=ALU.add).then_inc(x2_ready.sem, 1)
                    x2_ready.wait(dve, g, 1)
                    layernorm(x2, xn2, xn2_ready)
                elif name == "lg":
                    full[name].wait(dve, g, 0)
                    dve.tensor_copy(coef[:, :, :], bank_of(name, 0)[:, 0:NT * E1].rearrange(
                        "p (t e) -> p t e", t=NT)).then_inc(lg1_read.sem, 1)
                    lg1_read.wait(dve, g, 0)
                    first_of_largest(coef[:, :, :], top[:, 0, :], pick[0][:, :, :])
                    dve.tensor_tensor(lg1[:, :, :], coef[:, :, :], wide(top[:, 0, :]), ALU.subtract).then_inc(lg1_ready.sem, 1)
                    ex1_ready.wait(dve, g, 0)
                    chain.link(dve.tensor_reduce(best[:, :], ex1[:, :, :], AXX, ALU.add))
                    chain.link(dve.reciprocal(gw[:, 0, :], best[:, :]))
                    chain.link(dve.scalar_tensor_tensor(out=coef[:, :, :], in0=pick[0][:, :, :], scalar=EXPERT_SCALING,
                                                        in1=wide(gw[:, 0, :]), op0=ALU.mult, op1=ALU.mult))
                elif name == "h":
                    for t in range(NT):
                        full[name].wait(dve, g, t)
                        dve.tensor_tensor(hm[:, t, :].rearrange("p (e r) -> p e r", e=E1),
                                          bank_of(name, t)[:, :].rearrange("p (e r) -> p e r", e=E1),
                                          coef[:, t, :].unsqueeze(2).to_broadcast([P, E1, R1]),
                                          ALU.mult).then_inc(hm_ready.sem, 1)
                elif name == "hm":
                    for t in range(NT):
                        hmt_hi_ready.wait(dve, g, t)
                        hi, lo = [h[:, t, :, :].rearrange("p k n -> p (k n)") for h in hmt]
                        dve.tensor_tensor(lo, bank_of(name, t)[:, :], hi.bitcast(F32), ALU.subtract).then_inc(hmt_ready.sem, 1)
                elif name == "y":
                    for j in range(2):
                        full[name].wait(dve, g, j)
                        rows = x3[:, 2 * j:2 * j + 2, :].rearrange("p t d -> p (t d)")
                        dve.scalar_tensor_tensor(out=rows, in0=bank_of(name, j)[:, :], scalar=tg[:, 3:4], in1=rows,
                                                 op0=ALU.mult, op1=ALU.add).then_inc(y_ready.sem, 1)

            def next_norm(g):
                x1_in.wait(dve, g, 15)
                layernorm(x1, xn1, xn1_ready)

            def iteration(i, parts, last=False):
                for name, _, part, _ in RING:
                    if part in parts:
                        stage(name, i if part == "A" else i - 1)
                    if name == "h" and not last:
                        next_norm(i + 1)

            next_norm(0)
            iteration(0, "A")
            iteration(1, "AB")
            done = chain.n
            with dve.Fori(2, NG - 1) as i:
                chain.start(done + (i - 2) * CHAIN_PER)
                iteration(i, "AB")
                assert chain.n == CHAIN_PER, chain.n
            chain.start(done + (NG - 3) * CHAIN_PER)
            iteration(NG - 1, "AB", last=True)
            iteration(NG, "B", last=True)


_INS = ["x", "ctx_2048", "g_xattn", "g_ffn", "L0_xattn_q_w", "L0_xattn_q_b", "L0_xattn_ki_w", "L0_xattn_ki_b",
        "L0_xattn_vi_w", "L0_xattn_vi_b", "L0_xattn_o_w", "L0_xattn_o_b", "L0_xattn_nq_s", "L0_xattn_nki_s",
        "L0_ffn_W", "L0_ffn_b", "L0_ffn_lora_A", "L0_ffn_lora_B", "L0_ffn_gate_w", "L0_ffn_gate_b",
        "L1_ffn_A", "L1_ffn_Bw", "L1_ffn_Wg"]


def build(nc, a, out):
    x1 = nc.dram_tensor("x1_scratch", (NG, P, NT, D), F32, kind="Internal").ap()
    first_attention(nc, a["x"], a["ctx_2048"], a["g_xattn"],
                    *(a["L0_xattn_" + n] for n in ("q_w", "q_b", "ki_w", "ki_b", "vi_w", "vi_b", "o_w", "o_b",
                                                   "nq_s", "nki_s")), x1)
    remaining_layers(nc, x1, a["ctx_2048"], a["g_xattn"], a["g_ffn"],
                     *(a["L0_ffn_" + n] for n in ("W", "b", "lora_A", "lora_B", "gate_w", "gate_b")),
                     *(a["L1_ffn_" + n] for n in ("A", "Bw", "Wg")), out)


def kernel(**inputs):
    import numpy as _np
    import concourse.bacc as _bacc
    from concourse import mybir as _mybir
    from concourse.bass_utils import run_bass_kernel_spmd as _run

    nc = _bacc.Bacc("TRN2", target_bir_lowering=False, num_devices=1)
    arrays, args = {}, {}
    for name in _INS:
        a = _np.ascontiguousarray(inputs[name])
        arrays[f"in_{name}_dram"] = a
        args[name] = nc.dram_tensor(f"in_{name}_dram", a.shape, _mybir.dt.from_np(a.dtype), kind="ExternalInput").ap()
    out = nc.dram_tensor("out_dram", (BATCH, SEQ, D), F32, kind="ExternalOutput").ap()
    build(nc, args, out)
    return _run(nc, [arrays], core_ids=[0]).results[0]["out_dram"]
```

```python
from contextlib import ExitStack

import concourse.bass as bass
from concourse import mybir

F32 = mybir.dt.float32
F32R = mybir.dt.float32r
I32 = mybir.dt.int32
ALU = mybir.AluOpType
ACT = mybir.ActivationFunctionType
AXX = mybir.AxisListType.X

P = 128
BATCH, SEQ, D = 64, 64, 256
H, HD = 16, 128
INNER = H * HD
DC = D // P
NT = 4
GT = NT * P
NG = BATCH * SEQ // GT
E0, R0 = 8, 16
E1, R1 = 8, 64
K0 = 2
LN_EPS, RMS_EPS = 1e-5, 1e-6
LORA_SCALING, EXPERT_SCALING = 16.0 / 16.0, 64.0 / 16.0
RSQRT_SEED = 0x5F3759DF
BIG = 1e30


class Signal:

    def __init__(self, sem, per):
        self.sem, self.per = sem, per

    def wait(self, eng, g, i):
        value = g * self.per + (i + 1)
        if isinstance(g, int) and value <= 0:
            return
        eng.wait_ge(self.sem, value)


class Chain:

    def __init__(self, eng, sem):
        self.eng, self.sem, self.base, self.n = eng, sem, 0, 0

    def start(self, base):
        self.base, self.n = base, 0

    def mark(self, ins):
        self.n += 1
        ins.then_inc(self.sem, 1)

    def wait(self):
        self.eng.wait_ge(self.sem, self.base + self.n)

    def link(self, ins):
        self.mark(ins)
        self.wait()


def rsqrt_guess(dve, chain, y, t, v):
    chain.link(dve.tensor_scalar(t.bitcast(I32), v.bitcast(I32), 1, None, ALU.logical_shift_right))
    chain.link(dve.tensor_scalar(y.bitcast(I32), t.bitcast(I32), -1.0, float(RSQRT_SEED), ALU.mult, ALU.add))


def rsqrt_newton(dve, chain, y, t, v, steps):
    for _ in range(steps):
        chain.link(dve.tensor_tensor(t, y, y, ALU.mult))
        chain.link(dve.scalar_tensor_tensor(out=t, in0=t, scalar=-0.5, in1=v, op0=ALU.mult, op1=ALU.mult))
        chain.link(dve.scalar_tensor_tensor(out=y, in0=t, scalar=1.5, in1=y, op0=ALU.add, op1=ALU.mult))


def rsqrt(dve, chain, y, t, v):
    rsqrt_guess(dve, chain, y, t, v)
    rsqrt_newton(dve, chain, y, t, v, 3)


def moments(dve, chain, mean, var_eps, t, stats):
    chain.mark(dve.tensor_tensor(mean, stats[:, :, 1], stats[:, :, 4], ALU.add))
    chain.mark(dve.tensor_tensor(t, stats[:, :, 1], stats[:, :, 4], ALU.subtract))
    chain.link(dve.tensor_tensor(var_eps, stats[:, :, 2], stats[:, :, 5], ALU.add))
    chain.mark(dve.tensor_scalar(mean, mean, 0.5, None, ALU.mult))
    chain.link(dve.tensor_tensor(t, t, t, ALU.mult))
    chain.link(dve.scalar_tensor_tensor(out=t, in0=t, scalar=0.25 * D, in1=var_eps, op0=ALU.mult, op1=ALU.add))
    chain.link(dve.tensor_scalar(var_eps, t, 1.0 / D, LN_EPS, ALU.mult, ALU.add))


def identity(pool, sem, ident):
    pool.memset(ident, 0.0).then_inc(sem, 1)
    pool.wait_ge(sem, 1)
    pool.affine_select(out=ident, in_=ident, compare_op=ALU.not_equal, fill=1.0, base=0,
                       pattern=[[-1, P]], channel_multiplier=1).then_inc(sem, 1)


IDENT_READY = 2


def first_attention(nc, x, ctx, g_xattn, q_w, q_b, ki_w, ki_b, vi_w, vi_b, o_w, o_b, nq_s, nki_s, x1_dram):
    CHAIN_PER = 100
    PREP_USES = 2 + 2 * 10
    PREP_BANKS = 6
    RAW_SLOTS = 3
    BSQ_READY = 2
    ATT_LAG, OUT_LAG = 3, 4
    LN_STEP, TR_STEP, GRAM_STEP = 6, 8, 9
    x_t = x.rearrange("b s d -> (b s) d").rearrange("(g t p) d -> g p t d", g=NG, p=P)
    c_t = ctx.rearrange("b s d -> (b s) d").rearrange("(g t p) d -> g p t d", g=NG, p=P)
    with ExitStack() as stack:
        def sb(name, shape, dt=F32):
            return stack.enter_context(nc.sbuf_tensor(name, shape, dt))

        def sem(name):
            return stack.enter_context(nc.semaphore(name))

        def signal(name, per):
            return Signal(sem(name), per)

        w_hi = {n: sb(f"{n}_hi", [P, DC, INNER], F32R) for n in "qkv"}
        w_lo = {n: sb(f"{n}_lo", [P, DC, INNER], F32R) for n in "qkv"}
        wo_hi = sb("wo_hi", [P, H, D], F32R)
        wo_lo = sb("wo_lo", [P, H, D], F32R)
        gram = sb("gram", [P, 2, DC, D + 1])
        bsq = sb("bsq", [P, 2, H])
        beta = sb("beta", [P, 2])
        ident = sb("ident", [P, P])
        ones = sb("ones", [P, P])
        vecs = sb("vecs", [P, 5 * H])
        qscale = sb("qscale", [P, H])
        qbias = sb("qbias", [P, H])
        tg = sb("tg", [P, 2])
        obias = sb("obias", [P, D])
        xin = sb("xin", [P, NT, D])
        cin = sb("cin", [P, NT, D])
        stats = sb("stats", [P, NT, 6])
        mean = sb("mean", [P, NT])
        var_eps = sb("var_eps", [P, NT])
        rstd = sb("rstd", [P, NT])
        shift = sb("shift", [P, NT])
        nt_t = sb("nt_t", [P, NT])
        sums = sb("sums", [P, 2 * NT])
        sums_b = sb("sums_b", [P, 2 * NT])
        rqk = sb("rqk", [P, 2 * NT])
        nqk_t = sb("nqk_t", [P, 2 * NT])
        gram_j = sb("gram_j", [P, 2, D])
        xs = sb("xs", [P, DC, GT])
        cs = sb("cs", [P, DC, GT])
        rmax = sb("rmax", [P, NT])
        rsum = sb("rsum", [P, NT])
        rinv = sb("rinv", [P, NT])

        prep = ExitStack()
        raw = [prep.enter_context(nc.sbuf_tensor(f"raw{i}", [P, INNER], F32)) for i in range(RAW_SLOTS)]
        wt = prep.enter_context(nc.sbuf_tensor("wt", [P, H, D + 1], F32))
        vrow = prep.enter_context(nc.sbuf_tensor("vrow", [5 * H, HD], F32))
        prep.close()
        xt_hi = sb("xt_hi", [P, DC, GT], F32R)
        xt_lo = sb("xt_lo", [P, DC, GT], F32R)
        ct_hi = sb("ct_hi", [P, DC, GT], F32R)
        ct_lo = sb("ct_lo", [P, DC, GT], F32R)
        q_sb = sb("q_sb", [P, GT])
        k_sb = sb("k_sb", [P, 2, GT])
        v_sb = sb("v_sb", [P, 2, NT, 2 * HD])
        logit = sb("logit", [P, NT, SEQ])
        expo = sb("expo", [P, NT, SEQ])
        prob = sb("prob", [P, NT, SEQ])
        rr = sb("rr", [P, NT, SEQ])
        pt = sb("pt", [P, NT, P])
        ao_hi = sb("ao_hi", [P, GT], F32R)
        ao_lo = sb("ao_lo", [P, GT], F32R)
        diag = sb("diag", [P, NT, P])
        xres = sb("xres", [P, NT, D])

        banks = [stack.enter_context(nc.psum_tensor(f"bank{i}", [P, 512], F32)) for i in range(8)]
        o_ps, pj_ps, at_ps, pv_ps, tr_ps, gr_ps = banks[0:2], banks[2:4], banks[4], banks[5], banks[6], banks[7]

        s_ident = sem("s_ident")
        s_ones = sem("s_ones")
        s_vec = sem("s_vec")
        s_gate = sem("s_gate")
        s_obias = sem("s_obias")
        s_tanh = sem("s_tanh")
        s_raw = [sem(f"s_raw{i}") for i in range(RAW_SLOTS)]
        s_whi = sem("s_whi")
        s_wlo = sem("s_wlo")
        s_prep = sem("s_prep")
        s_prepev = sem("s_prepev")
        s_ptzero = sem("s_ptzero")
        s_chain = sem("s_chain")
        xin_in = signal("xin_in", 16)
        cin_in = signal("cin_in", 16)
        xres_in = signal("xres_in", 16)
        x1_out = signal("x1_out", 16)
        xres_ready = signal("xres_ready", 1)
        scales_ready = signal("scales_ready", 1)
        xn_ready = signal("xn_ready", 1)
        tr_full = signal("tr_full", NT)
        tr_read = signal("tr_read", NT)
        gr_full = signal("gr_full", NT)
        gr_read = signal("gr_read", NT)
        diag_ready = signal("diag_ready", 1)
        rk_full = signal("rk_full", 1)
        rr_ready = signal("rr_ready", 1)
        split_hi = signal("split_hi", 2)
        split_lo = signal("split_lo", 2)
        pj_full = signal("pj_full", 3 * H)
        pj_read = signal("pj_read", 3 * H)
        qk_full = signal("qk_full", H)
        l_ready = signal("l_ready", H)
        e_ready = signal("e_ready", H)
        p_ready = signal("p_ready", H)
        pt_full = signal("pt_full", H)
        pt_ready = signal("pt_ready", H)
        pv_full = signal("pv_full", H)
        ao_hi_ready = signal("ao_hi_ready", H)
        ao_ready = signal("ao_ready", H)
        o_full = signal("o_full", H)
        x1_ready = signal("x1_ready", 2)

        NAMES = [("q", 0), ("q", 1), ("k", 0), ("k", 1), ("v", 0), ("v", 1), ("o", 0), ("o", 1)]

        def tr_use(n, c, f):
            return 2 + 10 * n + 4 * c + f

        def raw_in(eng, i):
            eng.wait_ge(s_raw[i % RAW_SLOTS], 16 * (i // RAW_SLOTS + 1))

        def weight_parts(i):
            n, c = NAMES[i]
            if n == "o":
                half = slice(c * H // 2, (c + 1) * H // 2)
                return (wo_hi[:, half, :].rearrange("p h d -> p (h d)"),
                        wo_lo[:, half, :].rearrange("p h d -> p (h d)"))
            return w_hi[n][:, c, :], w_lo[n][:, c, :]

        def live(h, first):
            return h < H and (h >= 0 or not first)

        block = stack.enter_context(nc.Block())

        @block.sync
        def _(sp):
            src = {"q": q_w, "k": ki_w, "v": vi_w}

            def view(t, g):
                return t[g] if isinstance(g, int) else t[bass.ds(g, 1)].rearrange("g p t d -> p (g t) d")

            def load_inputs(g):
                gr_read.wait(sp, g, -1)
                sp.dma_start(xin[:, :, :], view(x_t, g)).then_inc(xin_in.sem, 16)
                sp.dma_start(cin[:, :, :], view(c_t, g)).then_inc(cin_in.sem, 16)

            def store(g):
                x1_ready.wait(sp, g, 1)
                sp.dma_start(view(x1_dram, g), xres[:, :, :]).then_inc(x1_out.sem, 16)

            for j, v in enumerate((q_b, nq_s, nki_s, ki_b, vi_b)):
                sp.dma_start(vrow[j * H:(j + 1) * H, :], v.rearrange("(h d) -> h d", h=H)).then_inc(s_vec, 16)
            for i, (n, c) in enumerate(NAMES):
                slot = i % RAW_SLOTS
                if i >= RAW_SLOTS:
                    before = i - RAW_SLOTS
                    sp.wait_ge(s_wlo, before + 1)
                    if before < 4:
                        sp.wait_ge(s_prep, 1 + tr_use(before // 2, before % 2, 3))
                if n == "o":
                    half = o_w.rearrange("(h p) d -> p h d", h=H)[:, c * H // 2:(c + 1) * H // 2, :]
                    sp.dma_start(raw[slot][:, :].rearrange("p (h d) -> p h d", d=D), half).then_inc(s_raw[slot], 16)
                else:
                    sp.dma_start(raw[slot][:, :], src[n][c * P:(c + 1) * P, :]).then_inc(s_raw[slot], 16)
                if i == 1:
                    load_inputs(0)

            def group(g, last):
                if not last:
                    load_inputs(g + 1)
                if isinstance(g, int) and g == 0:
                    sp.wait_ge(s_prepev, PREP_USES)
                    sp.wait_ge(s_wlo, 8)
                else:
                    store(g - 1)
                    x1_out.wait(sp, g - 1, 15)
                sp.dma_start(xres[:, :, :], view(x_t, g)).then_inc(xres_in.sem, 16)

            group(0, False)
            with sp.Fori(1, NG - 1) as g:
                group(g, False)
            group(NG - 1, True)
            store(NG - 1)
            x1_out.wait(sp, NG - 1, 15)

        @block.gpsimd
        def _(pool):
            identity(pool, s_ident, ident[:, :])
            pool.memset(ones[:, :], 1.0).then_inc(s_ones, 1)
            pool.dma_start(tg[:, :], g_xattn.partition_broadcast(P)).then_inc(s_gate, 16)
            pool.dma_start(obias[:, :], o_b.partition_broadcast(P)).then_inc(s_gate, 16)
            pool.wait_ge(s_prepev, PREP_USES)
            pool.wait_ge(s_wlo, 8)
            pool.memset(pt[:, :, :], 0.0).then_inc(s_ptzero, 1)
            pool.wait_ge(s_obias, 1)

            def group(g):
                xres_in.wait(pool, g, 15)
                pool.tensor_tensor(xres[:, :, :], xres[:, :, :],
                                   obias[:, :].unsqueeze(1).to_broadcast([P, NT, D]),
                                   ALU.add).then_inc(xres_ready.sem, 1)

            group(0)
            with pool.Fori(1, NG) as g:
                group(g)

        @block.scalar
        def _(act):
            act.wait_ge(s_gate, 32)
            act.activation(tg[:, :], tg[:, :], ACT.Tanh).then_inc(s_tanh, 1)

            def high_part(i):
                raw_in(act, i)
                act.activation(weight_parts(i)[0], raw[i % RAW_SLOTS][:, :], ACT.Copy).then_inc(s_whi, 1)

            def normalise(g):
                scales_ready.wait(act, g, 0)
                for t in range(NT):
                    last = act.activation(xin[:, t, :], xin[:, t, :], ACT.Identity, scale=rstd[:, t:t + 1],
                                          bias=shift[:, t:t + 1])
                last.then_inc(xn_ready.sem, 1)

            def transposed(g, t):
                tr_full.wait(act, g, t)
                act.activation(xs[:, :, t * P:(t + 1) * P],
                               tr_ps[:, 0:D].rearrange("p (c n) -> p c n", c=DC), ACT.Copy)
                act.activation(cs[:, :, t * P:(t + 1) * P],
                               tr_ps[:, D:2 * D].rearrange("p (c n) -> p c n", c=DC), ACT.Copy).then_inc(tr_read.sem, 1)

            def split(g):
                tr_read.wait(act, g, NT - 1)
                if isinstance(g, int) and g == 0:
                    act.wait_ge(s_wlo, 8)
                    act.wait_ge(s_prepev, PREP_USES)
                pj_full.wait(act, g, -1)
                act.activation(ct_hi[:, :, :], cs[:, :, :], ACT.Copy).then_inc(split_hi.sem, 1)
                act.activation(xt_hi[:, :, :], xs[:, :, :], ACT.Copy).then_inc(split_hi.sem, 1)

            def attn_hi(g, h):
                pv_full.wait(act, g, h)
                act.activation(ao_hi[:, :], pv_ps[:, :], ACT.Identity,
                               bias=vecs[:, 4 * H + h % H:4 * H + h % H + 1]).then_inc(ao_hi_ready.sem, 1)

            def exps(g, h):
                l_ready.wait(act, g, h)
                act.activation(expo[:, :, :], logit[:, :, :], ACT.Exp).then_inc(e_ready.sem, 1)

            def project(g, h, j):
                pj_full.wait(act, g, 3 * h + j)
                bank = pj_ps[(3 * h + j) % 2]
                if j == 0:
                    act.activation(k_sb[:, h % 2, :], bank[:, :], ACT.Identity,
                                   bias=vecs[:, 3 * H + h:3 * H + h + 1]).then_inc(pj_read.sem, 1)
                elif j == 1:
                    t = 2 * (h % 2)
                    act.activation(v_sb[:, (h // 2) % 2, t:t + 2, :],
                                   bank[:, :].rearrange("p (t n) -> p t n", t=2), ACT.Copy).then_inc(pj_read.sem, 1)
                else:
                    act.activation(q_sb[:, :], bank[:, :], ACT.Identity, scale=qscale[:, h:h + 1],
                                   bias=qbias[:, h:h + 1]).then_inc(pj_read.sem, 1)

            def step(g, h, first, last):
                if 0 < h < H:
                    project(g, h, 0)
                if live(h - ATT_LAG, first):
                    attn_hi(g, h - ATT_LAG)
                if h == 0:
                    project(g, h, 0)
                if h < H:
                    project(g, h, 1)
                if live(h - 1, first):
                    exps(g, h - 1)
                if h < H:
                    project(g, h, 2)
                if not last and h == LN_STEP + 1:
                    normalise(g + 1)
                if not last and TR_STEP <= h < TR_STEP + NT:
                    transposed(g + 1, h - TR_STEP)

            high_part(0)
            high_part(1)
            normalise(0)
            high_part(2)
            high_part(3)
            for t in range(NT):
                transposed(0, t)
            for i in range(4, len(NAMES)):
                high_part(i)
            split(0)
            for h in range(H):
                step(0, h, True, False)
            split(1)
            with act.Fori(1, NG - 1) as g:
                for h in range(H):
                    step(g, h, False, False)
                split(g + 1)
            for h in range(H + ATT_LAG):
                step(NG - 1, h, False, True)

        @block.tensor
        def _(pe):
            def three(out, lhs, rhs, start, stop, **kw):
                pairs = [(0, 0), (0, 1), (1, 0)]
                for n, (a, b) in enumerate(pairs):
                    last = pe.matmul(out, lhs[a], rhs[b], start=start and n == 0, stop=stop and n == 2, **kw)
                return last

            use = [0]

            def bank():
                if use[0] >= PREP_BANKS:
                    pe.wait_ge(s_prepev, use[0] - PREP_BANKS + 1)
                use[0] += 1
                return banks[(use[0] - 1) % PREP_BANKS]

            def turn_weight(n):
                for c in range(DC):
                    i = 2 * n + c
                    raw_in(pe, i)
                    for f in range(4):
                        assert use[0] == tr_use(n, c, f)
                        b = bank()
                        for j in range(4):
                            h = 4 * f + j
                            last = pe.transpose(b[:, j * P:(j + 1) * P], raw[i % RAW_SLOTS][:, h * P:(h + 1) * P],
                                                ident[:, :])
                        last.then_inc(s_prep, 1)

            def gram_matrix(n):
                pe.wait_ge(s_prepev, tr_use(n, DC - 1, 3) + 1)
                for c in range(DC):
                    b = bank()
                    for h in range(H):
                        last = pe.matmul(b[:, c * P:D + 1], wt[:, h, c * P:(c + 1) * P], wt[:, h, c * P:D + 1],
                                         start=h == 0, stop=h == H - 1)
                    last.then_inc(s_prep, 1)

            def transposes(g, t):
                tr_read.wait(pe, g, t - 1)
                if t > 0 and not (isinstance(g, int) and g == 0):
                    gr_read.wait(pe, g, t - 1)
                if t == 0:
                    xn_ready.wait(pe, g, 0)
                    cin_in.wait(pe, g, 15)
                    rr_ready.wait(pe, g, -1)
                for s, src in enumerate((xin, cin)):
                    for c in range(DC):
                        last = pe.transpose(tr_ps[:, (2 * s + c) * P:(2 * s + c + 1) * P],
                                            src[:, t, c * P:(c + 1) * P], ident[:, :])
                last.then_inc(tr_full.sem, 1)

            def gram_products(g, t, transposed):
                tr_read.wait(pe, g, transposed)
                gr_read.wait(pe, g, t - 1)
                for n, (b, src) in enumerate(((gr_ps, xs), (tr_ps, cs))):
                    for c in range(DC):
                        last = pe.matmul(b[:, c * P:D + 1], src[:, c, t * P:(t + 1) * P],
                                         gram[:, n, c, c * P:D + 1], start=c == 0, stop=c == DC - 1)
                last.then_inc(gr_full.sem, 1)

            def norms(g):
                diag_ready.wait(pe, g, 0)
                pe.matmul(tr_ps[:, :], ones[:, :], diag[:, :, :].rearrange("p t n -> p (t n)"),
                          start=True, stop=True).then_inc(rk_full.sem, 1)

            def prob_transpose(g, h):
                p_ready.wait(pe, g, h)
                l_ready.wait(pe, g, min(h + 1, H - 1))
                for q in range(2):
                    last = pe.transpose(at_ps[:, q * P:(q + 1) * P],
                                        prob[:, 2 * q:2 * q + 2, :].rearrange("p t l -> p (t l)"), ident[:, :])
                last.then_inc(pt_full.sem, 1)

            def attend(g, h):
                pt_ready.wait(pe, g, h)
                pj_read.wait(pe, g, 3 * (h + 1 - h % 2) + 1)
                ao_ready.wait(pe, g, h - 1)
                for t in range(NT):
                    last = pe.matmul(pv_ps[:, t * P:(t + 1) * P],
                                     v_sb[:, (h // 2) % 2, t, (h % 2) * HD:(h % 2 + 1) * HD],
                                     pt[:, t, :], start=True, stop=True)
                last.then_inc(pv_full.sem, 1)

            def scores(g, h):
                pj_read.wait(pe, g, 3 * h + 2)
                pt_ready.wait(pe, g, h + 1 - ATT_LAG)
                for t in range(NT):
                    for b in range(2):
                        s = slice(t * P + b * SEQ, t * P + (b + 1) * SEQ)
                        last = pe.matmul(at_ps[b * SEQ:(b + 1) * SEQ, t * SEQ:(t + 1) * SEQ],
                                         q_sb[:, s], k_sb[:, h % 2, s], start=True, stop=True)
                last.then_inc(qk_full.sem, 1)

            def output(g, h):
                ao_ready.wait(pe, g, h)
                for t in range(NT):
                    if h % H == 0 and t % 2 == 0:
                        x1_ready.wait(pe, g + h // H - 1, t // 2)
                    s = slice(t * P, (t + 1) * P)
                    last = three(o_ps[t // 2][:, (t % 2) * D:(t % 2 + 1) * D], (ao_hi[:, s], ao_lo[:, s]),
                                 (wo_hi[:, h % H, :], wo_lo[:, h % H, :]),
                                 start=h % H == 0 and t % 2 == 0, stop=h % H == H - 1, skip_group_check=True)
                last.then_inc(o_full.sem, 1)

            def bank_for(g, u):
                pj_read.wait(pe, g, u - 2)
                return pj_ps[u % 2]

            def values(g, h):
                b = bank_for(g, 3 * h + 1)
                pair = slice((h - h % 2) * HD, (h - h % 2 + 2) * HD)
                for i in range(2):
                    t = 2 * (h % 2) + i
                    s = slice(t * P, (t + 1) * P)
                    for c in range(DC):
                        last = three(b[:, i * 2 * HD:(i + 1) * 2 * HD], (ct_hi[:, c, s], ct_lo[:, c, s]),
                                     (w_hi["v"][:, c, pair], w_lo["v"][:, c, pair]), start=c == 0, stop=c == DC - 1)
                last.then_inc(pj_full.sem, 1)

            def project(g, h, j):
                b = bank_for(g, 3 * h + j)
                n, hi, lo = ("k", ct_hi, ct_lo) if j == 0 else ("q", xt_hi, xt_lo)
                if h == 0:
                    split_lo.wait(pe, g, j // 2)
                cols = slice(h * HD, (h + 1) * HD)
                for c in range(DC):
                    last = three(b[:, :], (w_hi[n][:, c, cols], w_lo[n][:, c, cols]), (hi[:, c, :], lo[:, c, :]),
                                 start=c == 0, stop=c == DC - 1)
                last.then_inc(pj_full.sem, 1)

            def step(g, h, first, last):
                if live(h - ATT_LAG, first):
                    prob_transpose(g, h - ATT_LAG)
                if live(h - OUT_LAG, first):
                    output(g, h - OUT_LAG)
                if 0 < h < H:
                    project(g, h, 0)
                if live(h - ATT_LAG, first):
                    attend(g, h - ATT_LAG)
                if live(h - 1, first):
                    scores(g, h - 1)
                if h == 0:
                    project(g, h, 0)
                if not last and GRAM_STEP <= h < GRAM_STEP + NT:
                    gram_products(g + 1, h - GRAM_STEP, h - GRAM_STEP)
                if h < H:
                    values(g, h)
                    project(g, h, 2)
                if not last:
                    if TR_STEP <= h < TR_STEP + NT:
                        transposes(g + 1, h - TR_STEP)
                    if h == H - 1:
                        norms(g + 1)

            pe.wait_ge(s_ident, IDENT_READY)
            pe.wait_ge(s_vec, 80)
            pe.transpose(bank()[:, 0:5 * H], vrow[:, :], ident[0:5 * H, 0:5 * H]).then_inc(s_prep, 1)
            pe.wait_ge(s_ones, 1)
            pe.wait_ge(s_chain, BSQ_READY)
            pe.matmul(bank()[:, 0:2 * H], ones[:, :], bsq[:, :, :].rearrange("p n h -> p (n h)"),
                      start=True, stop=True).then_inc(s_prep, 1)
            turn_weight(0)
            gram_matrix(0)
            turn_weight(1)
            for t in range(NT):
                transposes(0, t)
            gram_matrix(1)
            pe.wait_ge(s_prepev, PREP_USES)
            for t in range(NT):
                gram_products(0, t, NT - 1)
            pe.wait_ge(s_wlo, len(NAMES))
            for h in range(H):
                if h == ATT_LAG:
                    pe.wait_ge(s_ptzero, 1)
                step(0, h, True, False)
                if h == 0:
                    norms(0)
            with pe.Fori(1, NG - 1) as g:
                for h in range(H):
                    step(g, h, False, False)
            for h in range(H + OUT_LAG):
                step(NG - 1, h, False, True)

        @block.vector
        def _(dve):
            chain = Chain(dve, s_chain)
            use = [0]

            def prepared():
                use[0] += 1
                dve.wait_ge(s_prep, use[0])
                return banks[(use[0] - 1) % PREP_BANKS]

            def low_part(i):
                hi, lo = weight_parts(i)
                dve.wait_ge(s_whi, i + 1)
                dve.tensor_tensor(lo, raw[i % RAW_SLOTS][:, :], hi.bitcast(F32), ALU.subtract).then_inc(s_wlo, 1)

            def weight_copies(n):
                v = (0, 3)[n] * H
                dve.tensor_copy(wt[:, :, D:D + 1], vecs[:, v:v + H].unsqueeze(2))
                for c in range(DC):
                    for f in range(4):
                        dve.tensor_copy(wt[:, 4 * f:4 * f + 4, c * P:(c + 1) * P],
                                        prepared()[:, :].rearrange("p (h n) -> p h n", h=4)).then_inc(s_prepev, 1)

            def gram_copies(n):
                b = prepared()
                dve.tensor_copy(gram[:, n, 0, 0:P], b[:, 0:P])
                dve.tensor_scalar(gram[:, n, 0, P:D + 1], b[:, P:D + 1], 2.0, None, ALU.mult).then_inc(s_prepev, 1)
                b = prepared()
                dve.tensor_copy(gram[:, n, 1, P:D], b[:, P:D])
                dve.tensor_scalar(gram[:, n, 1, D:D + 1], b[:, D:D + 1], 2.0, None, ALU.mult).then_inc(s_prepev, 1)

            def tile_stats(g, t):
                if t == 0:
                    xin_in.wait(dve, g, 15)
                chain.mark(dve.bn_stats(stats[:, t, :], xin[:, t, :]))

            def tile_variances(g):
                chain.wait()
                moments(dve, chain, mean[:, :], var_eps[:, :], nt_t[:, :], stats)
                rsqrt_guess(dve, chain, rstd[:, :], nt_t[:, :], var_eps[:, :])

            def tile_scales(g):
                rsqrt_newton(dve, chain, rstd[:, :], nt_t[:, :], var_eps[:, :], 3)
                dve.scalar_tensor_tensor(out=shift[:, :], in0=mean[:, :], scalar=-1.0, in1=rstd[:, :],
                                         op0=ALU.mult, op1=ALU.mult).then_inc(scales_ready.sem, 1)

            def gram_sums(g, t):
                gr_full.wait(dve, g, t)
                for n, (b, src) in enumerate(((gr_ps, xin), (tr_ps, cin))):
                    last = dve.tensor_tensor_reduce(gram_j[:, n, :], b[:, 0:D], src[:, t, :], 1.0, b[:, D:D + 1], ALU.mult,
                                                    ALU.add, sums[:, n * NT + t:n * NT + t + 1])
                last.then_inc(gr_read.sem, 1)

            def square_norms(g):
                gr_read.wait(dve, g, NT - 1)
                for n in range(2):
                    half = slice(n * NT, (n + 1) * NT)
                    chain.mark(dve.tensor_scalar(sums_b[:, half], sums[:, half], beta[:, n:n + 1],
                                                 1.0 / INNER, ALU.add, ALU.mult))
                chain.wait()
                chain.link(dve.tensor_scalar(sums_b[:, :], sums_b[:, :], RMS_EPS, None, ALU.add))
                rsqrt_guess(dve, chain, rqk[:, :], nqk_t[:, :], sums_b[:, :])
                rsqrt_newton(dve, chain, rqk[:, :], nqk_t[:, :], sums_b[:, :], 1)

            def norm_factors(g):
                rsqrt_newton(dve, chain, rqk[:, :], nqk_t[:, :], sums_b[:, :], 2)
                for t in range(NT):
                    last = dve.tensor_scalar(diag[:, t, :], ident[:, :], rqk[:, NT + t:NT + t + 1], None, ALU.mult)
                last.then_inc(diag_ready.sem, 1)

            def score_factors(g):
                rk_full.wait(dve, g, 0)
                for t in range(NT):
                    for b in range(2):
                        rows = slice(b * SEQ, (b + 1) * SEQ)
                        last = dve.tensor_scalar(rr[rows, t, :], tr_ps[rows, t * P + b * SEQ:t * P + (b + 1) * SEQ],
                                                 rqk[rows, t:t + 1], float(HD) ** -0.5, ALU.mult, ALU.mult)
                last.then_inc(rr_ready.sem, 1)

            def split(g):
                for n, (lo, hi, src) in enumerate(((ct_lo, ct_hi, cs), (xt_lo, xt_hi, xs))):
                    split_hi.wait(dve, g, n)
                    dve.tensor_tensor(lo[:, :, :], src[:, :, :], hi[:, :, :].bitcast(F32),
                                      ALU.subtract).then_inc(split_lo.sem, 1)

            def prob_copy(g, h):
                pt_full.wait(dve, g, h)
                for q in range(2):
                    for b in range(2):
                        src = at_ps[q * SEQ:(q + 1) * SEQ, 0:2 * P].rearrange("p (t s) -> p t s", t=2)
                        last = dve.tensor_copy(pt[b * SEQ:(b + 1) * SEQ, q::2, b * SEQ:(b + 1) * SEQ],
                                               src[:, :, b * SEQ:(b + 1) * SEQ])
                last.then_inc(pt_ready.sem, 1)

            def attn_lo(g, h):
                v = 4 * H + h % H
                ao_hi_ready.wait(dve, g, h)
                dve.scalar_tensor_tensor(out=ao_lo[:, :], in0=pv_ps[:, :], scalar=vecs[:, v:v + 1],
                                         in1=ao_hi[:, :].bitcast(F32), op0=ALU.add,
                                         op1=ALU.subtract).then_inc(ao_ready.sem, 1)

            def logits(g, h):
                qk_full.wait(dve, g, h)
                if h == 0:
                    rr_ready.wait(dve, g, 0)
                chain.link(dve.tensor_tensor(logit[:, :, :], at_ps[:, 0:NT * SEQ].rearrange("p (t l) -> p t l", t=NT),
                                             rr[:, :, :], ALU.mult))
                chain.link(dve.tensor_reduce(rmax[:, :], logit[:, :, :], AXX, ALU.max))
                dve.tensor_tensor(logit[:, :, :], logit[:, :, :],
                                  rmax[:, :].unsqueeze(2).to_broadcast([P, NT, SEQ]),
                                  ALU.subtract).then_inc(l_ready.sem, 1)

            def probabilities(g, h):
                e_ready.wait(dve, g, h)
                chain.link(dve.tensor_reduce(rsum[:, :], expo[:, :, :], AXX, ALU.add))
                chain.link(dve.reciprocal(rinv[:, :], rsum[:, :]))
                dve.tensor_tensor(prob[:, :, :], expo[:, :, :], rinv[:, :].unsqueeze(2).to_broadcast([P, NT, SEQ]),
                                  ALU.mult).then_inc(p_ready.sem, 1)

            def residual(g, i):
                if i == 0:
                    o_full.wait(dve, g, H - 1)
                    xres_ready.wait(dve, g, 0)
                rows = xres[:, 2 * i:2 * i + 2, :].rearrange("p t d -> p (t d)")
                dve.scalar_tensor_tensor(out=rows, in0=o_ps[i][:, :], scalar=tg[:, 0:1], in1=rows,
                                         op0=ALU.mult, op1=ALU.add).then_inc(x1_ready.sem, 1)

            def step(g, h, first, last):
                if live(h - ATT_LAG, first):
                    prob_copy(g, h - ATT_LAG)
                if h == 0 and not first:
                    split(g)
                if live(h - 2, first):
                    probabilities(g, h - 2)
                if live(h - ATT_LAG, first):
                    attn_lo(g, h - ATT_LAG)
                if h == OUT_LAG - 1 and not first:
                    residual(g - 1, 0)
                if live(h - 1, first):
                    logits(g, h - 1)
                if h == 0:
                    score_factors(g)
                if h == OUT_LAG - 1 and not first:
                    residual(g - 1, 1)
                if not last:
                    if LN_STEP - NT <= h < LN_STEP:
                        tile_stats(g + 1, h - LN_STEP + NT)
                    if h == LN_STEP:
                        tile_variances(g + 1)
                    if h == LN_STEP + 1:
                        tile_scales(g + 1)
                    if GRAM_STEP <= h < GRAM_STEP + NT:
                        gram_sums(g + 1, h - GRAM_STEP)
                    if h == GRAM_STEP + NT:
                        square_norms(g + 1)
                    if h == GRAM_STEP + NT + 1:
                        norm_factors(g + 1)

            dve.tensor_copy(vecs[:, :], prepared()[:, 0:5 * H]).then_inc(s_prepev, 1)
            dve.wait_ge(s_prepev, 1)
            chain.mark(dve.tensor_tensor(bsq[:, 0, :], vecs[:, 0:H], vecs[:, 0:H], ALU.mult))
            chain.mark(dve.tensor_tensor(bsq[:, 1, :], vecs[:, 3 * H:4 * H], vecs[:, 3 * H:4 * H], ALU.mult))
            assert chain.n == BSQ_READY
            chain.link(dve.tensor_tensor(qscale[:, :], vecs[:, H:2 * H], vecs[:, 2 * H:3 * H], ALU.mult))
            chain.mark(dve.tensor_tensor(qbias[:, :], vecs[:, 0:H], qscale[:, :], ALU.mult))
            dve.tensor_reduce(beta[:, :], prepared()[:, 0:2 * H].rearrange("p (n h) -> p n h", n=2), AXX,
                              ALU.add).then_inc(s_prepev, 1)
            weight_copies(0)
            low_part(0)
            low_part(1)
            for t in range(NT):
                tile_stats(0, t)
            tile_variances(0)
            tile_scales(0)
            gram_copies(0)
            weight_copies(1)
            for i in range(2, 6):
                low_part(i)
            gram_copies(1)
            dve.wait_ge(s_prepev, PREP_USES)
            dve.wait_ge(s_tanh, 1)
            dve.tensor_scalar(obias[:, :], obias[:, :], tg[:, 0:1], None, ALU.mult).then_inc(s_obias, 1)
            low_part(6)
            for t in range(NT):
                gram_sums(0, t)
            square_norms(0)
            norm_factors(0)
            low_part(7)
            split(0)
            for h in range(H):
                if h == ATT_LAG:
                    dve.wait_ge(s_ptzero, 1)
                step(0, h, True, False)
            done = chain.n
            with dve.Fori(1, NG - 1) as g:
                chain.start(done + (g - 1) * CHAIN_PER)
                for h in range(H):
                    step(g, h, False, False)
                assert chain.n == CHAIN_PER, chain.n
            chain.start(done + (NG - 2) * CHAIN_PER)
            for h in range(H + ATT_LAG):
                step(NG - 1, h, False, True)
            for i in range(2):
                residual(NG - 1, i)


def remaining_layers(nc, x1_dram, ctx, g_xattn, g_ffn, w0, b0, lora_a, lora_b, gate_w, gate_b, a1, b1, wg1, out):
    CHAIN_PER = 92
    LAG = {"A": 0, "B": 1, "C": 2}
    c_t = ctx.rearrange("b s d -> (b s) d").rearrange("(g t p) d -> g p t d", g=NG, p=P)
    out_t = out.rearrange("b s d -> (b s) d").rearrange("(g t p) d -> g p t d", g=NG, p=P)
    C0, C1 = E0 * R0, E1 * R1
    CT1 = C1 // P
    B_NT = 2 * NT
    with ExitStack() as stack:
        def sb(name, shape, dt=F32):
            return stack.enter_context(nc.sbuf_tensor(name, shape, dt))

        def sem(name):
            return stack.enter_context(nc.semaphore(name))

        def signal(name, per):
            return Signal(sem(name), per)

        def both(name, shape):
            return sb(name + "_hi", shape, F32R), sb(name + "_lo", shape, F32R)

        w0t = both("w0t", [P, DC, D])
        a0t = both("a0t", [P, DC, C0 + E0])
        b0t = both("b0t", [P, D])
        a1t = both("a1t", [P, DC, C1])
        g1t = sb("g1t", [P, DC, E1])
        b1t = both("b1t", [P, CT1, D])
        raw_w0 = sb("raw_w0", [P, DC, D])
        raw_a0 = sb("raw_a0", [P, D])
        raw_g = sb("raw_g", [E0, 2, D])
        raw_b0 = sb("raw_b0", [P, 2, E0, R0])
        raw_a1 = sb("raw_a1", [P, CT1, D])
        raw_b1 = sb("raw_b1", [P, 2, E1, R1])
        ident = sb("ident2", [P, P])
        tg = sb("tg2", [P, 4])
        tgh = sb("tgh", [P, 1])
        bias0 = sb("bias0", [P, D])
        gbias = sb("gbias", [P, E0])
        prefer = sb("prefer", [P, NT, E0])

        stats = sb("stats2", [P, NT, 6])
        mean = sb("mean2", [P, NT])
        var_eps = sb("var_eps2", [P, NT])
        ntmp = sb("ntmp2", [P, NT])
        rstd = [sb(f"rstd2_{n}", [P, NT]) for n in range(3)]
        shift = [sb(f"shift{n}", [P, NT]) for n in range(3)]
        x1 = sb("x1", [P, NT, D])
        x1b = sb("x1b", [P, NT, D])
        xn1 = sb("xn1", [P, NT, D])
        xt1_f = sb("xt1_f", [P, DC, GT])
        xt1 = both("xt1", [P, DC, GT])
        xa = sb("xa", [P, NT, C0])
        lg0 = sb("lg0", [P, NT, E0])
        work = sb("work", [P, NT, E0])
        pick = [sb(f"pick{i}", [P, NT, E0]) for i in range(2)]
        top = sb("top", [P, 2, NT])
        best = sb("best", [P, NT])
        gexp = sb("gexp", [P, NT])
        gw = sb("gw", [P, 2, NT])
        gates = sb("gates", [P, NT, E0])
        xg = sb("xg", [P, NT, C0])
        xgt = both("xgt", [P, GT])
        x2 = sb("x2", [P, NT, D])
        xn2 = sb("xn2", [P, NT, D])
        cin = sb("cin2", [P, NT, D])
        ct = sb("ct", [P, DC, GT])
        csum = sb("csum", [P, NT])
        x2c = sb("x2c", [P, NT, D])
        th = sb("th", [P, B_NT, DC, D])
        x3 = sb("x3", [P, NT, D])
        xn3 = sb("xn3", [P, NT, D])
        xt3_f = sb("xt3_f", [P, DC, GT])
        xt3 = both("xt3", [P, DC, GT])
        lg1 = sb("lg1", [P, NT, E1])
        ex1 = sb("ex1", [P, NT, E1])
        coef = sb("coef", [P, NT, E1])
        hm = sb("hm", [P, NT, C1])
        hmt_f = sb("hmt_f", [P, NT, CT1, P])
        hmt = both("hmt", [P, NT, CT1, P])
        result = sb("result", [P, NT, D])
        banks = [stack.enter_context(nc.psum_tensor(f"ban2k{i}", [P, 512], F32)) for i in range(8)]

        s_ident = sem("s_ident2")
        s_const = sem("s_const")
        s_raw = sem("s_rawin")
        s_gate = sem("s_gate2")
        s_tanh = sem("s_tanh2")
        s_scaled = sem("s_scaled")
        s_prep = sem("s_prep2")
        s_prep_hi = sem("s_prep_hi")
        s_prep_lo = sem("s_prep_lo")
        s_chain = sem("s_chain2")
        x1_in = signal("x1_in2", 16)
        cin_in = signal("cin_in2", 16)
        out_sent = signal("out_sent", 16)
        x1b_ready = signal("x1b_ready", 1)
        scales = [signal(f"scales{n}", 1) for n in range(3)]
        xn1_ready = signal("xn1_ready", 1)
        xn2_ready = signal("xn2_ready", 1)
        xn3_ready = signal("xn3_ready", 1)
        xt1_hi_ready = signal("xt1_hi_ready", 2)
        xt1_ready = signal("xt1_ready", 2)
        xa_ready = signal("xa_ready", 2)
        lg0_ready = signal("lg0_ready", 2)
        gap_ready = signal("gap_ready", 1)
        gexp_ready = signal("gexp_ready", 1)
        xg_ready = signal("xg_ready", 1)
        xgt_hi_ready = signal("xgt_hi_ready", 1)
        xgt_ready = signal("xgt_ready", 1)
        x2_ready = signal("x2_ready", 2)
        ct_ready = signal("ct_ready", 2)
        csum_ready = signal("csum_ready", 1)
        x2c_ready = signal("x2c_ready", 1)
        th_ready = signal("th_ready", B_NT)
        x3_ready = signal("x3_ready", 2)
        xt3_hi_ready = signal("xt3_hi_ready", 2)
        xt3_ready = signal("xt3_ready", 2)
        lg1_ready = signal("lg1_ready", 1)
        lg1_read = signal("lg1_read", 1)
        ex1_ready = signal("ex1_ready", 1)
        hm_ready = signal("hm_ready", NT)
        hmt_hi_ready = signal("hmt_hi_ready", NT)
        hmt_ready = signal("hmt_ready", NT)
        y_ready = signal("y_ready", 2)

        RING = [("xt1", 2, "A", xt1_hi_ready), ("ct", 2, "B", ct_ready), ("aff", B_NT, "B", th_ready),
                ("xa", 2, "A", lg0_ready), ("xt3", 2, "C", xt3_hi_ready), ("lg", 1, "C", lg1_read),
                ("h", NT, "C", hm_ready), ("xg", 1, "A", xgt_ready), ("hm", NT, "C", hmt_hi_ready),
                ("lora", 2, "A", x2_ready), ("y", 2, "C", y_ready), ("att", 2, "B", x3_ready)]
        full = {name: signal(f"{name}_full", n) for name, n, _, _ in RING}
        USES = [(name, i, part, read) for name, n, part, read in RING for i in range(n)]
        PLACE = {(name, i): u for u, (name, i, _, _) in enumerate(USES)}
        assert len(USES) % len(banks) == 0

        def bank_of(name, i):
            return banks[PLACE[name, i] % len(banks)]

        def token_major(bank):
            return bank[:, :].rearrange("p (t c n) -> p t c n", t=2, c=DC)

        def feature_major(buf, i):
            return buf[:, :, 2 * i * P:2 * (i + 1) * P].rearrange("p c (t n) -> p t c n", t=2)

        block = stack.enter_context(nc.Block())

        @block.sync
        def _(sp):
            def at(t, g):
                return t[g] if isinstance(g, int) else t[bass.ds(g, 1)].rearrange("g p t d -> p (g t) d")

            def load_x1(g):
                xn1_ready.wait(sp, g - 1, 0)
                x1b_ready.wait(sp, g - 1, 0)
                sp.dma_start(x1[:, :, :], at(x1_dram, g)).then_inc(x1_in.sem, 16)

            def load_ctx(g):
                th_ready.wait(sp, g - 1, B_NT - 1)
                csum_ready.wait(sp, g - 1, 0)
                sp.dma_start(cin[:, :, :], at(c_t, g)).then_inc(cin_in.sem, 16)

            def store(g):
                y_ready.wait(sp, g, 1)
                sp.dma_start(at(out_t, g), result[:, :, :]).then_inc(out_sent.sem, 16)

            load_x1(0)
            sp.dma_start(raw_w0[:, :, :], w0.rearrange("(c p) d -> p c d", p=P)).then_inc(s_raw, 16)
            sp.dma_start(raw_a0[:, :], lora_a.rearrange("e r d -> (e r) d")).then_inc(s_raw, 16)
            sp.dma_start(raw_g[:, 0, :], gate_w).then_inc(s_raw, 16)
            sp.dma_start(raw_g[:, 1, :], wg1).then_inc(s_raw, 16)
            load_ctx(0)
            load_x1(1)
            load_x1(2)
            load_ctx(1)
            with sp.Fori(2, NG - 1) as i:
                load_x1(i + 1)
                load_ctx(i)
                store(i - 2)
            load_ctx(NG - 1)
            for g in range(NG - 3, NG):
                store(g)
            out_sent.wait(sp, NG - 1, 15)

        @block.gpsimd
        def _(pool):
            pool.dma_start(tg[:, 0:2], g_xattn.partition_broadcast(P)).then_inc(s_gate, 16)
            pool.dma_start(tg[:, 2:4], g_ffn.partition_broadcast(P)).then_inc(s_gate, 16)
            pool.dma_start(bias0[:, :], b0.partition_broadcast(P)).then_inc(s_gate, 16)
            pool.dma_start(gbias[:, :], gate_b.partition_broadcast(P)).then_inc(s_gate, 16)
            identity(pool, s_ident, ident[:, :])
            for e in range(E0):
                pool.memset(prefer[:, :, e:e + 1], float(E0 - e)).then_inc(s_const, 1)
            pool.wait_ge(s_scaled, 1)

            def biased(g):
                x1_in.wait(pool, g, 15)
                x2_ready.wait(pool, g - 1, 1)
                pool.tensor_tensor(x1b[:, :, :], x1[:, :, :], bias0[:, :].unsqueeze(1).to_broadcast([P, NT, D]),
                                   ALU.add).then_inc(x1b_ready.sem, 1)

            def low_parts(g, whole, parts, hi_ready, ready):
                for j in range(2):
                    hi_ready.wait(pool, g, j)
                    hi, lo = [feature_major(h, j) for h in parts]
                    pool.tensor_tensor(lo, feature_major(whole, j), hi.bitcast(F32), ALU.subtract).then_inc(ready.sem, 1)

            def iteration(i, parts):
                if "A" in parts:
                    low_parts(i, xt1_f, xt1, xt1_hi_ready, xt1_ready)
                if "B" in parts:
                    csum_ready.wait(pool, i - 1, 0)
                    x2_ready.wait(pool, i - 1, 1)
                    x3_ready.wait(pool, i - 2, 1)
                    pool.tensor_tensor(x2c[:, :, :], x2[:, :, :], csum[:, :].unsqueeze(2).to_broadcast([P, NT, D]),
                                       ALU.add).then_inc(x2c_ready.sem, 1)
                if "C" in parts:
                    low_parts(i - 2, xt3_f, xt3, xt3_hi_ready, xt3_ready)
                    for t in range(NT):
                        hmt_hi_ready.wait(pool, i - 2, t)
                        hi, lo, whole = [h[:, t, :, :].rearrange("p k n -> p (k n)") for h in (*hmt, hmt_f)]
                        pool.tensor_tensor(lo, whole, hi.bitcast(F32), ALU.subtract).then_inc(hmt_ready.sem, 1)

            biased(0)
            iteration(0, "A")
            biased(1)
            iteration(1, "AB")
            biased(2)
            with pool.Fori(2, NG - 1) as i:
                iteration(i, "ABC")
                biased(i + 1)
            iteration(NG - 1, "ABC")
            iteration(NG, "BC")
            iteration(NG + 1, "C")

        def prep_uses():
            return [
                ([(raw_w0[:, o, c * P:(c + 1) * P], P, c * D + o * P) for c in range(DC) for o in range(2)],
                 [(0, DC * D, [t[:, :, :].rearrange("p c d -> p (c d)") for t in w0t])]),
                ([(raw_a0[:, c * P:(c + 1) * P], P, c * C0) for c in range(DC)]
                 + [(raw_g[:, w, c * P:(c + 1) * P], E0, DC * C0 + (w * DC + c) * E0) for w in range(2) for c in range(DC)],
                 [(c * C0, C0, [t[:, c, 0:C0] for t in a0t]) for c in range(DC)]
                 + [(DC * C0 + c * E0, E0, [t[:, c, C0:C0 + E0] for t in a0t]) for c in range(DC)]
                 + [(DC * C0 + DC * E0, DC * E1, [g1t[:, :, :].rearrange("p c e -> p (c e)")])]),
                ([(raw_b0[:, o, :, :].rearrange("p e r -> p (e r)"), P, o * P) for o in range(2)],
                 [(0, D, [t[:, :] for t in b0t])]),
                *[([(raw_a1[:, r, c * P:(c + 1) * P], P, r * P) for r in range(CT1)],
                   [(0, C1, [t[:, c, :] for t in a1t])]) for c in range(DC)],
                *[([(raw_b1[:, o, 2 * k:2 * k + 2, :].rearrange("p e r -> p (e r)"), P, (k - k0) * D + o * P)
                    for k in (k0, k0 + 1) for o in range(2)],
                   [(0, 2 * D, [t[:, k0:k0 + 2, :].rearrange("p k d -> p (k d)") for t in b1t])])
                  for k0 in range(0, CT1, 2)],
            ]

        @block.scalar
        def _(act):
            for o in range(2):
                act.dma_start(raw_b0[:, o, :, :], lora_b[:, o * P:(o + 1) * P, :].rearrange("e p r -> p e r")).then_inc(s_raw, 16)
                act.dma_start(raw_b1[:, o, :, :], b1[:, o * P:(o + 1) * P, :].rearrange("e p r -> p e r")).then_inc(s_raw, 16)
            act.dma_start(raw_a1[:, :, :], a1.rearrange("e r d -> (e r) d").rearrange("(c p) d -> p c d", p=P)).then_inc(s_raw, 16)
            act.wait_ge(s_gate, 64)
            act.activation(tg[:, :], tg[:, :], ACT.Tanh).then_inc(s_tanh, 1)

            def normalise(g, n, src, dst, ready):
                scales[n].wait(act, g, 0)
                for t in range(NT):
                    last = act.activation(dst[:, t, :], src[:, t, :], ACT.Identity, scale=rstd[n][:, t:t + 1],
                                          bias=shift[n][:, t:t + 1])
                last.then_inc(ready.sem, 1)

            def turned(g, name, whole, hi, ready):
                for i in range(2):
                    full[name].wait(act, g, i)
                    for dst in (whole, hi):
                        if dst is not None:
                            last = act.activation(feature_major(dst, i), token_major(bank_of(name, i)), ACT.Copy)
                    last.then_inc(ready.sem, 1)

            def iteration(i, parts, last=False):
                a, b, c = i, i - 1, i - 2
                if "A" in parts:
                    turned(a, "xt1", xt1_f, xt1[0], xt1_hi_ready)
                if "B" in parts:
                    turned(b, "ct", ct, None, ct_ready)
                for j in range(B_NT):
                    if "B" in parts:
                        full["aff"].wait(act, b, j)
                        act.activation(th[:, j, :, :].rearrange("p c d -> p (c d)"), bank_of("aff", j)[:, :], ACT.Tanh,
                                       scale=0.5 * float(SEQ) ** -0.5).then_inc(th_ready.sem, 1)
                    if "C" in parts and j == B_NT - 3:
                        normalise(c, 2, x3, xn3, xn3_ready)
                if "A" in parts:
                    for j in range(2):
                        full["xa"].wait(act, a, j)
                        act.activation(xa[:, 2 * j:2 * j + 2, :],
                                       bank_of("xa", j)[:, 0:2 * (C0 + E0)].rearrange("p (t n) -> p t n", t=2)[:, :, 0:C0],
                                       ACT.Copy).then_inc(xa_ready.sem, 1)
                if "C" in parts:
                    turned(c, "xt3", xt3_f, xt3[0], xt3_hi_ready)
                if "A" in parts:
                    gap_ready.wait(act, a, 0)
                    act.activation(gexp[:, :], best[:, :], ACT.Exp).then_inc(gexp_ready.sem, 1)
                if "C" in parts:
                    lg1_ready.wait(act, c, 0)
                    act.activation(ex1[:, :, :], lg1[:, :, :], ACT.Exp).then_inc(ex1_ready.sem, 1)
                if "A" in parts:
                    full["xg"].wait(act, a, 0)
                    act.activation(xgt[0][:, :], bank_of("xg", 0)[:, :], ACT.Copy).then_inc(xgt_hi_ready.sem, 1)
                if "C" in parts:
                    for t in range(NT):
                        full["hm"].wait(act, c, t)
                        for dst in (hmt_f, hmt[0]):
                            end = act.activation(dst[:, t, :, :].rearrange("p k n -> p (k n)"), bank_of("hm", t)[:, :],
                                                 ACT.Copy)
                        end.then_inc(hmt_hi_ready.sem, 1)
                if "A" in parts:
                    if not last:
                        normalise(a + 1, 0, x1, xn1, xn1_ready)
                    normalise(a, 1, x2, xn2, xn2_ready)

            normalise(0, 0, x1, xn1, xn1_ready)
            for u, (_, parts) in enumerate(prep_uses()):
                act.wait_ge(s_prep, u + 1)
                for at, n, dst in parts:
                    end = act.activation(dst[0], banks[u][:, at:at + n], ACT.Copy)
                end.then_inc(s_prep_hi, 1)
            iteration(0, "A")
            iteration(1, "AB")
            with act.Fori(2, NG - 1) as i:
                iteration(i, "ABC")
            iteration(NG - 1, "ABC", last=True)
            iteration(NG, "BC")
            iteration(NG + 1, "C")

        @block.tensor
        def _(pe):
            def three(out, lhs, rhs, start, stop, **kw):
                pairs = [(0, 0), (0, 1), (1, 0)]
                for n, (a, b) in enumerate(pairs):
                    last = pe.matmul(out, lhs[a], rhs[b], start=start and n == 0, stop=stop and n == 2, **kw)
                return last

            pe.wait_ge(s_ident, IDENT_READY)
            pe.wait_ge(s_raw, 9 * 16)
            for u, (blocks, _) in enumerate(prep_uses()):
                for src, rows, at in blocks:
                    last = pe.transpose(banks[u][:, at:at + rows], src, ident[0:rows, 0:rows])
                last.then_inc(s_prep, 1)
            pe.wait_ge(s_prep_lo, len(prep_uses()))

            def take(i, parts, before, name, j):
                u = PLACE[name, j]
                for back in range(len(banks), 2 * len(USES), len(banks)):
                    v, it = (u - back) % len(USES), i - (0 if back <= u else (back - u - 1) // len(USES) + 1)
                    prev, k, part, read = USES[v]
                    if part in (parts if back <= u else before):
                        read.wait(pe, it - LAG[part], k)
                        break
                return banks[u % len(banks)]

            def stage(name, g, i, parts, before):
                def bank(j):
                    return take(i, parts, before, name, j)

                def turned(j, src):
                    b = bank(j)
                    for t in range(2):
                        for c in range(DC):
                            last = pe.transpose(b[:, (t * DC + c) * P:(t * DC + c + 1) * P],
                                                src[:, 2 * j + t, c * P:(c + 1) * P], ident[:, :])
                    last.then_inc(full[name].sem, 1)

                if name == "xt1":
                    xn1_ready.wait(pe, g, 0)
                    for j in range(2):
                        turned(j, xn1)
                elif name == "ct":
                    cin_in.wait(pe, g, 15)
                    for j in range(2):
                        turned(j, cin)
                elif name == "xt3":
                    xn3_ready.wait(pe, g, 0)
                    for j in range(2):
                        turned(j, xn3)
                elif name == "aff":
                    xn2_ready.wait(pe, g, 0)
                    for j in range(B_NT):
                        b, t, rows = bank(j), j // 2, slice(j % 2 * SEQ, (j % 2 + 1) * SEQ)
                        for c in range(DC):
                            last = pe.matmul(b[:, c * D:(c + 1) * D], xn2[rows, t, c * P:(c + 1) * P], cin[rows, t, :],
                                             start=True, stop=True)
                        last.then_inc(full[name].sem, 1)
                elif name == "xa":
                    for j in range(2):
                        xt1_ready.wait(pe, g, j)
                        b = bank(j)
                        for t in range(2):
                            s = slice((2 * j + t) * P, (2 * j + t + 1) * P)
                            for c in range(DC):
                                last = three(b[:, t * (C0 + E0):(t + 1) * (C0 + E0)], [h[:, c, s] for h in xt1],
                                             [h[:, c, :] for h in a0t], start=c == 0, stop=c == DC - 1)
                        last.then_inc(full[name].sem, 1)
                elif name == "att":
                    for j in range(2):
                        ct_ready.wait(pe, g, j)
                        th_ready.wait(pe, g, 4 * j + 3)
                        b = bank(j)
                        for t in range(2):
                            for c in range(DC):
                                for h in range(2):
                                    tok = (2 * j + t) * P + h * SEQ
                                    last = pe.matmul(b[h * SEQ:(h + 1) * SEQ, t * D:(t + 1) * D],
                                                     ct[:, c, tok:tok + SEQ], th[:, 4 * j + 2 * t + h, c, :],
                                                     start=c == 0, stop=c == DC - 1)
                        last.then_inc(full[name].sem, 1)
                elif name == "xg":
                    xg_ready.wait(pe, g, 0)
                    b = bank(0)
                    for t in range(NT):
                        last = pe.transpose(b[:, t * P:(t + 1) * P], xg[:, t, :], ident[:, :])
                    last.then_inc(full[name].sem, 1)
                elif name == "lora":
                    xgt_ready.wait(pe, g, 0)
                    for j in range(2):
                        b = bank(j)
                        for t in range(2):
                            s = slice((2 * j + t) * P, (2 * j + t + 1) * P)
                            dst = b[:, t * D:(t + 1) * D]
                            for c in range(DC):
                                three(dst, [h[:, c, s] for h in xt1], [h[:, c, :] for h in w0t],
                                      start=c == 0, stop=False)
                            last = three(dst, [h[:, s] for h in xgt], [h[:, :] for h in b0t], start=False, stop=True)
                        last.then_inc(full[name].sem, 1)
                elif name == "lg":
                    b = bank(0)
                    for t in range(NT):
                        xt3_hi_ready.wait(pe, g, t // 2)
                        s = slice(t * P, (t + 1) * P)
                        for c in range(DC):
                            last = pe.matmul(b[:, t * E1:(t + 1) * E1], xt3_f[:, c, s], g1t[:, c, :],
                                             start=c == 0, stop=c == DC - 1)
                    last.then_inc(full[name].sem, 1)
                elif name == "h":
                    for t in range(NT):
                        xt3_ready.wait(pe, g, t // 2)
                        b = bank(t)
                        s = slice(t * P, (t + 1) * P)
                        for c in range(DC):
                            last = three(b[:, :], [h[:, c, s] for h in xt3], [h[:, c, :] for h in a1t],
                                         start=c == 0, stop=c == DC - 1)
                        last.then_inc(full[name].sem, 1)
                elif name == "hm":
                    for t in range(NT):
                        hm_ready.wait(pe, g, t)
                        b = bank(t)
                        for k in range(CT1):
                            last = pe.transpose(b[:, k * P:(k + 1) * P], hm[:, t, k * P:(k + 1) * P], ident[:, :])
                        last.then_inc(full[name].sem, 1)
                elif name == "y":
                    for j in range(2):
                        b = bank(j)
                        for t in range(2):
                            hmt_ready.wait(pe, g, 2 * j + t)
                            for k in range(CT1):
                                last = three(b[:, t * D:(t + 1) * D], [h[:, 2 * j + t, k, :] for h in hmt],
                                             [h[:, k, :] for h in b1t], start=k == 0, stop=k == CT1 - 1)
                        last.then_inc(full[name].sem, 1)

            def iteration(i, parts, before):
                for name, _, part, _ in RING:
                    if part in parts:
                        stage(name, i - LAG[part], i, parts, before)

            iteration(0, "A", "")
            iteration(1, "AB", "A")
            iteration(2, "ABC", "AB")
            with pe.Fori(3, NG) as i:
                iteration(i, "ABC", "ABC")
            iteration(NG, "BC", "ABC")
            iteration(NG + 1, "C", "BC")

        @block.vector
        def _(dve):
            chain = Chain(dve, s_chain)

            def wide(v):
                return v.unsqueeze(2).to_broadcast([P, NT, E0])

            def layernorm(g, n, src):
                for t in range(NT):
                    chain.mark(dve.bn_stats(stats[:, t, :], src[:, t, :]))
                chain.wait()
                moments(dve, chain, mean[:, :], var_eps[:, :], ntmp[:, :], stats)
                rsqrt(dve, chain, rstd[n][:, :], ntmp[:, :], var_eps[:, :])
                dve.scalar_tensor_tensor(out=shift[n][:, :], in0=mean[:, :], scalar=-1.0, in1=rstd[n][:, :],
                                         op0=ALU.mult, op1=ALU.mult).then_inc(scales[n].sem, 1)
                scales[n].wait(dve, g, 0)

            def first_of_largest(values, top, pick):
                chain.link(dve.tensor_reduce(top, values, AXX, ALU.max))
                chain.link(dve.tensor_tensor(work[:, :, :], values, wide(top), ALU.is_ge))
                chain.link(dve.tensor_tensor(work[:, :, :], work[:, :, :], prefer[:, :, :], ALU.mult))
                chain.link(dve.tensor_reduce(best[:, :], work[:, :, :], AXX, ALU.max))
                chain.link(dve.tensor_tensor(pick, work[:, :, :], wide(best[:, :]), ALU.is_equal))

            def context_sum(g):
                cin_in.wait(dve, g, 15)
                chain.link(dve.tensor_reduce(csum[:, :], cin[:, :, :], AXX, ALU.add))
                dve.tensor_scalar(csum[:, :], csum[:, :], tgh[:, 0:1], None, ALU.mult).then_inc(csum_ready.sem, 1)

            def mixture_gates(g):
                for j in range(2):
                    xa_ready.wait(dve, g, j)
                    src = bank_of("xa", j)[:, 0:2 * (C0 + E0)].rearrange("p (t n) -> p t n", t=2)[:, :, C0:C0 + E0]
                    dve.tensor_tensor(lg0[:, 2 * j:2 * j + 2, :], src,
                                      gbias[:, :].unsqueeze(1).to_broadcast([P, 2, E0]),
                                      ALU.add).then_inc(lg0_ready.sem, 1)
                lg0_ready.wait(dve, g, 1)
                first_of_largest(lg0[:, :, :], top[:, 0, :], pick[0][:, :, :])
                chain.link(dve.scalar_tensor_tensor(out=lg0[:, :, :], in0=pick[0][:, :, :], scalar=-BIG,
                                                    in1=lg0[:, :, :], op0=ALU.mult, op1=ALU.add))
                first_of_largest(lg0[:, :, :], top[:, 1, :], pick[1][:, :, :])
                dve.tensor_tensor(best[:, :], top[:, 1, :], top[:, 0, :], ALU.subtract).then_inc(gap_ready.sem, 1)
                gexp_ready.wait(dve, g, 0)
                chain.link(dve.tensor_scalar(gw[:, 1, :], gexp[:, :], 1.0, None, ALU.add))
                chain.link(dve.reciprocal(gw[:, 0, :], gw[:, 1, :]))
                chain.link(dve.tensor_tensor(gw[:, 1, :], gexp[:, :], gw[:, 0, :], ALU.mult))
                for k in range(K0):
                    chain.mark(dve.tensor_tensor(pick[k][:, :, :], pick[k][:, :, :], wide(gw[:, k, :]), ALU.mult))
                chain.wait()
                chain.link(dve.tensor_tensor(gates[:, :, :], pick[0][:, :, :], pick[1][:, :, :], ALU.add))
                dve.tensor_tensor(xg[:, :, :].rearrange("p t (e r) -> p (t e) r", r=R0),
                                  xa[:, :, :].rearrange("p t (e r) -> p (t e) r", r=R0),
                                  gates[:, :, :].rearrange("p t e -> p (t e)").unsqueeze(2).to_broadcast([P, NT * E0, R0]),
                                  ALU.mult).then_inc(xg_ready.sem, 1)

            def expert_scale(g):
                full["lg"].wait(dve, g, 0)
                dve.tensor_copy(coef[:, :, :], bank_of("lg", 0)[:, 0:NT * E1].rearrange(
                    "p (t e) -> p t e", t=NT)).then_inc(lg1_read.sem, 1)
                lg1_read.wait(dve, g, 0)
                first_of_largest(coef[:, :, :], top[:, 0, :], pick[0][:, :, :])
                dve.tensor_tensor(lg1[:, :, :], coef[:, :, :], wide(top[:, 0, :]), ALU.subtract).then_inc(lg1_ready.sem, 1)
                ex1_ready.wait(dve, g, 0)
                chain.link(dve.tensor_reduce(best[:, :], ex1[:, :, :], AXX, ALU.add))
                chain.link(dve.reciprocal(gw[:, 0, :], best[:, :]))
                chain.link(dve.scalar_tensor_tensor(out=coef[:, :, :], in0=pick[0][:, :, :], scalar=EXPERT_SCALING,
                                                    in1=wide(gw[:, 0, :]), op0=ALU.mult, op1=ALU.mult))

            def chosen_expert(g):
                for t in range(NT):
                    full["h"].wait(dve, g, t)
                    dve.tensor_tensor(hm[:, t, :].rearrange("p (e r) -> p e r", e=E1),
                                      bank_of("h", t)[:, :].rearrange("p (e r) -> p e r", e=E1),
                                      coef[:, t, :].unsqueeze(2).to_broadcast([P, E1, R1]),
                                      ALU.mult).then_inc(hm_ready.sem, 1)

            def residual(g, name, dst, gate, src, ready):
                for j in range(2):
                    full[name].wait(dve, g, j)
                    new, old = [v[:, 2 * j:2 * j + 2, :].rearrange("p t d -> p (t d)") for v in (dst, src)]
                    dve.scalar_tensor_tensor(out=new, in0=bank_of(name, j)[:, :], scalar=gate, in1=old,
                                             op0=ALU.mult, op1=ALU.add).then_inc(ready.sem, 1)

            def iteration(i, parts, last=False):
                a, b, c = i, i - 1, i - 2
                if "B" in parts:
                    context_sum(b)
                if "A" in parts:
                    mixture_gates(a)
                if "C" in parts:
                    expert_scale(c)
                    chosen_expert(c)
                if "A" in parts:
                    xgt_hi_ready.wait(dve, a, 0)
                    dve.tensor_tensor(xgt[1][:, :], bank_of("xg", 0)[:, :], xgt[0][:, :].bitcast(F32),
                                      ALU.subtract).then_inc(xgt_ready.sem, 1)
                    if not last:
                        x1_in.wait(dve, a + 1, 15)
                        layernorm(a + 1, 0, x1)
                    x1b_ready.wait(dve, a, 0)
                    x2c_ready.wait(dve, a - 1, 0)
                    residual(a, "lora", x2, tg[:, 2:3], x1b, x2_ready)
                    x2_ready.wait(dve, a, 1)
                    layernorm(a, 1, x2)
                if "C" in parts:
                    out_sent.wait(dve, c - 1, 15)
                    residual(c, "y", result, tg[:, 3:4], x3, y_ready)
                if "B" in parts:
                    x2c_ready.wait(dve, b, 0)
                    y_ready.wait(dve, b - 1, 1)
                    residual(b, "att", x3, tgh[:, 0:1], x2c, x3_ready)
                    x3_ready.wait(dve, b, 1)
                    layernorm(b, 2, x3)

            x1_in.wait(dve, 0, 15)
            layernorm(0, 0, x1)
            dve.wait_ge(s_tanh, 1)
            dve.tensor_scalar(bias0[:, :], bias0[:, :], tg[:, 2:3], None, ALU.mult).then_inc(s_scaled, 1)
            chain.mark(dve.tensor_scalar(tgh[:, :], tg[:, 1:2], 0.5, None, ALU.mult))
            for u, (_, parts) in enumerate(prep_uses()):
                dve.wait_ge(s_prep_hi, u + 1)
                for at, n, dst in parts:
                    if len(dst) == 2:
                        end = dve.tensor_tensor(dst[1], banks[u][:, at:at + n], dst[0].bitcast(F32), ALU.subtract)
                end.then_inc(s_prep_lo, 1)
            dve.wait_ge(s_const, E0)
            chain.wait()
            iteration(0, "A")
            iteration(1, "AB")
            done = chain.n
            with dve.Fori(2, NG - 1) as i:
                chain.start(done + (i - 2) * CHAIN_PER)
                iteration(i, "ABC")
                assert chain.n == CHAIN_PER, chain.n
            chain.start(done + (NG - 3) * CHAIN_PER)
            iteration(NG - 1, "ABC", last=True)
            iteration(NG, "BC")
            iteration(NG + 1, "C")


_INS = ["x", "ctx_2048", "g_xattn", "g_ffn", "L0_xattn_q_w", "L0_xattn_q_b", "L0_xattn_ki_w", "L0_xattn_ki_b",
        "L0_xattn_vi_w", "L0_xattn_vi_b", "L0_xattn_o_w", "L0_xattn_o_b", "L0_xattn_nq_s", "L0_xattn_nki_s",
        "L0_ffn_W", "L0_ffn_b", "L0_ffn_lora_A", "L0_ffn_lora_B", "L0_ffn_gate_w", "L0_ffn_gate_b",
        "L1_ffn_A", "L1_ffn_Bw", "L1_ffn_Wg"]


def build(nc, a, out):
    x1 = nc.dram_tensor("x1_scratch", (NG, P, NT, D), F32, kind="Internal").ap()
    first_attention(nc, a["x"], a["ctx_2048"], a["g_xattn"],
                    *(a["L0_xattn_" + n] for n in ("q_w", "q_b", "ki_w", "ki_b", "vi_w", "vi_b", "o_w", "o_b",
                                                   "nq_s", "nki_s")), x1)
    remaining_layers(nc, x1, a["ctx_2048"], a["g_xattn"], a["g_ffn"],
                     *(a["L0_ffn_" + n] for n in ("W", "b", "lora_A", "lora_B", "gate_w", "gate_b")),
                     *(a["L1_ffn_" + n] for n in ("A", "Bw", "Wg")), out)


def kernel(**inputs):
    import numpy as _np
    import concourse.bacc as _bacc
    from concourse import mybir as _mybir
    from concourse.bass_utils import run_bass_kernel_spmd as _run

    nc = _bacc.Bacc("TRN2", target_bir_lowering=False, num_devices=1)
    arrays, args = {}, {}
    for name in _INS:
        a = _np.ascontiguousarray(inputs[name])
        arrays[f"in_{name}_dram"] = a
        args[name] = nc.dram_tensor(f"in_{name}_dram", a.shape, _mybir.dt.from_np(a.dtype), kind="ExternalInput").ap()
    out = nc.dram_tensor("out_dram", (BATCH, SEQ, D), F32, kind="ExternalOutput").ap()
    build(nc, args, out)
    return _run(nc, [arrays], core_ids=[0]).results[0]["out_dram"]
```

```python
from contextlib import ExitStack

import concourse.bass as bass
from concourse import mybir

F32 = mybir.dt.float32
F32R = mybir.dt.float32r
I32 = mybir.dt.int32
ALU = mybir.AluOpType
ACT = mybir.ActivationFunctionType
AXX = mybir.AxisListType.X

P = 128
BATCH, SEQ, D = 64, 64, 256
H, HD = 16, 128
INNER = H * HD
DC = D // P
NT = 4
GT = NT * P
NG = BATCH * SEQ // GT
E0, R0 = 8, 16
E1, R1 = 8, 64
K0 = 2
LN_EPS, RMS_EPS = 1e-5, 1e-6
EXPERT_SCALING = 64.0 / 16.0
RSQRT_SEED = 0x5F3759DF
BIG = 1e30


class Signal:

    def __init__(self, sem, per):
        self.sem, self.per = sem, per

    def count(self, g, i):
        return g * self.per + (i + 1)

    def wait(self, eng, g, i):
        if not isinstance(g, int) or self.count(g, i) > 0:
            eng.wait_ge(self.sem, self.count(g, i))


class Chain:

    def __init__(self, eng, sem):
        self.eng, self.sem, self.base, self.n = eng, sem, 0, 0

    def start(self, base):
        self.base, self.n = base, 0

    def mark(self, ins):
        self.n += 1
        ins.then_inc(self.sem, 1)

    def wait(self):
        self.eng.wait_ge(self.sem, self.base + self.n)

    def link(self, ins):
        self.mark(ins)
        self.wait()


def rsqrt_guess(dve, chain, y, t, v):
    chain.link(dve.tensor_scalar(t.bitcast(I32), v.bitcast(I32), 1, None, ALU.logical_shift_right))
    chain.link(dve.tensor_scalar(y.bitcast(I32), t.bitcast(I32), -1.0, float(RSQRT_SEED), ALU.mult, ALU.add))


def rsqrt_newton(dve, chain, y, t, v, steps):
    for _ in range(steps):
        chain.link(dve.tensor_tensor(t, y, y, ALU.mult))
        chain.link(dve.scalar_tensor_tensor(out=t, in0=t, scalar=-0.5, in1=v, op0=ALU.mult, op1=ALU.mult))
        chain.link(dve.scalar_tensor_tensor(out=y, in0=t, scalar=1.5, in1=y, op0=ALU.add, op1=ALU.mult))


def rsqrt(dve, chain, y, t, v):
    rsqrt_guess(dve, chain, y, t, v)
    rsqrt_newton(dve, chain, y, t, v, 3)


def moments(dve, chain, mean, var_eps, t, stats):
    chain.mark(dve.tensor_tensor(mean, stats[:, :, 1], stats[:, :, 4], ALU.add))
    chain.mark(dve.tensor_tensor(t, stats[:, :, 1], stats[:, :, 4], ALU.subtract))
    chain.link(dve.tensor_tensor(var_eps, stats[:, :, 2], stats[:, :, 5], ALU.add))
    chain.mark(dve.tensor_scalar(mean, mean, 0.5, None, ALU.mult))
    chain.link(dve.tensor_tensor(t, t, t, ALU.mult))
    chain.link(dve.scalar_tensor_tensor(out=t, in0=t, scalar=0.25 * D, in1=var_eps, op0=ALU.mult, op1=ALU.add))
    chain.link(dve.tensor_scalar(var_eps, t, 1.0 / D, LN_EPS, ALU.mult, ALU.add))


def identity(pool, sem, ident):
    pool.memset(ident, 0.0).then_inc(sem, 1)
    pool.wait_ge(sem, 1)
    pool.affine_select(out=ident, in_=ident, compare_op=ALU.not_equal, fill=1.0, base=0,
                       pattern=[[-1, P]], channel_multiplier=1).then_inc(sem, 1)


IDENT_READY = 2
REST = "rest"


class Shared:

    def __init__(self, nc, stack):
        def sb(name, shape):
            return stack.enter_context(nc.sbuf_tensor(name, shape, F32))

        def sem(name):
            return stack.enter_context(nc.semaphore(name))

        self.ident = sb("ident", [P, P])
        self.tg = sb("tg", [P, 4])
        self.bias0 = sb("bias0", [P, D])
        self.gbias = sb("gbias", [P, E0])
        self.prefer = sb("prefer", [P, NT, E0])
        self.tokens = sb("tokens", [P, NT, D])
        self.context = sb("context", [P, NT, D])
        self.xs = sb("xs", [P, DC, GT])
        self.cs = sb("cs", [P, DC, GT])
        self.gram = sb("gram", [P, 2, DC, D + 1])
        self.gram_j = sb("gram_j", [P, 2, D])
        self.xres = sb("xres", [P, NT, D])
        self.s_raw = sem("s_raw_rest")
        self.rstd = sb("rstd", [P, NT])
        self.shift = sb("shift", [P, NT])
        self.scales = Signal(sem("scales_rest"), 1)
        self.x1_out = Signal(sem("x1_out"), 16)
        self.x1_in = Signal(sem("x1_in"), 16)
        self.cin_in = Signal(sem("cin_in_rest"), 16)


def raw_weights(shared):
    cs = shared.cs[:, :, :].rearrange("p c n -> p (c n)")
    return (cs[:, 0:DC * D].rearrange("p (c d) -> p c d", c=DC),
            cs[:, DC * D:DC * D + D],
            cs[:, DC * D + D:DC * D + 2 * D].rearrange("p (o e r) -> p o e r", o=2, e=E0),
            shared.xs[:, :, :].rearrange("p c n -> p (c n)").rearrange("p (c d) -> p c d", d=D),
            shared.gram[:, :, :, :].rearrange("p n c d -> p (n c d)")[:, 0:2 * E1 * R1].rearrange(
                "p (o e r) -> p o e r", o=2, e=E1),
            shared.gram_j[0:E0, :, :])


def first_attention(nc, shared, late, x, ctx, g_xattn, g_ffn, b0, gate_b,
                    q_w, q_b, ki_w, ki_b, vi_w, vi_b, o_w, o_b, nq_s, nki_s, x1_dram):
    CHAIN_PER = 100
    PREP_USES = 2 + 2 * 10
    PREP_BANKS = 6
    RAW_SLOTS = 3
    BSQ_READY = 2
    ATT_LAG, OUT_LAG = 3, 4
    LN_STEP, TR_STEP, GRAM_STEP = 6, 8, 9
    x_t = x.rearrange("b s d -> (b s) d").rearrange("(g t p) d -> g p t d", g=NG, p=P)
    c_t = ctx.rearrange("b s d -> (b s) d").rearrange("(g t p) d -> g p t d", g=NG, p=P)
    with ExitStack() as stack:
        def sb(name, shape, dt=F32):
            return stack.enter_context(nc.sbuf_tensor(name, shape, dt))

        def sem(name):
            return stack.enter_context(nc.semaphore(name))

        def signal(name, per):
            return Signal(sem(name), per)

        w_hi = {n: sb(f"{n}_hi", [P, DC, INNER], F32R) for n in "qkv"}
        w_lo = {n: sb(f"{n}_lo", [P, DC, INNER], F32R) for n in "qkv"}
        wo_hi = sb("wo_hi", [P, H, D], F32R)
        wo_lo = sb("wo_lo", [P, H, D], F32R)
        gram = shared.gram
        bsq = sb("bsq", [P, 2, H])
        beta = sb("beta", [P, 2])
        ident, xin, cin, xs, cs, xres, tg = (shared.ident, shared.tokens, shared.context, shared.xs, shared.cs,
                                             shared.xres, shared.tg)
        ones = sb("ones", [P, P])
        vecs = sb("vecs", [P, 5 * H])
        qscale = sb("qscale", [P, H])
        qbias = sb("qbias", [P, H])
        obias = sb("obias", [P, D])
        stats = sb("stats", [P, NT, 6])
        mean = sb("mean", [P, NT])
        var_eps = sb("var_eps", [P, NT])
        rstd, shift = shared.rstd, shared.shift
        nt_t = sb("nt_t", [P, NT])
        sums = sb("sums", [P, 2 * NT])
        sums_b = sb("sums_b", [P, 2 * NT])
        rqk = sb("rqk", [P, 2 * NT])
        nqk_t = sb("nqk_t", [P, 2 * NT])
        gram_j = shared.gram_j
        rmax = sb("rmax", [P, NT])
        rsum = sb("rsum", [P, NT])
        rinv = sb("rinv", [P, NT])

        prep = ExitStack()
        raw = [prep.enter_context(nc.sbuf_tensor(f"raw{i}", [P, INNER], F32)) for i in range(RAW_SLOTS)]
        wt = prep.enter_context(nc.sbuf_tensor("wt", [P, H, D + 1], F32))
        vrow = prep.enter_context(nc.sbuf_tensor("vrow", [5 * H, HD], F32))
        prep.close()
        xt_hi = sb("xt_hi", [P, DC, GT], F32R)
        xt_lo = sb("xt_lo", [P, DC, GT], F32R)
        ct_hi = sb("ct_hi", [P, DC, GT], F32R)
        ct_lo = sb("ct_lo", [P, DC, GT], F32R)
        q_sb = sb("q_sb", [P, GT])
        k_sb = sb("k_sb", [P, 2, GT])
        v_sb = sb("v_sb", [P, 2, NT, 2 * HD])
        logit = sb("logit", [P, NT, SEQ])
        expo = sb("expo", [P, NT, SEQ])
        prob = sb("prob", [P, NT, SEQ])
        rr = sb("rr", [P, NT, SEQ])
        pt = sb("pt", [P, NT, P])
        ao_hi = sb("ao_hi", [P, GT], F32R)
        ao_lo = sb("ao_lo", [P, GT], F32R)
        diag = sb("diag", [P, NT, P])

        banks = [stack.enter_context(nc.psum_tensor(f"bank{i}", [P, 512], F32)) for i in range(8)]
        o_ps, pj_ps, at_ps, pv_ps, tr_ps, gr_ps = banks[0:2], banks[2:4], banks[4], banks[5], banks[6], banks[7]

        s_ident = sem("s_ident")
        s_ones = sem("s_ones")
        s_vec = sem("s_vec")
        s_gate = sem("s_gate")
        s_bias = sem("s_bias")
        s_obias = sem("s_obias")
        s_tanh = sem("s_tanh")
        s_raw = [sem(f"s_raw{i}") for i in range(RAW_SLOTS)]
        s_first = sem("s_first")
        s_whi = sem("s_whi")
        s_wlo = [sem(f"s_wlo{i}") for i in range(2)]
        s_prep = sem("s_prep")
        s_prepev = sem("s_prepev")
        s_ptzero = sem("s_ptzero")
        s_chain = sem("s_chain")
        xin_in = signal("xin_in", 16)
        cin_in = signal("cin_in", 16)
        xres_in = signal("xres_in", 16)
        x1_out = shared.x1_out
        xres_ready = signal("xres_ready", 1)
        scales_ready = signal("scales_ready", 1)
        xn_ready = signal("xn_ready", 1)
        tr_full = signal("tr_full", NT)
        tr_read = signal("tr_read", NT)
        gr_full = signal("gr_full", NT)
        gr_read = signal("gr_read", NT)
        diag_ready = signal("diag_ready", 1)
        rk_full = signal("rk_full", 1)
        rr_ready = signal("rr_ready", 1)
        split_hi = signal("split_hi", 2)
        split_lo = signal("split_lo", 2)
        pj_full = signal("pj_full", 3 * H)
        pj_read = signal("pj_read", 3 * H)
        qk_full = signal("qk_full", H)
        l_ready = signal("l_ready", H)
        e_ready = signal("e_ready", H)
        p_ready = signal("p_ready", H)
        pt_full = signal("pt_full", H)
        pt_ready = signal("pt_ready", H)
        pv_full = signal("pv_full", H)
        ao_hi_ready = signal("ao_hi_ready", H)
        ao_ready = signal("ao_ready", H)
        o_full = signal("o_full", H)
        x1_ready = signal("x1_ready", 2)

        NAMES = [("q", 0), ("q", 1), ("k", 0), ("k", 1), ("v", 0), ("v", 1), ("o", 0), ("o", 1)]

        def tr_use(n, c, f):
            return 2 + 10 * n + 4 * c + f

        def raw_in(eng, i):
            if i == 0:
                eng.wait_ge(s_first, 16)
            eng.wait_ge(s_raw[i % RAW_SLOTS], 16 * (i // RAW_SLOTS + 1))

        def weight_parts(i):
            n, c = NAMES[i]
            if n == "o":
                half = slice(c * H // 2, (c + 1) * H // 2)
                return (wo_hi[:, half, :].rearrange("p h d -> p (h d)"),
                        wo_lo[:, half, :].rearrange("p h d -> p (h d)"))
            return w_hi[n][:, c, :], w_lo[n][:, c, :]

        POOL_LOWS = (1, 2, 6)

        def low_taken(eng, i):
            by_pool = i in POOL_LOWS
            eng.wait_ge(s_wlo[by_pool], sum((j in POOL_LOWS) == by_pool for j in range(i + 1)))

        def low_part(eng, i):
            hi, lo = weight_parts(i)
            eng.wait_ge(s_whi, i + 1)
            eng.tensor_tensor(lo, raw[i % RAW_SLOTS][:, :], hi.bitcast(F32), ALU.subtract).then_inc(s_wlo[i in POOL_LOWS], 1)

        def first_group(g):
            return isinstance(g, int) and g == 0

        def tr_bank(g, t):
            return gr_ps if first_group(g) and t % 2 else tr_ps

        def live(h, first):
            return h < H and (h >= 0 or not first)

        block = stack.enter_context(nc.Block())

        @block.sync
        def _(sp):
            src = {"q": q_w, "k": ki_w, "v": vi_w}

            def view(t, g):
                return t[g] if isinstance(g, int) else t[bass.ds(g, 1)].rearrange("g p t d -> p (g t) d")

            def load_inputs(g):
                gr_read.wait(sp, g, -1)
                sp.dma_start(xin[:, :, :], view(x_t, g)).then_inc(xin_in.sem, 16)
                sp.dma_start(cin[:, :, :], view(c_t, g)).then_inc(cin_in.sem, 16)

            def store(g):
                sp.wait_ge(x1_ready.sem, x1_ready.count(g, 1))
                sp.dma_start(view(x1_dram, g), xres[:, :, :]).then_inc(x1_out.sem, 16)

            def load_rest():
                w0, a0, b0, a1, b1, gates = raw_weights(shared)
                lora_w, lora_a, lora_b, gate_w, exp_a, exp_b, wg1 = late
                gr_read.wait(sp, NG - 1, NT - 1)
                sp.dma_start(xin[:, :, :], view(x1_dram, 0)).then_inc(shared.x1_in.sem, 16)
                sp.dma_start(cin[:, :, :], view(c_t, 0)).then_inc(shared.cin_in.sem, 16)
                for n, v in enumerate((gate_w, wg1)):
                    sp.dma_start(gates[:, n, :], v).then_inc(shared.s_raw, 16)
                for o in range(2):
                    sp.dma_start(b1[:, o, :, :],
                                 exp_b[:, o * P:(o + 1) * P, :].rearrange("e p r -> p e r")).then_inc(shared.s_raw, 16)
                split_lo.wait(sp, NG - 1, 1)
                sp.dma_start(w0, lora_w.rearrange("(c p) d -> p c d", p=P)).then_inc(shared.s_raw, 16)
                sp.dma_start(a0, lora_a.rearrange("e r d -> (e r) d")).then_inc(shared.s_raw, 16)
                for o in range(2):
                    sp.dma_start(b0[:, o, :, :],
                                 lora_b[:, o * P:(o + 1) * P, :].rearrange("e p r -> p e r")).then_inc(shared.s_raw, 16)
                sp.dma_start(a1, exp_a.rearrange("e r d -> (e r) d").rearrange("(c p) d -> p c d", p=P)).then_inc(
                    shared.s_raw, 16)

            sp.dma_start(raw[0][:, 0:INNER // 2], q_w[0:P, 0:INNER // 2]).then_inc(s_first, 16)
            for j, v in enumerate((q_b, nq_s, nki_s, ki_b, vi_b)):
                sp.dma_start(vrow[j * H:(j + 1) * H, :], v.rearrange("(h d) -> h d", h=H)).then_inc(s_vec, 16)
            for i, (n, c) in enumerate(NAMES):
                slot = i % RAW_SLOTS
                if i >= RAW_SLOTS:
                    before = i - RAW_SLOTS
                    low_taken(sp, before)
                    if before < 4:
                        sp.wait_ge(s_prep, 1 + tr_use(before // 2, before % 2, 3))
                if n == "o":
                    half = o_w.rearrange("(h p) d -> p h d", h=H)[:, c * H // 2:(c + 1) * H // 2, :]
                    sp.dma_start(raw[slot][:, :].rearrange("p (h d) -> p h d", d=D), half).then_inc(s_raw[slot], 16)
                else:
                    cols = slice(INNER // 2 if i == 0 else 0, INNER)
                    sp.dma_start(raw[slot][:, cols], src[n][c * P:(c + 1) * P, cols]).then_inc(s_raw[slot], 16)
                if i == 1:
                    load_inputs(0)

            def group(g, last):
                if not last:
                    load_inputs(g + 1)
                if not first_group(g):
                    store(g - 1)
                    x1_out.wait(sp, g - 1, 15)
                sp.dma_start(xres[:, :, :], view(x_t, g)).then_inc(xres_in.sem, 16)

            group(0, False)
            with sp.Fori(1, NG - 1) as g:
                group(g, False)
            group(NG - 1, True)
            load_rest()
            store(NG - 1)

        @block.gpsimd
        def _(pool):
            identity(pool, s_ident, ident[:, :])
            pool.memset(ones[:, :], 1.0).then_inc(s_ones, 1)
            pool.dma_start(tg[:, 0:2], g_xattn.partition_broadcast(P)).then_inc(s_gate, 16)
            pool.dma_start(tg[:, 2:4], g_ffn.partition_broadcast(P)).then_inc(s_gate, 16)
            pool.dma_start(obias[:, :], o_b.partition_broadcast(P)).then_inc(s_bias, 16)
            pool.dma_start(shared.bias0[:, :], b0.partition_broadcast(P)).then_inc(s_bias, 16)
            pool.dma_start(shared.gbias[:, :], gate_b.partition_broadcast(P)).then_inc(s_bias, 16)
            for e in range(E0):
                pool.memset(shared.prefer[:, :, e:e + 1], float(E0 - e)).then_inc(s_ones, 1)
            for i in POOL_LOWS:
                low_part(pool, i)
            pool.wait_ge(s_prepev, PREP_USES)
            pool.wait_ge(s_wlo[0], len(NAMES) - len(POOL_LOWS))
            pool.wait_ge(s_wlo[1], len(POOL_LOWS))
            pool.memset(pt[:, :, :], 0.0).then_inc(s_ptzero, 1)
            pool.wait_ge(s_obias, 1)

            def group(g):
                pool.wait_ge(xres_in.sem, xres_in.count(g, 15))
                pool.tensor_tensor(xres[:, :, :], xres[:, :, :],
                                   obias[:, :].unsqueeze(1).to_broadcast([P, NT, D]),
                                   ALU.add).then_inc(xres_ready.sem, 1)

            group(0)
            with pool.Fori(1, NG) as g:
                group(g)

        @block.scalar
        def _(act):
            act.wait_ge(s_gate, 32)
            act.activation(tg[:, :], tg[:, :], ACT.Tanh).then_inc(s_tanh, 1)

            def high_part(i):
                raw_in(act, i)
                act.activation(weight_parts(i)[0], raw[i % RAW_SLOTS][:, :], ACT.Copy).then_inc(s_whi, 1)

            def normalise(g):
                act.wait_ge(scales_ready.sem, scales_ready.count(g, 0))
                for t in range(NT):
                    last = act.activation(xin[:, t, :], xin[:, t, :], ACT.Identity, scale=rstd[:, t:t + 1],
                                          bias=shift[:, t:t + 1])
                last.then_inc(xn_ready.sem, 1)

            def transposed(g, t):
                act.wait_ge(tr_full.sem, tr_full.count(g, t))
                b = tr_bank(g, t)
                act.activation(xs[:, :, t * P:(t + 1) * P],
                               b[:, 0:D].rearrange("p (c n) -> p c n", c=DC), ACT.Copy)
                act.activation(cs[:, :, t * P:(t + 1) * P],
                               b[:, D:2 * D].rearrange("p (c n) -> p c n", c=DC), ACT.Copy).then_inc(tr_read.sem, 1)

            def split(g):
                act.wait_ge(tr_read.sem, tr_read.count(g, NT - 1))
                if first_group(g):
                    act.wait_ge(s_wlo[0], len(NAMES) - len(POOL_LOWS))
                    act.wait_ge(s_wlo[1], len(POOL_LOWS))
                    act.wait_ge(s_prepev, PREP_USES)
                pj_full.wait(act, g, -1)
                act.activation(ct_hi[:, :, :], cs[:, :, :], ACT.Copy).then_inc(split_hi.sem, 1)
                act.activation(xt_hi[:, :, :], xs[:, :, :], ACT.Copy).then_inc(split_hi.sem, 1)

            def attn_hi(g, h):
                act.wait_ge(pv_full.sem, pv_full.count(g, h))
                act.activation(ao_hi[:, :], pv_ps[:, :], ACT.Identity,
                               bias=vecs[:, 4 * H + h % H:4 * H + h % H + 1]).then_inc(ao_hi_ready.sem, 1)

            def exps(g, h):
                act.wait_ge(l_ready.sem, l_ready.count(g, h))
                act.activation(expo[:, :, :], logit[:, :, :], ACT.Exp).then_inc(e_ready.sem, 1)

            def project(g, h, j):
                act.wait_ge(pj_full.sem, pj_full.count(g, 3 * h + j))
                bank = pj_ps[(3 * h + j) % 2]
                if j == 0:
                    act.activation(k_sb[:, h % 2, :], bank[:, :], ACT.Identity,
                                   bias=vecs[:, 3 * H + h:3 * H + h + 1]).then_inc(pj_read.sem, 1)
                elif j == 1:
                    t = 2 * (h % 2)
                    act.activation(v_sb[:, (h // 2) % 2, t:t + 2, :],
                                   bank[:, :].rearrange("p (t n) -> p t n", t=2), ACT.Copy).then_inc(pj_read.sem, 1)
                else:
                    act.activation(q_sb[:, :], bank[:, :], ACT.Identity, scale=qscale[:, h:h + 1],
                                   bias=qbias[:, h:h + 1]).then_inc(pj_read.sem, 1)

            def step(g, h, first, last):
                if 0 < h < H:
                    project(g, h, 0)
                if live(h - ATT_LAG, first):
                    attn_hi(g, h - ATT_LAG)
                if h == 0:
                    project(g, h, 0)
                if h < H:
                    project(g, h, 1)
                if live(h - 1, first):
                    exps(g, h - 1)
                if h < H:
                    project(g, h, 2)
                if not last and h == LN_STEP + 1:
                    normalise(g + 1)
                if not last and TR_STEP <= h < TR_STEP + NT:
                    transposed(g + 1, h - TR_STEP)

            high_part(0)
            high_part(1)
            normalise(0)
            high_part(2)
            high_part(3)
            high_part(4)
            for t in range(NT):
                transposed(0, t)
            for i in range(5, len(NAMES)):
                high_part(i)
            split(0)
            for h in range(H):
                step(0, h, True, False)
            split(1)
            with act.Fori(1, NG - 1) as g:
                for h in range(H):
                    step(g, h, False, False)
                split(g + 1)
            for h in range(H + ATT_LAG):
                step(NG - 1, h, False, True)

        @block.tensor
        def _(pe):
            def three(out, lhs, rhs, start, stop, **kw):
                pairs = [(0, 0), (0, 1), (1, 0)]
                for n, (a, b) in enumerate(pairs):
                    last = pe.matmul(out, lhs[a], rhs[b], start=start and n == 0, stop=stop and n == 2, **kw)
                return last

            use = [0]

            def bank():
                if use[0] >= PREP_BANKS:
                    pe.wait_ge(s_prepev, use[0] - PREP_BANKS + 1)
                use[0] += 1
                return banks[(use[0] - 1) % PREP_BANKS]

            def turn_weight(n):
                for c in range(DC):
                    i = 2 * n + c
                    if i > 0:
                        raw_in(pe, i)
                    for f in range(4):
                        if i == 0 and f == 0:
                            pe.wait_ge(s_first, 16)
                        if i == 0 and f == 2:
                            raw_in(pe, i)
                        assert use[0] == tr_use(n, c, f)
                        b = bank()
                        for j in range(4):
                            h = 4 * f + j
                            last = pe.transpose(b[:, j * P:(j + 1) * P], raw[i % RAW_SLOTS][:, h * P:(h + 1) * P],
                                                ident[:, :])
                        last.then_inc(s_prep, 1)

            def gram_matrix(n):
                pe.wait_ge(s_prepev, tr_use(n, DC - 1, 3) + 1)
                for c in range(DC):
                    b = bank()
                    for h in range(H):
                        last = pe.matmul(b[:, c * P:D + 1], wt[:, h, c * P:(c + 1) * P], wt[:, h, c * P:D + 1],
                                         start=h == 0, stop=h == H - 1)
                    last.then_inc(s_prep, 1)

            def transposes(g, t):
                b = tr_bank(g, t)
                tr_read.wait(pe, g, t - 2 if first_group(g) else t - 1)
                if t > 0 and not first_group(g):
                    gr_read.wait(pe, g, t - 1)
                if t == 0:
                    pe.wait_ge(xn_ready.sem, xn_ready.count(g, 0))
                    pe.wait_ge(cin_in.sem, cin_in.count(g, 15))
                    rr_ready.wait(pe, g, -1)
                for s, src in enumerate((xin, cin)):
                    for c in range(DC):
                        last = pe.transpose(b[:, (2 * s + c) * P:(2 * s + c + 1) * P],
                                            src[:, t, c * P:(c + 1) * P], ident[:, :])
                last.then_inc(tr_full.sem, 1)

            def gram_products(g, t, transposed):
                pe.wait_ge(tr_read.sem, tr_read.count(g, transposed))
                gr_read.wait(pe, g, t - 1)
                for n, (b, src) in enumerate(((gr_ps, xs), (tr_ps, cs))):
                    for c in range(DC):
                        last = pe.matmul(b[:, c * P:D + 1], src[:, c, t * P:(t + 1) * P],
                                         gram[:, n, c, c * P:D + 1], start=c == 0, stop=c == DC - 1)
                last.then_inc(gr_full.sem, 1)

            def norms(g):
                pe.wait_ge(diag_ready.sem, diag_ready.count(g, 0))
                pe.matmul(tr_ps[:, :], ones[:, :], diag[:, :, :].rearrange("p t n -> p (t n)"),
                          start=True, stop=True).then_inc(rk_full.sem, 1)

            def prob_transpose(g, h):
                pe.wait_ge(p_ready.sem, p_ready.count(g, h))
                pe.wait_ge(l_ready.sem, l_ready.count(g, min(h + 1, H - 1)))
                for q in range(2):
                    last = pe.transpose(at_ps[:, q * P:(q + 1) * P],
                                        prob[:, 2 * q:2 * q + 2, :].rearrange("p t l -> p (t l)"), ident[:, :])
                last.then_inc(pt_full.sem, 1)

            def attend(g, h):
                pe.wait_ge(pt_ready.sem, pt_ready.count(g, h))
                pe.wait_ge(pj_read.sem, pj_read.count(g, 3 * (h + 1 - h % 2) + 1))
                ao_ready.wait(pe, g, h - 1)
                for t in range(NT):
                    last = pe.matmul(pv_ps[:, t * P:(t + 1) * P],
                                     v_sb[:, (h // 2) % 2, t, (h % 2) * HD:(h % 2 + 1) * HD],
                                     pt[:, t, :], start=True, stop=True)
                last.then_inc(pv_full.sem, 1)

            def scores(g, h):
                pe.wait_ge(pj_read.sem, pj_read.count(g, 3 * h + 2))
                pt_ready.wait(pe, g, h + 1 - ATT_LAG)
                for t in range(NT):
                    for b in range(2):
                        s = slice(t * P + b * SEQ, t * P + (b + 1) * SEQ)
                        last = pe.matmul(at_ps[b * SEQ:(b + 1) * SEQ, t * SEQ:(t + 1) * SEQ],
                                         q_sb[:, s], k_sb[:, h % 2, s], start=True, stop=True)
                last.then_inc(qk_full.sem, 1)

            def output(g, h):
                pe.wait_ge(ao_ready.sem, ao_ready.count(g, h))
                for t in range(NT):
                    if h % H == 0 and t % 2 == 0:
                        x1_ready.wait(pe, g + h // H - 1, t // 2)
                    s = slice(t * P, (t + 1) * P)
                    last = three(o_ps[t // 2][:, (t % 2) * D:(t % 2 + 1) * D], (ao_hi[:, s], ao_lo[:, s]),
                                 (wo_hi[:, h % H, :], wo_lo[:, h % H, :]),
                                 start=h % H == 0 and t % 2 == 0, stop=h % H == H - 1, skip_group_check=True)
                last.then_inc(o_full.sem, 1)

            def bank_for(g, u):
                pj_read.wait(pe, g, u - 2)
                return pj_ps[u % 2]

            def values(g, h):
                b = bank_for(g, 3 * h + 1)
                pair = slice((h - h % 2) * HD, (h - h % 2 + 2) * HD)
                for i in range(2):
                    t = 2 * (h % 2) + i
                    s = slice(t * P, (t + 1) * P)
                    for c in range(DC):
                        last = three(b[:, i * 2 * HD:(i + 1) * 2 * HD], (ct_hi[:, c, s], ct_lo[:, c, s]),
                                     (w_hi["v"][:, c, pair], w_lo["v"][:, c, pair]), start=c == 0, stop=c == DC - 1)
                last.then_inc(pj_full.sem, 1)

            def project(g, h, j):
                b = bank_for(g, 3 * h + j)
                n, hi, lo = ("k", ct_hi, ct_lo) if j == 0 else ("q", xt_hi, xt_lo)
                if h == 0:
                    pe.wait_ge(split_lo.sem, split_lo.count(g, j // 2))
                cols = slice(h * HD, (h + 1) * HD)
                for c in range(DC):
                    last = three(b[:, :], (w_hi[n][:, c, cols], w_lo[n][:, c, cols]), (hi[:, c, :], lo[:, c, :]),
                                 start=c == 0, stop=c == DC - 1)
                last.then_inc(pj_full.sem, 1)

            def step(g, h, first, last):
                if live(h - ATT_LAG, first):
                    prob_transpose(g, h - ATT_LAG)
                if live(h - OUT_LAG, first):
                    output(g, h - OUT_LAG)
                if 0 < h < H:
                    project(g, h, 0)
                if live(h - ATT_LAG, first):
                    attend(g, h - ATT_LAG)
                if live(h - 1, first):
                    scores(g, h - 1)
                if h == 1 and first:
                    norms(0)
                if h == 0:
                    project(g, h, 0)
                    if first:
                        gram_products(0, 2, NT - 1)
                if not last and GRAM_STEP <= h < GRAM_STEP + NT:
                    gram_products(g + 1, h - GRAM_STEP, h - GRAM_STEP)
                if h < H:
                    values(g, h)
                    if h == 0 and first:
                        gram_products(0, 3, NT - 1)
                    project(g, h, 2)
                if not last:
                    if TR_STEP <= h < TR_STEP + NT:
                        transposes(g + 1, h - TR_STEP)
                    if h == H - 1:
                        norms(g + 1)

            pe.wait_ge(s_ident, IDENT_READY)
            pe.wait_ge(s_vec, 80)
            pe.transpose(bank()[:, 0:5 * H], vrow[:, :], ident[0:5 * H, 0:5 * H]).then_inc(s_prep, 1)
            pe.wait_ge(s_ones, 1)
            pe.wait_ge(s_chain, BSQ_READY)
            pe.matmul(bank()[:, 0:2 * H], ones[:, :], bsq[:, :, :].rearrange("p n h -> p (n h)"),
                      start=True, stop=True).then_inc(s_prep, 1)
            turn_weight(0)
            gram_matrix(0)
            turn_weight(1)
            for t in range(NT):
                transposes(0, t)
            gram_matrix(1)
            pe.wait_ge(s_prepev, PREP_USES)
            gram_products(0, 0, NT - 1)
            gram_products(0, 1, NT - 1)
            pe.wait_ge(s_wlo[0], len(NAMES) - len(POOL_LOWS))
            pe.wait_ge(s_wlo[1], len(POOL_LOWS))
            for h in range(H):
                if h == ATT_LAG:
                    pe.wait_ge(s_ptzero, 1)
                step(0, h, True, False)
            with pe.Fori(1, NG - 1) as g:
                for h in range(H):
                    step(g, h, False, False)
            for h in range(H + OUT_LAG):
                step(NG - 1, h, False, True)

        @block.vector
        def _(dve):
            chain = Chain(dve, s_chain)
            use = [0]

            def prepared():
                use[0] += 1
                dve.wait_ge(s_prep, use[0])
                return banks[(use[0] - 1) % PREP_BANKS]

            def weight_copies(n):
                v = (0, 3)[n] * H
                dve.tensor_copy(wt[:, :, D:D + 1], vecs[:, v:v + H].unsqueeze(2))
                for c in range(DC):
                    for f in range(4):
                        dve.tensor_copy(wt[:, 4 * f:4 * f + 4, c * P:(c + 1) * P],
                                        prepared()[:, :].rearrange("p (h n) -> p h n", h=4)).then_inc(s_prepev, 1)

            def gram_copies(n):
                b = prepared()
                dve.tensor_copy(gram[:, n, 0, 0:P], b[:, 0:P])
                dve.tensor_scalar(gram[:, n, 0, P:D + 1], b[:, P:D + 1], 2.0, None, ALU.mult).then_inc(s_prepev, 1)
                b = prepared()
                dve.tensor_copy(gram[:, n, 1, P:D], b[:, P:D])
                dve.tensor_scalar(gram[:, n, 1, D:D + 1], b[:, D:D + 1], 2.0, None, ALU.mult).then_inc(s_prepev, 1)

            def tile_stats(g, t):
                if t == 0:
                    if g is REST:
                        dve.wait_ge(shared.x1_in.sem, shared.x1_in.count(0, 15))
                    else:
                        dve.wait_ge(xin_in.sem, xin_in.count(g, 15))
                chain.mark(dve.bn_stats(stats[:, t, :], xin[:, t, :]))

            def tile_variances(g):
                chain.wait()
                moments(dve, chain, mean[:, :], var_eps[:, :], nt_t[:, :], stats)
                rsqrt_guess(dve, chain, rstd[:, :], nt_t[:, :], var_eps[:, :])

            def tile_scales(g):
                rsqrt_newton(dve, chain, rstd[:, :], nt_t[:, :], var_eps[:, :], 3)
                dve.scalar_tensor_tensor(out=shift[:, :], in0=mean[:, :], scalar=-1.0, in1=rstd[:, :],
                                         op0=ALU.mult, op1=ALU.mult).then_inc(
                    shared.scales.sem if g is REST else scales_ready.sem, 1)

            def gram_sums(g, t):
                dve.wait_ge(gr_full.sem, gr_full.count(g, t))
                for n, (b, src) in enumerate(((gr_ps, xin), (tr_ps, cin))):
                    last = dve.tensor_tensor_reduce(gram_j[:, n, :], b[:, 0:D], src[:, t, :], 1.0, b[:, D:D + 1], ALU.mult,
                                                    ALU.add, sums[:, n * NT + t:n * NT + t + 1])
                last.then_inc(gr_read.sem, 1)

            def square_norms(g):
                dve.wait_ge(gr_read.sem, gr_read.count(g, NT - 1))
                for n in range(2):
                    half = slice(n * NT, (n + 1) * NT)
                    chain.mark(dve.tensor_scalar(sums_b[:, half], sums[:, half], beta[:, n:n + 1],
                                                 1.0 / INNER, ALU.add, ALU.mult))
                chain.wait()
                chain.link(dve.tensor_scalar(sums_b[:, :], sums_b[:, :], RMS_EPS, None, ALU.add))
                rsqrt_guess(dve, chain, rqk[:, :], nqk_t[:, :], sums_b[:, :])
                rsqrt_newton(dve, chain, rqk[:, :], nqk_t[:, :], sums_b[:, :], 1)

            def norm_factors(g):
                rsqrt_newton(dve, chain, rqk[:, :], nqk_t[:, :], sums_b[:, :], 2)
                for t in range(NT):
                    last = dve.tensor_scalar(diag[:, t, :], ident[:, :], rqk[:, NT + t:NT + t + 1], None, ALU.mult)
                last.then_inc(diag_ready.sem, 1)

            def score_factors(g):
                dve.wait_ge(rk_full.sem, rk_full.count(g, 0))
                for t in range(NT):
                    for b in range(2):
                        rows = slice(b * SEQ, (b + 1) * SEQ)
                        last = dve.tensor_scalar(rr[rows, t, :], tr_ps[rows, t * P + b * SEQ:t * P + (b + 1) * SEQ],
                                                 rqk[rows, t:t + 1], float(HD) ** -0.5, ALU.mult, ALU.mult)
                last.then_inc(rr_ready.sem, 1)

            def split(g):
                for n, (lo, hi, src) in enumerate(((ct_lo, ct_hi, cs), (xt_lo, xt_hi, xs))):
                    dve.wait_ge(split_hi.sem, split_hi.count(g, n))
                    dve.tensor_tensor(lo[:, :, :], src[:, :, :], hi[:, :, :].bitcast(F32),
                                      ALU.subtract).then_inc(split_lo.sem, 1)

            def prob_copy(g, h):
                dve.wait_ge(pt_full.sem, pt_full.count(g, h))
                for q in range(2):
                    for b in range(2):
                        src = at_ps[q * SEQ:(q + 1) * SEQ, 0:2 * P].rearrange("p (t s) -> p t s", t=2)
                        last = dve.tensor_copy(pt[b * SEQ:(b + 1) * SEQ, q::2, b * SEQ:(b + 1) * SEQ],
                                               src[:, :, b * SEQ:(b + 1) * SEQ])
                last.then_inc(pt_ready.sem, 1)

            def attn_lo(g, h):
                v = 4 * H + h % H
                dve.wait_ge(ao_hi_ready.sem, ao_hi_ready.count(g, h))
                dve.scalar_tensor_tensor(out=ao_lo[:, :], in0=pv_ps[:, :], scalar=vecs[:, v:v + 1],
                                         in1=ao_hi[:, :].bitcast(F32), op0=ALU.add,
                                         op1=ALU.subtract).then_inc(ao_ready.sem, 1)

            def logits(g, h):
                dve.wait_ge(qk_full.sem, qk_full.count(g, h))
                if h == 0:
                    dve.wait_ge(rr_ready.sem, rr_ready.count(g, 0))
                chain.link(dve.tensor_tensor(logit[:, :, :], at_ps[:, 0:NT * SEQ].rearrange("p (t l) -> p t l", t=NT),
                                             rr[:, :, :], ALU.mult))
                chain.link(dve.tensor_reduce(rmax[:, :], logit[:, :, :], AXX, ALU.max))
                dve.tensor_tensor(logit[:, :, :], logit[:, :, :],
                                  rmax[:, :].unsqueeze(2).to_broadcast([P, NT, SEQ]),
                                  ALU.subtract).then_inc(l_ready.sem, 1)

            def probabilities(g, h):
                dve.wait_ge(e_ready.sem, e_ready.count(g, h))
                chain.link(dve.tensor_reduce(rsum[:, :], expo[:, :, :], AXX, ALU.add))
                chain.link(dve.reciprocal(rinv[:, :], rsum[:, :]))
                dve.tensor_tensor(prob[:, :, :], expo[:, :, :], rinv[:, :].unsqueeze(2).to_broadcast([P, NT, SEQ]),
                                  ALU.mult).then_inc(p_ready.sem, 1)

            def residual(g, i):
                if i == 0:
                    dve.wait_ge(o_full.sem, o_full.count(g, H - 1))
                    dve.wait_ge(xres_ready.sem, xres_ready.count(g, 0))
                rows = xres[:, 2 * i:2 * i + 2, :].rearrange("p t d -> p (t d)")
                dve.scalar_tensor_tensor(out=rows, in0=o_ps[i][:, :], scalar=tg[:, 0:1], in1=rows,
                                         op0=ALU.mult, op1=ALU.add).then_inc(x1_ready.sem, 1)

            def step(g, h, first, last):
                if live(h - ATT_LAG, first):
                    prob_copy(g, h - ATT_LAG)
                if h == 0 and not first:
                    split(g)
                if live(h - 2, first):
                    probabilities(g, h - 2)
                if live(h - ATT_LAG, first):
                    attn_lo(g, h - ATT_LAG)
                if h == OUT_LAG - 1 and not first:
                    residual(g - 1, 0)
                if h == 1 and first:
                    score_factors(g)
                if live(h - 1, first):
                    logits(g, h - 1)
                if h == 0 and not first:
                    score_factors(g)
                if h == OUT_LAG - 1 and not first:
                    residual(g - 1, 1)
                ln_step, ln_group = (LN_STEP + 4, REST) if last else (LN_STEP, g + 1)
                if ln_step - NT <= h < ln_step:
                    tile_stats(ln_group, h - ln_step + NT)
                if h == ln_step:
                    tile_variances(ln_group)
                if h == ln_step + 1:
                    tile_scales(ln_group)
                if not last:
                    if GRAM_STEP <= h < GRAM_STEP + NT:
                        gram_sums(g + 1, h - GRAM_STEP)
                    if h == GRAM_STEP + NT:
                        square_norms(g + 1)
                    if h == GRAM_STEP + NT + 1:
                        norm_factors(g + 1)

            dve.tensor_copy(vecs[:, :], prepared()[:, 0:5 * H]).then_inc(s_prepev, 1)
            dve.wait_ge(s_prepev, 1)
            chain.mark(dve.tensor_tensor(bsq[:, 0, :], vecs[:, 0:H], vecs[:, 0:H], ALU.mult))
            chain.mark(dve.tensor_tensor(bsq[:, 1, :], vecs[:, 3 * H:4 * H], vecs[:, 3 * H:4 * H], ALU.mult))
            assert chain.n == BSQ_READY
            chain.link(dve.tensor_tensor(qscale[:, :], vecs[:, H:2 * H], vecs[:, 2 * H:3 * H], ALU.mult))
            chain.mark(dve.tensor_tensor(qbias[:, :], vecs[:, 0:H], qscale[:, :], ALU.mult))
            dve.tensor_reduce(beta[:, :], prepared()[:, 0:2 * H].rearrange("p (n h) -> p n h", n=2), AXX,
                              ALU.add).then_inc(s_prepev, 1)
            weight_copies(0)
            low_part(dve, 0)
            for t in range(NT):
                tile_stats(0, t)
            tile_variances(0)
            tile_scales(0)
            gram_copies(0)
            weight_copies(1)
            low_part(dve, 3)
            low_part(dve, 4)
            low_part(dve, 5)
            gram_copies(1)
            dve.wait_ge(s_prepev, PREP_USES)
            gram_sums(0, 0)
            low_part(dve, 7)
            gram_sums(0, 1)
            split(0)
            gram_sums(0, 2)
            gram_sums(0, 3)
            square_norms(0)
            norm_factors(0)
            dve.wait_ge(s_tanh, 1)
            dve.wait_ge(s_bias, 48)
            dve.tensor_scalar(obias[:, :], obias[:, :], tg[:, 0:1], None, ALU.mult).then_inc(s_obias, 1)
            dve.tensor_scalar(shared.bias0[:, :], shared.bias0[:, :], tg[:, 2:3], None, ALU.mult)
            for h in range(H):
                if h == ATT_LAG:
                    dve.wait_ge(s_ptzero, 1)
                step(0, h, True, False)
            done = chain.n
            with dve.Fori(1, NG - 1) as g:
                chain.start(done + (g - 1) * CHAIN_PER)
                for h in range(H):
                    step(g, h, False, False)
                assert chain.n == CHAIN_PER, chain.n
            chain.start(done + (NG - 2) * CHAIN_PER)
            for h in range(H + ATT_LAG):
                step(NG - 1, h, False, True)
            for i in range(2):
                residual(NG - 1, i)


def remaining_layers(nc, shared, x1_dram, ctx, out):
    CHAIN_PER = 92
    LAG = {"A": 0, "B": 1, "C": 2}
    c_t = ctx.rearrange("b s d -> (b s) d").rearrange("(g t p) d -> g p t d", g=NG, p=P)
    out_t = out.rearrange("b s d -> (b s) d").rearrange("(g t p) d -> g p t d", g=NG, p=P)
    C0, C1 = E0 * R0, E1 * R1
    CT1 = C1 // P
    B_NT = 2 * NT
    with ExitStack() as stack:
        def sb(name, shape, dt=F32):
            return stack.enter_context(nc.sbuf_tensor(name, shape, dt))

        def sem(name):
            return stack.enter_context(nc.semaphore(name))

        def signal(name, per):
            return Signal(sem(name), per)

        def both(name, shape):
            return sb(name + "_hi", shape, F32R), sb(name + "_lo", shape, F32R)

        w0t = both("w0t", [P, DC, D])
        a0t = both("a0t", [P, DC, C0 + E0])
        b0t = both("b0t", [P, D])
        a1t = both("a1t", [P, DC, C1])
        g1t = both("g1t", [P, DC, E1])
        b1t = both("b1t", [P, CT1, D])
        raw_w0, raw_a0, raw_b0, raw_a1, raw_b1, raw_g = raw_weights(shared)
        ident, tg, bias0, gbias, prefer = shared.ident, shared.tg, shared.bias0, shared.gbias, shared.prefer
        tgh = sb("tgh", [P, 1])

        stats = sb("stats2", [P, NT, 6])
        mean = sb("mean2", [P, NT])
        var_eps = sb("var_eps2", [P, NT])
        ntmp = sb("ntmp2", [P, NT])
        rstd = [shared.rstd] + [sb(f"rstd{n}", [P, NT]) for n in (1, 2)]
        shift = [shared.shift] + [sb(f"shift{n}", [P, NT]) for n in (1, 2)]
        x1 = shared.tokens
        x1b = sb("x1b", [P, NT, D])
        xn1 = sb("xn1", [P, NT, D])
        xt1_f = sb("xt1_f", [P, DC, GT])
        xt1 = both("xt1", [P, DC, GT])
        xa = sb("xa", [P, NT, C0])
        lg0 = sb("lg0", [P, NT, E0])
        work = sb("work", [P, NT, E0])
        pick = [sb(f"pick{i}", [P, NT, E0]) for i in range(2)]
        top = sb("top", [P, 2, NT])
        best = sb("best", [P, NT])
        gexp = sb("gexp", [P, NT])
        gw = sb("gw", [P, 2, NT])
        gates = sb("gates", [P, NT, E0])
        xg = sb("xg", [P, NT, C0])
        xgt = both("xgt", [P, GT])
        x2 = sb("x2", [P, NT, D])
        xn2 = sb("xn2", [P, NT, D])
        cin = shared.context
        ct = sb("ct", [P, DC, GT])
        csum = sb("csum", [P, NT])
        x2c = sb("x2c", [P, NT, D])
        th = sb("th", [P, B_NT, DC, D])
        x3 = sb("x3", [P, NT, D])
        xn3 = sb("xn3", [P, NT, D])
        xt3_f = sb("xt3_f", [P, DC, GT])
        xt3 = both("xt3", [P, DC, GT])
        lg1 = sb("lg1", [P, NT, E1])
        ex1 = sb("ex1", [P, NT, E1])
        coef = sb("coef", [P, NT, E1])
        hm = sb("hm", [P, NT, C1])
        hmt_f = sb("hmt_f", [P, NT, CT1, P])
        hmt = both("hmt", [P, NT, CT1, P])
        result = sb("result", [P, NT, D])
        banks = [stack.enter_context(nc.psum_tensor(f"ban2k{i}", [P, 512], F32)) for i in range(8)]

        s_prep = sem("s_prep2")
        s_prep_hi = sem("s_prep_hi")
        s_prep_lo = sem("s_prep_lo")
        s_chain = sem("s_chain2")
        x1_in, cin_in = shared.x1_in, shared.cin_in
        out_sent = signal("out_sent", 16)
        x1b_ready = signal("x1b_ready", 1)
        scales = [shared.scales] + [signal(f"scales{n}", 1) for n in (1, 2)]
        xn1_ready = signal("xn1_ready", 1)
        xn2_ready = signal("xn2_ready", 1)
        xn3_ready = signal("xn3_ready", 1)
        xt1_hi_ready = signal("xt1_hi_ready", 2)
        xt1_ready = signal("xt1_ready", 2)
        xa_ready = signal("xa_ready", 2)
        lg0_ready = signal("lg0_ready", 2)
        gap_ready = signal("gap_ready", 1)
        gexp_ready = signal("gexp_ready", 1)
        xg_ready = signal("xg_ready", 1)
        xgt_hi_ready = signal("xgt_hi_ready", 1)
        xgt_ready = signal("xgt_ready", 1)
        x2_ready = signal("x2_ready", 2)
        ct_ready = signal("ct_ready", 2)
        csum_ready = signal("csum_ready", 1)
        x2c_ready = signal("x2c_ready", 1)
        th_ready = signal("th_ready", B_NT)
        x3_ready = signal("x3_ready", 2)
        x3_copied = signal("x3_copied", 1)
        xt3_hi_ready = signal("xt3_hi_ready", 2)
        xt3_ready = signal("xt3_ready", 2)
        lg1_ready = signal("lg1_ready", 1)
        lg1_read = signal("lg1_read", 1)
        ex1_ready = signal("ex1_ready", 1)
        hm_ready = signal("hm_ready", NT)
        hmt_hi_ready = signal("hmt_hi_ready", NT)
        hmt_ready = signal("hmt_ready", NT)
        y_ready = signal("y_ready", 2)

        RING = [("xt1", range(2), "A", xt1_hi_ready), ("ct", range(2), "B", ct_ready),
                ("aff", range(B_NT // 2), "B", th_ready), ("xa", range(2), "A", lg0_ready),
                ("aff", range(B_NT // 2, B_NT - 3), "B", th_ready), ("xt3", range(2), "C", xt3_hi_ready),
                ("aff", range(B_NT - 3, B_NT), "B", th_ready), ("h", range(1), "C", hm_ready),
                ("lg", range(1), "C", lg1_read), ("h", range(1, 3), "C", hm_ready), ("xg", range(1), "A", xgt_ready),
                ("h", range(3, NT), "C", hm_ready), ("lora", range(2), "A", x2_ready),
                ("hm", range(NT), "C", hmt_hi_ready), ("att", range(2), "B", x3_ready),
                ("y", range(2), "C", y_ready)]
        full = {name: signal(f"{name}_full", js.stop) for name, js in {name: js for name, js, _, _ in RING}.items()}
        USES = [(name, i, part, read) for name, js, part, read in RING for i in js]
        PLACE = {(name, i): u for u, (name, i, _, _) in enumerate(USES)}
        assert len(USES) % len(banks) == 0

        def bank_of(name, i):
            return banks[PLACE[name, i] % len(banks)]

        def token_major(bank):
            return bank[:, :].rearrange("p (t c n) -> p t c n", t=2, c=DC)

        def feature_major(buf, i):
            return buf[:, :, 2 * i * P:2 * (i + 1) * P].rearrange("p c (t n) -> p t c n", t=2)

        block = stack.enter_context(nc.Block())

        @block.sync
        def _(sp):
            def at(t, g):
                return t[g] if isinstance(g, int) else t[bass.ds(g, 1)].rearrange("g p t d -> p (g t) d")

            def load_x1(g):
                xn1_ready.wait(sp, g - 1, 0)
                x1b_ready.wait(sp, g - 1, 0)
                sp.dma_start(x1[:, :, :], at(x1_dram, g)).then_inc(x1_in.sem, 16)

            def load_ctx(g):
                th_ready.wait(sp, g - 1, B_NT - 1)
                csum_ready.wait(sp, g - 1, 0)
                sp.dma_start(cin[:, :, :], at(c_t, g)).then_inc(cin_in.sem, 16)

            def store(g):
                sp.wait_ge(y_ready.sem, y_ready.count(g, 1))
                sp.dma_start(at(out_t, g), result[:, :, :]).then_inc(out_sent.sem, 16)

            shared.x1_out.wait(sp, NG - 1, 15)
            load_x1(1)
            load_x1(2)
            load_ctx(1)
            load_x1(3)
            load_ctx(2)
            with sp.Fori(3, NG - 1) as i:
                load_x1(i + 1)
                store(i - 3)
                load_ctx(i)
            store(NG - 4)
            load_ctx(NG - 1)
            for g in range(NG - 3, NG):
                store(g)
            out_sent.wait(sp, NG - 1, 15)

        @block.gpsimd
        def _(pool):
            def biased(g):
                pool.wait_ge(x1_in.sem, x1_in.count(g, 15))
                x2_ready.wait(pool, g - 1, 1)
                pool.tensor_tensor(x1b[:, :, :], x1[:, :, :], bias0[:, :].unsqueeze(1).to_broadcast([P, NT, D]),
                                   ALU.add).then_inc(x1b_ready.sem, 1)

            def low_parts(g, whole, parts, hi_ready, ready):
                for j in range(2):
                    pool.wait_ge(hi_ready.sem, hi_ready.count(g, j))
                    hi, lo = [feature_major(h, j) for h in parts]
                    pool.tensor_tensor(lo, feature_major(whole, j), hi.bitcast(F32), ALU.subtract).then_inc(ready.sem, 1)

            def iteration(i, parts):
                if "A" in parts:
                    low_parts(i, xt1_f, xt1, xt1_hi_ready, xt1_ready)
                if "B" in parts:
                    csum_ready.wait(pool, i - 1, 0)
                    x2_ready.wait(pool, i - 1, 1)
                    x3_ready.wait(pool, i - 2, 1)
                    pool.tensor_tensor(x2c[:, :, :], x2[:, :, :], csum[:, :].unsqueeze(2).to_broadcast([P, NT, D]),
                                       ALU.add).then_inc(x2c_ready.sem, 1)
                if "C" in parts:
                    low_parts(i - 2, xt3_f, xt3, xt3_hi_ready, xt3_ready)
                    for t in range(NT):
                        hmt_hi_ready.wait(pool, i - 2, t)
                        hi, lo, whole = [h[:, t, :, :].rearrange("p k n -> p (k n)") for h in (*hmt, hmt_f)]
                        pool.tensor_tensor(lo, whole, hi.bitcast(F32), ALU.subtract).then_inc(hmt_ready.sem, 1)

            biased(0)
            iteration(0, "A")
            biased(1)
            iteration(1, "AB")
            biased(2)
            with pool.Fori(2, NG - 1) as i:
                iteration(i, "ABC")
                biased(i + 1)
            iteration(NG - 1, "ABC")
            iteration(NG, "BC")
            iteration(NG + 1, "C")

        def prep_uses():
            return [
                ([(raw_w0[:, o, c * P:(c + 1) * P], P, c * D + o * P) for c in range(DC) for o in range(2)],
                 [(0, DC * D, [t[:, :, :].rearrange("p c d -> p (c d)") for t in w0t])]),
                ([(raw_a0[:, c * P:(c + 1) * P], P, c * C0) for c in range(DC)]
                 + [(raw_g[:, w, c * P:(c + 1) * P], E0, DC * C0 + (w * DC + c) * E0) for w in range(2) for c in range(DC)],
                 [(c * C0, C0, [t[:, c, 0:C0] for t in a0t]) for c in range(DC)]
                 + [(DC * C0 + c * E0, E0, [t[:, c, C0:C0 + E0] for t in a0t]) for c in range(DC)]
                 + [(DC * C0 + DC * E0, DC * E1, [t[:, :, :].rearrange("p c e -> p (c e)") for t in g1t])]),
                ([(raw_b0[:, o, :, :].rearrange("p e r -> p (e r)"), P, o * P) for o in range(2)],
                 [(0, D, [t[:, :] for t in b0t])]),
                *[([(raw_a1[:, r, c * P:(c + 1) * P], P, r * P) for r in range(CT1)],
                   [(0, C1, [t[:, c, :] for t in a1t])]) for c in range(DC)],
                *[([(raw_b1[:, o, 2 * k:2 * k + 2, :].rearrange("p e r -> p (e r)"), P, (k - k0) * D + o * P)
                    for k in (k0, k0 + 1) for o in range(2)],
                   [(0, 2 * D, [t[:, k0:k0 + 2, :].rearrange("p k d -> p (k d)") for t in b1t])])
                  for k0 in range(0, CT1, 2)],
            ]

        @block.scalar
        def _(act):
            def normalise(g, n, src, dst, ready):
                act.wait_ge(scales[n].sem, scales[n].count(g, 0))
                for t in range(NT):
                    last = act.activation(dst[:, t, :], src[:, t, :], ACT.Identity, scale=rstd[n][:, t:t + 1],
                                          bias=shift[n][:, t:t + 1])
                last.then_inc(ready.sem, 1)

            def turned(g, name, whole, hi, ready):
                for i in range(2):
                    act.wait_ge(full[name].sem, full[name].count(g, i))
                    for dst in (whole, hi):
                        if dst is not None:
                            last = act.activation(feature_major(dst, i), token_major(bank_of(name, i)), ACT.Copy)
                    last.then_inc(ready.sem, 1)

            def sigmoids(g, js, live):
                for j in js if live else ():
                    act.wait_ge(full["aff"].sem, full["aff"].count(g, j))
                    act.activation(th[:, j, :, :].rearrange("p c d -> p (c d)"), bank_of("aff", j)[:, :], ACT.Tanh,
                                   scale=0.5 * float(SEQ) ** -0.5).then_inc(th_ready.sem, 1)

            def iteration(i, parts, last=False):
                a, b, c = i, i - 1, i - 2
                if "A" in parts:
                    turned(a, "xt1", xt1_f, xt1[0], xt1_hi_ready)
                if "B" in parts:
                    turned(b, "ct", ct, None, ct_ready)
                sigmoids(b, range(B_NT // 2), "B" in parts)
                if "C" in parts:
                    normalise(c, 2, x3, xn3, xn3_ready)
                if "A" in parts:
                    for k in range(2):
                        act.wait_ge(full["xa"].sem, full["xa"].count(a, k))
                        act.activation(xa[:, 2 * k:2 * k + 2, :],
                                       bank_of("xa", k)[:, 0:2 * (C0 + E0)].rearrange("p (t n) -> p t n", t=2)[:, :, 0:C0],
                                       ACT.Copy).then_inc(xa_ready.sem, 1)
                sigmoids(b, range(B_NT // 2, B_NT - 3), "B" in parts)
                if "C" in parts:
                    turned(c, "xt3", xt3_f, xt3[0], xt3_hi_ready)
                sigmoids(b, range(B_NT - 3, B_NT), "B" in parts)
                if "A" in parts and not last:
                    normalise(a + 1, 0, x1, xn1, xn1_ready)
                if "C" in parts:
                    out_sent.wait(act, c - 1, 15)
                    act.activation(result[:, :, :], x3[:, :, :], ACT.Copy).then_inc(x3_copied.sem, 1)
                if "A" in parts:
                    act.wait_ge(gap_ready.sem, gap_ready.count(a, 0))
                    act.activation(gexp[:, :], best[:, :], ACT.Exp).then_inc(gexp_ready.sem, 1)
                if "A" in parts:
                    act.wait_ge(full["xg"].sem, full["xg"].count(a, 0))
                    act.activation(xgt[0][:, :], bank_of("xg", 0)[:, :], ACT.Copy).then_inc(xgt_hi_ready.sem, 1)
                if "C" in parts:
                    act.wait_ge(lg1_ready.sem, lg1_ready.count(c, 0))
                    act.activation(ex1[:, :, :], lg1[:, :, :], ACT.Exp).then_inc(ex1_ready.sem, 1)
                if "C" in parts:
                    for t in range(NT):
                        act.wait_ge(full["hm"].sem, full["hm"].count(c, t))
                        for dst in (hmt_f, hmt[0]):
                            end = act.activation(dst[:, t, :, :].rearrange("p k n -> p (k n)"), bank_of("hm", t)[:, :],
                                                 ACT.Copy)
                        end.then_inc(hmt_hi_ready.sem, 1)
                if "A" in parts:
                    normalise(a, 1, x2, xn2, xn2_ready)

            normalise(0, 0, x1, xn1, xn1_ready)
            for u, (_, parts) in enumerate(prep_uses()):
                act.wait_ge(s_prep, u + 1)
                for at, n, dst in parts:
                    end = act.activation(dst[0], banks[u][:, at:at + n], ACT.Copy)
                end.then_inc(s_prep_hi, 1)
            iteration(0, "A")
            iteration(1, "AB")
            with act.Fori(2, NG - 1) as i:
                iteration(i, "ABC")
            iteration(NG - 1, "ABC", last=True)
            iteration(NG, "BC")
            iteration(NG + 1, "C")

        @block.tensor
        def _(pe):
            def three(out, lhs, rhs, start, stop, **kw):
                pairs = [(0, 0), (0, 1), (1, 0)]
                for n, (a, b) in enumerate(pairs):
                    last = pe.matmul(out, lhs[a], rhs[b], start=start and n == 0, stop=stop and n == 2, **kw)
                return last

            pe.wait_ge(shared.s_raw, 9 * 16)
            for u, (blocks, _) in enumerate(prep_uses()):
                for src, rows, at in blocks:
                    last = pe.transpose(banks[u][:, at:at + rows], src, ident[0:rows, 0:rows])
                last.then_inc(s_prep, 1)
            pe.wait_ge(s_prep_lo, 2)

            AWAKE = {(0, "xg"): 14, (1, "xa"): 4, (1, "aff"): 16, (1, "xg"): 12, (2, "aff"): 8, (2, "h"): 4, (NG + 1, "h"): 2}

            def take(i, parts, before, name, j):
                u = PLACE[name, j]
                for back in range(len(banks), 2 * len(USES), len(banks)):
                    v, it = (u - back) % len(USES), i - (0 if back <= u else (back - u - 1) // len(USES) + 1)
                    prev, k, part, read = USES[v]
                    if part in (parts if back <= u else before):
                        read.wait(pe, it - LAG[part], k)
                        break
                return banks[u % len(banks)]

            def stay_awake(i, name, bank):
                for _ in range(AWAKE.get((i, name), 0) if isinstance(i, int) else 0):
                    pe.matmul(bank[:, :], w0t[0][:, 0, 0:P], w0t[0][:, :, :].rearrange("p c d -> p (c d)"),
                              start=True, stop=True)

            def gate_logits(g, tiles):
                for t in tiles:
                    pe.wait_ge(xt3_ready.sem, xt3_ready.count(g, t // 2))
                    s = slice(t * P, (t + 1) * P)
                    for c in range(DC):
                        last = three(bank_of("lg", 0)[:, t * E1:(t + 1) * E1], [h[:, c, s] for h in xt3],
                                     [h[:, c, :] for h in g1t], start=c == 0, stop=c == DC - 1)
                if t == NT - 1:
                    last.then_inc(full["lg"].sem, 1)

            def stage(name, js, g, i, parts, before):
                def bank(j):
                    return take(i, parts, before, name, j)

                def turned(j, src):
                    b = bank(j)
                    for t in range(2):
                        for c in range(DC):
                            last = pe.transpose(b[:, (t * DC + c) * P:(t * DC + c + 1) * P],
                                                src[:, 2 * j + t, c * P:(c + 1) * P], ident[:, :])
                    last.then_inc(full[name].sem, 1)

                if name == "xt1":
                    pe.wait_ge(xn1_ready.sem, xn1_ready.count(g, 0))
                    for j in range(2):
                        turned(j, xn1)
                elif name == "ct":
                    pe.wait_ge(cin_in.sem, cin_in.count(g, 15))
                    for j in range(2):
                        turned(j, cin)
                elif name == "xt3":
                    pe.wait_ge(xn3_ready.sem, xn3_ready.count(g, 0))
                    for j in range(2):
                        turned(j, xn3)
                elif name == "aff":
                    if js.start == 0:
                        stay_awake(i, name, bank(0))
                    pe.wait_ge(xn2_ready.sem, xn2_ready.count(g, 0))
                    for j in js:
                        b, t, rows = bank(j), j // 2, slice(j % 2 * SEQ, (j % 2 + 1) * SEQ)
                        for c in range(DC):
                            last = pe.matmul(b[:, c * D:(c + 1) * D], xn2[rows, t, c * P:(c + 1) * P], cin[rows, t, :],
                                             start=True, stop=True)
                        last.then_inc(full[name].sem, 1)
                elif name == "xa":
                    for j in range(2):
                        b = bank(j)
                        if j == 0:
                            stay_awake(i, name, b)
                        pe.wait_ge(xt1_ready.sem, xt1_ready.count(g, j))
                        for t in range(2):
                            s = slice((2 * j + t) * P, (2 * j + t + 1) * P)
                            for c in range(DC):
                                last = three(b[:, t * (C0 + E0):(t + 1) * (C0 + E0)], [h[:, c, s] for h in xt1],
                                             [h[:, c, :] for h in a0t], start=c == 0, stop=c == DC - 1)
                        last.then_inc(full[name].sem, 1)
                elif name == "att":
                    for j in range(2):
                        pe.wait_ge(ct_ready.sem, ct_ready.count(g, j))
                        pe.wait_ge(th_ready.sem, th_ready.count(g, 4 * j + 3))
                        b = bank(j)
                        for t in range(2):
                            for c in range(DC):
                                for h in range(2):
                                    tok = (2 * j + t) * P + h * SEQ
                                    last = pe.matmul(b[h * SEQ:(h + 1) * SEQ, t * D:(t + 1) * D],
                                                     ct[:, c, tok:tok + SEQ], th[:, 4 * j + 2 * t + h, c, :],
                                                     start=c == 0, stop=c == DC - 1)
                        last.then_inc(full[name].sem, 1)
                elif name == "xg":
                    b = bank(0)
                    stay_awake(i, name, b)
                    pe.wait_ge(xg_ready.sem, xg_ready.count(g, 0))
                    for t in range(NT):
                        last = pe.transpose(b[:, t * P:(t + 1) * P], xg[:, t, :], ident[:, :])
                    last.then_inc(full[name].sem, 1)
                elif name == "lora":
                    pe.wait_ge(xgt_ready.sem, xgt_ready.count(g, 0))
                    for j in range(2):
                        b = bank(j)
                        for t in range(2):
                            s = slice((2 * j + t) * P, (2 * j + t + 1) * P)
                            dst = b[:, t * D:(t + 1) * D]
                            for c in range(DC):
                                three(dst, [h[:, c, s] for h in xt1], [h[:, c, :] for h in w0t],
                                      start=c == 0, stop=False)
                            last = three(dst, [h[:, s] for h in xgt], [h[:, :] for h in b0t], start=False, stop=True)
                        last.then_inc(full[name].sem, 1)
                elif name == "lg":
                    bank(0)
                    gate_logits(g, (0, 1))
                elif name == "h":
                    for t in js:
                        b = bank(t)
                        if t == 0:
                            stay_awake(i, name, b)
                        pe.wait_ge(xt3_ready.sem, xt3_ready.count(g, t // 2))
                        s = slice(t * P, (t + 1) * P)
                        for c in range(DC):
                            last = three(b[:, :], [h[:, c, s] for h in xt3], [h[:, c, :] for h in a1t],
                                         start=c == 0, stop=c == DC - 1)
                        last.then_inc(full[name].sem, 1)
                        if t == 1:
                            gate_logits(g, (2, 3))
                elif name == "hm":
                    for t in range(NT):
                        pe.wait_ge(hm_ready.sem, hm_ready.count(g, t))
                        b = bank(t)
                        for k in range(CT1):
                            last = pe.transpose(b[:, k * P:(k + 1) * P], hm[:, t, k * P:(k + 1) * P], ident[:, :])
                        last.then_inc(full[name].sem, 1)
                elif name == "y":
                    for j in range(2):
                        b = bank(j)
                        for t in range(2):
                            pe.wait_ge(hmt_ready.sem, hmt_ready.count(g, 2 * j + t))
                            for k in range(CT1):
                                last = three(b[:, t * D:(t + 1) * D], [h[:, 2 * j + t, k, :] for h in hmt],
                                             [h[:, k, :] for h in b1t], start=k == 0, stop=k == CT1 - 1)
                        last.then_inc(full[name].sem, 1)

            def iteration(i, parts, before):
                for name, js, part, _ in RING:
                    if part in parts:
                        if isinstance(i, int) and i == 0 and name == "xa":
                            pe.wait_ge(s_prep_lo, len(prep_uses()))
                        stage(name, js, i - LAG[part], i, parts, before)

            iteration(0, "A", "")
            iteration(1, "AB", "A")
            iteration(2, "ABC", "AB")
            with pe.Fori(3, NG) as i:
                iteration(i, "ABC", "ABC")
            iteration(NG, "BC", "ABC")
            iteration(NG + 1, "C", "BC")

        @block.vector
        def _(dve):
            chain = Chain(dve, s_chain)

            def wide(v):
                return v.unsqueeze(2).to_broadcast([P, NT, E0])

            def layernorm(g, n, src):
                for t in range(NT):
                    chain.mark(dve.bn_stats(stats[:, t, :], src[:, t, :]))
                chain.wait()
                moments(dve, chain, mean[:, :], var_eps[:, :], ntmp[:, :], stats)
                rsqrt(dve, chain, rstd[n][:, :], ntmp[:, :], var_eps[:, :])
                dve.scalar_tensor_tensor(out=shift[n][:, :], in0=mean[:, :], scalar=-1.0, in1=rstd[n][:, :],
                                         op0=ALU.mult, op1=ALU.mult).then_inc(scales[n].sem, 1)
                dve.wait_ge(scales[n].sem, scales[n].count(g, 0))

            def first_of_largest(values, top, pick):
                chain.link(dve.tensor_reduce(top, values, AXX, ALU.max))
                chain.link(dve.tensor_tensor(work[:, :, :], values, wide(top), ALU.is_ge))
                chain.link(dve.tensor_tensor(work[:, :, :], work[:, :, :], prefer[:, :, :], ALU.mult))
                chain.link(dve.tensor_reduce(best[:, :], work[:, :, :], AXX, ALU.max))
                chain.link(dve.tensor_tensor(pick, work[:, :, :], wide(best[:, :]), ALU.is_equal))

            def context_sum(g):
                dve.wait_ge(cin_in.sem, cin_in.count(g, 15))
                chain.link(dve.tensor_reduce(csum[:, :], cin[:, :, :], AXX, ALU.add))
                dve.tensor_scalar(csum[:, :], csum[:, :], tgh[:, 0:1], None, ALU.mult).then_inc(csum_ready.sem, 1)

            def mixture_gates(g):
                for j in range(2):
                    dve.wait_ge(xa_ready.sem, xa_ready.count(g, j))
                    src = bank_of("xa", j)[:, 0:2 * (C0 + E0)].rearrange("p (t n) -> p t n", t=2)[:, :, C0:C0 + E0]
                    dve.tensor_tensor(lg0[:, 2 * j:2 * j + 2, :], src,
                                      gbias[:, :].unsqueeze(1).to_broadcast([P, 2, E0]),
                                      ALU.add).then_inc(lg0_ready.sem, 1)
                dve.wait_ge(lg0_ready.sem, lg0_ready.count(g, 1))
                first_of_largest(lg0[:, :, :], top[:, 0, :], pick[0][:, :, :])
                chain.link(dve.scalar_tensor_tensor(out=lg0[:, :, :], in0=pick[0][:, :, :], scalar=-BIG,
                                                    in1=lg0[:, :, :], op0=ALU.mult, op1=ALU.add))
                first_of_largest(lg0[:, :, :], top[:, 1, :], pick[1][:, :, :])
                dve.tensor_tensor(best[:, :], top[:, 1, :], top[:, 0, :], ALU.subtract).then_inc(gap_ready.sem, 1)
                dve.wait_ge(gexp_ready.sem, gexp_ready.count(g, 0))
                chain.link(dve.tensor_scalar(gw[:, 1, :], gexp[:, :], 1.0, None, ALU.add))
                chain.link(dve.reciprocal(gw[:, 0, :], gw[:, 1, :]))
                chain.link(dve.tensor_tensor(gw[:, 1, :], gexp[:, :], gw[:, 0, :], ALU.mult))
                for k in range(K0):
                    chain.mark(dve.tensor_tensor(pick[k][:, :, :], pick[k][:, :, :], wide(gw[:, k, :]), ALU.mult))
                chain.wait()
                chain.link(dve.tensor_tensor(gates[:, :, :], pick[0][:, :, :], pick[1][:, :, :], ALU.add))
                dve.tensor_tensor(xg[:, :, :].rearrange("p t (e r) -> p (t e) r", r=R0),
                                  xa[:, :, :].rearrange("p t (e r) -> p (t e) r", r=R0),
                                  gates[:, :, :].rearrange("p t e -> p (t e)").unsqueeze(2).to_broadcast([P, NT * E0, R0]),
                                  ALU.mult).then_inc(xg_ready.sem, 1)

            def expert_scale(g):
                dve.wait_ge(full["lg"].sem, full["lg"].count(g, 0))
                dve.tensor_copy(coef[:, :, :], bank_of("lg", 0)[:, 0:NT * E1].rearrange(
                    "p (t e) -> p t e", t=NT)).then_inc(lg1_read.sem, 1)
                dve.wait_ge(lg1_read.sem, lg1_read.count(g, 0))
                first_of_largest(coef[:, :, :], top[:, 0, :], pick[0][:, :, :])
                dve.tensor_tensor(lg1[:, :, :], coef[:, :, :], wide(top[:, 0, :]), ALU.subtract).then_inc(lg1_ready.sem, 1)
                dve.wait_ge(ex1_ready.sem, ex1_ready.count(g, 0))
                chain.link(dve.tensor_reduce(best[:, :], ex1[:, :, :], AXX, ALU.add))
                chain.link(dve.reciprocal(gw[:, 0, :], best[:, :]))
                chain.link(dve.scalar_tensor_tensor(out=coef[:, :, :], in0=pick[0][:, :, :], scalar=EXPERT_SCALING,
                                                    in1=wide(gw[:, 0, :]), op0=ALU.mult, op1=ALU.mult))

            def chosen_expert(g):
                for t in range(NT):
                    dve.wait_ge(full["h"].sem, full["h"].count(g, t))
                    dve.tensor_tensor(hm[:, t, :].rearrange("p (e r) -> p e r", e=E1),
                                      bank_of("h", t)[:, :].rearrange("p (e r) -> p e r", e=E1),
                                      coef[:, t, :].unsqueeze(2).to_broadcast([P, E1, R1]),
                                      ALU.mult).then_inc(hm_ready.sem, 1)

            def residual(g, name, dst, gate, src, ready):
                for j in range(2):
                    dve.wait_ge(full[name].sem, full[name].count(g, j))
                    new, old = [v[:, 2 * j:2 * j + 2, :].rearrange("p t d -> p (t d)") for v in (dst, src)]
                    dve.scalar_tensor_tensor(out=new, in0=bank_of(name, j)[:, :], scalar=gate, in1=old,
                                             op0=ALU.mult, op1=ALU.add).then_inc(ready.sem, 1)

            def iteration(i, parts, last=False):
                a, b, c = i, i - 1, i - 2
                if "B" in parts:
                    context_sum(b)
                if "A" in parts:
                    if not last:
                        dve.wait_ge(x1_in.sem, x1_in.count(a + 1, 15))
                        dve.wait_ge(xn1_ready.sem, xn1_ready.count(a, 0))
                        layernorm(a + 1, 0, x1)
                    mixture_gates(a)
                    dve.wait_ge(xgt_hi_ready.sem, xgt_hi_ready.count(a, 0))
                    dve.tensor_tensor(xgt[1][:, :], bank_of("xg", 0)[:, :], xgt[0][:, :].bitcast(F32),
                                      ALU.subtract).then_inc(xgt_ready.sem, 1)
                if "C" in parts:
                    expert_scale(c)
                    chosen_expert(c)
                if "A" in parts:
                    dve.wait_ge(x1b_ready.sem, x1b_ready.count(a, 0))
                    x2c_ready.wait(dve, a - 1, 0)
                    residual(a, "lora", x2, tg[:, 2:3], x1b, x2_ready)
                    dve.wait_ge(x2_ready.sem, x2_ready.count(a, 1))
                    layernorm(a, 1, x2)
                if "B" in parts:
                    dve.wait_ge(x2c_ready.sem, x2c_ready.count(b, 0))
                    x3_copied.wait(dve, b - 1, 0)
                    residual(b, "att", x3, tgh[:, 0:1], x2c, x3_ready)
                    dve.wait_ge(x3_ready.sem, x3_ready.count(b, 1))
                    layernorm(b, 2, x3)
                if "C" in parts:
                    dve.wait_ge(x3_copied.sem, x3_copied.count(c, 0))
                    residual(c, "y", result, tg[:, 3:4], result, y_ready)

            chain.mark(dve.tensor_scalar(tgh[:, :], tg[:, 1:2], 0.5, None, ALU.mult))
            for u, (_, parts) in enumerate(prep_uses()):
                dve.wait_ge(s_prep_hi, u + 1)
                for at, n, dst in parts:
                    end = dve.tensor_tensor(dst[1], banks[u][:, at:at + n], dst[0].bitcast(F32), ALU.subtract)
                end.then_inc(s_prep_lo, 1)
            chain.wait()
            iteration(0, "A")
            iteration(1, "AB")
            done = chain.n
            with dve.Fori(2, NG - 1) as i:
                chain.start(done + (i - 2) * CHAIN_PER)
                iteration(i, "ABC")
                assert chain.n == CHAIN_PER, chain.n
            chain.start(done + (NG - 3) * CHAIN_PER)
            iteration(NG - 1, "ABC", last=True)
            iteration(NG, "BC")
            iteration(NG + 1, "C")


_INS = ["x", "ctx_2048", "g_xattn", "g_ffn", "L0_xattn_q_w", "L0_xattn_q_b", "L0_xattn_ki_w", "L0_xattn_ki_b",
        "L0_xattn_vi_w", "L0_xattn_vi_b", "L0_xattn_o_w", "L0_xattn_o_b", "L0_xattn_nq_s", "L0_xattn_nki_s",
        "L0_ffn_W", "L0_ffn_b", "L0_ffn_lora_A", "L0_ffn_lora_B", "L0_ffn_gate_w", "L0_ffn_gate_b",
        "L1_ffn_A", "L1_ffn_Bw", "L1_ffn_Wg"]


def build(nc, a, out):
    x1 = nc.dram_tensor("x1_scratch", (NG, P, NT, D), F32, kind="Internal").ap()
    late = [a[n] for n in ("L0_ffn_W", "L0_ffn_lora_A", "L0_ffn_lora_B", "L0_ffn_gate_w",
                           "L1_ffn_A", "L1_ffn_Bw", "L1_ffn_Wg")]
    with ExitStack() as stack:
        shared = Shared(nc, stack)
        first_attention(nc, shared, late, a["x"], a["ctx_2048"], a["g_xattn"], a["g_ffn"], a["L0_ffn_b"],
                        a["L0_ffn_gate_b"],
                        *(a["L0_xattn_" + n] for n in ("q_w", "q_b", "ki_w", "ki_b", "vi_w", "vi_b", "o_w", "o_b",
                                                       "nq_s", "nki_s")), x1)
        remaining_layers(nc, shared, x1, a["ctx_2048"], out)


def kernel(**inputs):
    import numpy as _np
    import concourse.bacc as _bacc
    from concourse import mybir as _mybir
    from concourse.bass_utils import run_bass_kernel_spmd as _run

    nc = _bacc.Bacc("TRN2", target_bir_lowering=False, num_devices=1)
    arrays, args = {}, {}
    for name in _INS:
        a = _np.ascontiguousarray(inputs[name])
        arrays[f"in_{name}_dram"] = a
        args[name] = nc.dram_tensor(f"in_{name}_dram", a.shape, _mybir.dt.from_np(a.dtype), kind="ExternalInput").ap()
    out = nc.dram_tensor("out_dram", (BATCH, SEQ, D), F32, kind="ExternalOutput").ap()
    build(nc, args, out)
    return _run(nc, [arrays], core_ids=[0]).results[0]["out_dram"]
```
